# Optimizing a Trainium2 kernel written in Bass

```python
import numpy as np
import jax
import jax.numpy as jnp

def _softmax(x, axis=-1):
    return jax.nn.softmax(x, axis=axis)

def _gelu(x):
    return jax.nn.gelu(x, approximate=True)

def _silu(x):
    return jax.nn.silu(x)

def _sigmoid(x):
    return jax.nn.sigmoid(x)

def _layernorm(x, axis=-1, eps=1e-05):
    m = jnp.mean(x, axis=axis, keepdims=True)
    v = jnp.var(x, axis=axis, keepdims=True)
    return (x - m) / jnp.sqrt(v + eps)

def _scatter_add(tgt, idx, src, axis=0):
    return tgt.at[idx].add(src)

def _segment_sum(src, seg, n):
    return jax.ops.segment_sum(src, seg, n)
kernel_name = 'mk_adaln_d1_jaxref_r8_38269f'

def setup_inputs(seed: int=0):
    np.random.seed(seed)
    _w = jnp.asarray

    def _L0_attn_setup():
        import jax, jax.numpy as jnp
        import numpy as np
        import math
        B, S, DIM = (2, 256, 256)
        H, NOPE, ROPE, VDIM = (16, 128, 64, 128)
        Q_RANK, KV_RANK = (128, 64)
        EPS = 1e-06
        ROPE_THETA = 10000.0

        def _rmsnorm(x, w, eps=EPS):
            return x * jax.lax.rsqrt(jnp.mean(x * x, axis=-1, keepdims=True) + eps) * w

        def _rope_cos_sin(seq_len, head_dim, dtype=jnp.float32):
            inv_freq = 1.0 / ROPE_THETA ** (jnp.arange(0, head_dim, 2, dtype=jnp.float32) / head_dim)
            t = jnp.arange(seq_len, dtype=jnp.float32)
            freqs = jnp.outer(t, inv_freq)
            return (jnp.cos(freqs).astype(dtype), jnp.sin(freqs).astype(dtype))

        def _apply_rope(x, cos, sin):
            x1, x2 = (x[..., 0::2], x[..., 1::2])
            c = cos[None, :, None, :]
            s = sin[None, :, None, :]
            o1 = x1 * c - x2 * s
            o2 = x1 * s + x2 * c
            return jnp.stack([o1, o2], axis=-1).reshape(x.shape)
        key = jax.random.key(seed)
        ks = jax.random.split(key, 9)
        s = 0.02
        return {'x': jax.random.normal(ks[0], (B, S, DIM), jnp.float32), 'wq_down': jax.random.normal(ks[1], (Q_RANK, DIM), jnp.float32) * s, 'q_norm_w': jnp.ones((Q_RANK,), jnp.float32), 'wq_up': jax.random.normal(ks[2], (H * NOPE, Q_RANK), jnp.float32) * s, 'wq_rope': jax.random.normal(ks[3], (H * ROPE, Q_RANK), jnp.float32) * s, 'wkv_down': jax.random.normal(ks[4], (KV_RANK, DIM), jnp.float32) * s, 'kv_norm_w': jnp.ones((KV_RANK,), jnp.float32), 'wkv_up': jax.random.normal(ks[5], (H * (NOPE + VDIM), KV_RANK), jnp.float32) * s, 'wk_rope': jax.random.normal(ks[6], (ROPE, DIM), jnp.float32) * s, 'wo': jax.random.normal(ks[7], (DIM, H * VDIM), jnp.float32) * s}
    _L0_attn_in = _L0_attn_setup()

    def _L0_ffn_setup():
        import jax, jax.numpy as jnp
        import numpy as np
        DIM = 256
        HID = 704
        ZERO_POINT = 128.0

        def _qlinear(x, wq, scale):
            W = (wq.astype(jnp.float32) - ZERO_POINT) * scale[:, None]
            return jnp.einsum('bsd,hd->bsh', x, W)
        key = jax.random.key(seed)
        ks = jax.random.split(key, 7)
        B, S = (4, 256)
        sg = jax.random.uniform(ks[1], (HID,)) * (0.02 / np.sqrt(DIM)) + 0.0001
        su = jax.random.uniform(ks[3], (HID,)) * (0.02 / np.sqrt(DIM)) + 0.0001
        sd = jax.random.uniform(ks[5], (DIM,)) * (0.02 / np.sqrt(HID)) + 0.0001
        return {'x': jax.random.normal(ks[0], (B, S, DIM), dtype=jnp.float32), 'wq_gate': jax.random.randint(ks[2], (HID, DIM), 0, 32, dtype=jnp.int32), 's_gate': sg, 'wq_up': jax.random.randint(ks[4], (HID, DIM), 0, 32, dtype=jnp.int32), 's_up': su, 'wq_down': jax.random.randint(ks[6], (DIM, HID), 0, 32, dtype=jnp.int32), 's_down': sd}
    _L0_ffn_in = _L0_ffn_setup()
    _L0_c = _w((lambda *s: np.random.randn(*s).astype(np.float32) * 0.05)(1, 256))
    _L0_wmod = _w((lambda *s: np.random.randn(*s).astype(np.float32) * 0.05)(256, 6 * 256) * 256 ** (-0.5))
    _d = {'L0_attn_x': _L0_attn_in['x'], 'L0_attn_wq_down': _L0_attn_in['wq_down'], 'L0_attn_q_norm_w': _L0_attn_in['q_norm_w'], 'L0_attn_wq_up': _L0_attn_in['wq_up'], 'L0_attn_wq_rope': _L0_attn_in['wq_rope'], 'L0_attn_wkv_down': _L0_attn_in['wkv_down'], 'L0_attn_kv_norm_w': _L0_attn_in['kv_norm_w'], 'L0_attn_wkv_up': _L0_attn_in['wkv_up'], 'L0_attn_wk_rope': _L0_attn_in['wk_rope'], 'L0_attn_wo': _L0_attn_in['wo'], 'L0_ffn_wq_gate': _L0_ffn_in['wq_gate'], 'L0_ffn_s_gate': _L0_ffn_in['s_gate'], 'L0_ffn_wq_up': _L0_ffn_in['wq_up'], 'L0_ffn_s_up': _L0_ffn_in['s_up'], 'L0_ffn_wq_down': _L0_ffn_in['wq_down'], 'L0_ffn_s_down': _L0_ffn_in['s_down'], 'L0_c': _L0_c, 'L0_wmod': _L0_wmod}
    _x0 = _d['L0_attn_x']
    _d['L0_attn_x'] = jax.random.normal(jax.random.fold_in(jax.random.key(seed), 1), (1, 2048, 256), dtype=_x0.dtype)
    del _x0
    return _d

def reference(L0_attn_x, L0_attn_wq_down, L0_attn_q_norm_w, L0_attn_wq_up, L0_attn_wq_rope, L0_attn_wkv_down, L0_attn_kv_norm_w, L0_attn_wkv_up, L0_attn_wk_rope, L0_attn_wo, L0_ffn_wq_gate, L0_ffn_s_gate, L0_ffn_wq_up, L0_ffn_s_up, L0_ffn_wq_down, L0_ffn_s_down, L0_c, L0_wmod):

    def _L0_attn_ref(x, wq_down, q_norm_w, wq_up, wq_rope, wkv_down, kv_norm_w, wkv_up, wk_rope, wo):
        import jax, jax.numpy as jnp
        import numpy as np
        import math
        B, S, DIM = (2, 256, 256)
        H, NOPE, ROPE, VDIM = (16, 128, 64, 128)
        Q_RANK, KV_RANK = (128, 64)
        EPS = 1e-06
        ROPE_THETA = 10000.0

        def _rmsnorm(x, w, eps=EPS):
            return x * jax.lax.rsqrt(jnp.mean(x * x, axis=-1, keepdims=True) + eps) * w

        def _rope_cos_sin(seq_len, head_dim, dtype=jnp.float32):
            inv_freq = 1.0 / ROPE_THETA ** (jnp.arange(0, head_dim, 2, dtype=jnp.float32) / head_dim)
            t = jnp.arange(seq_len, dtype=jnp.float32)
            freqs = jnp.outer(t, inv_freq)
            return (jnp.cos(freqs).astype(dtype), jnp.sin(freqs).astype(dtype))

        def _apply_rope(x, cos, sin):
            x1, x2 = (x[..., 0::2], x[..., 1::2])
            c = cos[None, :, None, :]
            s = sin[None, :, None, :]
            o1 = x1 * c - x2 * s
            o2 = x1 * s + x2 * c
            return jnp.stack([o1, o2], axis=-1).reshape(x.shape)
        bs, seq_len, _ = x.shape
        q_c = _rmsnorm(x @ wq_down.T, q_norm_w)
        q_nope = (q_c @ wq_up.T).reshape(bs, seq_len, H, NOPE)
        q_pe = (q_c @ wq_rope.T).reshape(bs, seq_len, H, ROPE)
        kv_c = _rmsnorm(x @ wkv_down.T, kv_norm_w)
        kv_up = (x_kv := (kv_c @ wkv_up.T)).reshape(bs, seq_len, H, NOPE + VDIM)
        k_nope, v = (kv_up[..., :NOPE], kv_up[..., NOPE:])
        k_rope_shared = (x @ wk_rope.T).reshape(bs, seq_len, 1, ROPE)
        cos, sin = _rope_cos_sin(seq_len, ROPE, x.dtype)
        q_pe = _apply_rope(q_pe, cos, sin)
        k_rope_shared = _apply_rope(k_rope_shared, cos, sin)
        k_rope = jnp.broadcast_to(k_rope_shared, (bs, seq_len, H, ROPE))
        q = jnp.concatenate([q_nope, q_pe], axis=-1)
        k = jnp.concatenate([k_nope, k_rope], axis=-1)
        scale = 1.0 / math.sqrt(NOPE + ROPE)
        scores = jnp.einsum('bqhd,bkhd->bhqk', q, k) * scale
        causal = jnp.tril(jnp.ones((seq_len, seq_len), bool))
        scores = jnp.where(causal[None, None], scores, -jnp.inf)
        probs = jax.nn.softmax(scores.astype(jnp.float32), axis=-1).astype(q.dtype)
        out = jnp.einsum('bhqk,bkhv->bqhv', probs, v).reshape(bs, seq_len, H * VDIM)
        return out @ wo.T

    def _L0_ffn_ref(x, wq_gate, s_gate, wq_up, s_up, wq_down, s_down):
        import jax, jax.numpy as jnp
        import numpy as np
        DIM = 256
        HID = 704
        ZERO_POINT = 128.0

        def _qlinear(x, wq, scale):
            W = (wq.astype(jnp.float32) - ZERO_POINT) * scale[:, None]
            return jnp.einsum('bsd,hd->bsh', x, W)
        gate = _qlinear(x, wq_gate, s_gate)
        gate = jax.nn.silu(gate)
        up = _qlinear(x, wq_up, s_up)
        return _qlinear(gate * up, wq_down, s_down)
    x = L0_attn_x
    mod = (_silu(L0_c) @ L0_wmod).reshape(L0_c.shape[0], 6, 1, -1)
    sa, ca, ga, sb, cb, gb = (mod[:, 0], mod[:, 1], mod[:, 2], mod[:, 3], mod[:, 4], mod[:, 5])
    ga = (2 * (ga >= 0) - 1) * jnp.maximum(jnp.abs(ga), 0.25)
    gb = (2 * (gb >= 0) - 1) * jnp.maximum(jnp.abs(gb), 0.25)
    h = _layernorm(x, axis=-1) * (1 + ca) + sa
    x = x + ga * _L0_attn_ref(h, L0_attn_wq_down, L0_attn_q_norm_w, L0_attn_wq_up, L0_attn_wq_rope, L0_attn_wkv_down, L0_attn_kv_norm_w, L0_attn_wkv_up, L0_attn_wk_rope, L0_attn_wo)
    h = _layernorm(x, axis=-1) * (1 + cb) + sb
    x = x + gb * _L0_ffn_ref(h, L0_ffn_wq_gate, L0_ffn_s_gate, L0_ffn_wq_up, L0_ffn_s_up, L0_ffn_wq_down, L0_ffn_s_down)
    return x

_drawn_inputs = setup_inputs


def setup_inputs(seed=0):
    import zlib

    import numpy as np

    out = dict(_drawn_inputs(seed))
    spreads = {'L0_attn_q_norm_w': (1.0, 0.6), 'L0_attn_kv_norm_w': (1.0, 0.6)}
    factors = {'L0_attn_wq_down': 8.0,
     'L0_attn_wq_up': 8.0,
     'L0_attn_wq_rope': 8.0,
     'L0_attn_wkv_down': 8.0,
     'L0_attn_wkv_up': 8.0,
     'L0_attn_wk_rope': 8.0,
     'L0_attn_wo': 8.0,
     'L0_ffn_s_gate': 8.0,
     'L0_ffn_s_up': 8.0,
     'L0_ffn_s_down': 8.0,
     'L0_c': 8.0,
     'L0_wmod': 8.0}
    for name, (base, spread) in spreads.items():
        noise = np.random.default_rng([zlib.crc32(name.encode()), seed]).standard_normal(out[name].shape)
        drawn = base * np.exp(spread * noise) if base else spread * noise
        out[name] = jnp.asarray(drawn.astype(out[name].dtype))
    for name, factor in factors.items():
        out[name] = (out[name] * factor).astype(out[name].dtype)
    return out
```

```python
from contextlib import ExitStack

import numpy as np

import concourse.bass as bass
from concourse import mybir

F32 = mybir.dt.float32
F32R = mybir.dt.float32r
BF16 = mybir.dt.bfloat16
I32 = mybir.dt.int32
ALU = mybir.AluOpType
ACT = mybir.ActivationFunctionType
AX = mybir.AxisListType

P = 128
S = 2048
D = 256
DH = D // P
H = 16
PAIRS = H // 2
NOPE, ROPE, VD = 128, 64, 128
QR, KR = 128, 64
HID = 704
HB = 6
TT = S // P
C = 512
NC = S // C
CB = C // P
NEG = -1.0e30
SCALE = float(1.0 / np.sqrt(NOPE + ROPE))
LN_EPS, RMS_EPS = 1e-5, 1e-6

UNITS = [CB * (c + 1) for c in range(NC)]
PIECES = [2 * CB * (c + 1) for c in range(NC)]


def units_before(c, p):
    return PAIRS * sum(UNITS[:c]) + p * UNITS[c]


def pieces_before(c, p):
    return PAIRS * sum(PIECES[:c]) + p * PIECES[c]


def build(nc, x, wq_down, q_norm_w, wq_up, wq_rope, wkv_down, kv_norm_w, wkv_up, wk_rope, wo,
          wq_gate, s_gate, wq_up_ffn, s_up, wq_down_ffn, s_down, cvec, wmod,
          ident_c, masks_c, rope_nat, rope_q, out):
    with ExitStack() as base:
        base.enter_context(nc.allow_non_contiguous_dma(reason="vectors of a few hundred elements laid over the partitions"))
        def sb(stack, name, shape, dt=F32):
            return stack.enter_context(nc.sbuf_tensor(name, shape, dt))

        def sem(name):
            return base.enter_context(nc.semaphore(name))

        ps = base.enter_context(nc.psum_tensor("ps", [P, 8, C], F32))
        X = sb(base, "X", [P, TT, D])
        ident = sb(base, "ident", [P, P])
        identb = sb(base, "identb", [P, P], BF16)
        masks = sb(base, "masks", [P, 2, P])
        maskb = sb(base, "maskb", [P, 2, P], BF16)
        ones = sb(base, "ones", [P, 64])
        modc = sb(base, "modc", [P, 12])
        scale1 = sb(base, "scale1", [P, 4])
        gates = sb(base, "gates", [P, 4])
        small = sb(base, "small", [P, 64])
        st = sb(base, "st", [P, TT, 6])
        mv = sb(base, "mv", [P, TT, 2])
        rs = sb(base, "rs", [P, 3, 2 * TT])

        attn_kept = base.enter_context(ExitStack())
        QT = [sb(attn_kept, n, [P, S], F32R) for n in ("qt_hi", "qt_lo")]
        K = [[sb(attn_kept, f"k{v}_{n}", [P, S], F32R) for n in ("hi", "lo")] for v in range(2)]
        KN = sb(attn_kept, "KN", [P, TT, 192])
        WQ = sb(attn_kept, "WQ", [P, PAIRS, 2, 3, P], F32R)
        WVO = sb(attn_kept, "WVO", [P, PAIRS, D])

        with ExitStack() as scratch:
            Z = sb(scratch, "Z", [P, TT, D])
            hT = sb(scratch, "hT", [P, DH, S])
            WU = sb(scratch, "WU", [P, H, QR])
            WKV = sb(scratch, "WKV", [P, 2 * H, KR])
            WR = sb(scratch, "WR", [P, PAIRS, QR])
            WO = sb(scratch, "WO", [P, DH, H * VD])
            WMOD = sb(scratch, "WMOD", [P, DH, 6 * D])
            WD = sb(scratch, "WD", [P, 2, D])
            WDT = sb(scratch, "WDT", [P, DH, D])
            ropeN = sb(scratch, "ropeN", [P, 2, TT, ROPE // 2])
            cc = sb(scratch, "cc", [P, 6, DH])
            qnw = sb(scratch, "qnw", [P, 1])
            kvw = sb(scratch, "kvw", [P, 3])
            PJ = Z
            SQ = hT[:, :, :].rearrange("p a b -> p (a b)")[:, 0:TT * 192].rearrange("p (t c) -> p t c", t=TT)
            woT = hT[:, :, :].rearrange("p a (h d) -> p (a h) d", d=D)
            WQf = KN[:, :, :].rearrange("p t c -> p (t c)").rearrange("p (g m r) -> p g m r", g=PAIRS, m=3)
            TF = WMOD[:, :, :].rearrange("p a b -> p (a b)")[:, 0:4 * C].rearrange("p (s c) -> p s c", s=4)

            jobs = (["A"] + ["V"] + ["V"] * 4 + ["A"] * 8 + ["A"] * 8 + ["A"] * 12 + ["V"] * 8 + ["V"] * 4)
            J_WD, J_MOD, J_ABS, J_ROPE, J_ZT, J_PROJ, J_QK, J_WOT, J_WVO = 0, 1, 2, 4, 6, 14, 22, 34, 42

            x_landed, small_landed, wd_landed, abs_landed = [sem(f"x_landed_{q}") for q in range(4)], sem("small_landed"), sem("wd_landed"), sem("abs_landed")
            wr_landed = sem("wr_landed")
            const_landed, rope_landed, wmod_landed, wo_landed = sem("const_landed"), sem("rope_landed"), sem("wmod_landed"), sem("wo_landed")
            filled = sem("prep_bank_filled")
            emptied = {"A": sem("prep_emptied_by_scalar"), "V": sem("prep_emptied_by_vector")}
            dve_step, act_step = sem("prep_vector_step"), sem("prep_scalar_step")
            z_ready, silu_exp, var_rec, std_ready = sem("z_ready"), sem("silu_exp"), sem("var_rec"), sem("std_ready")
            silu_ready, mod_ready, rms_rec, rms_root = sem("silu_ready"), sem("mod_ready"), sem("rms_rec"), sem("rms_root")
            ones_set, wq_full, nat_ready, wo_scaled, tf_free = sem("ones_set"), sem("wq_full"), sem("nat_ready"), sem("wo_scaled"), sem("tf_free")

            def emptied_count(job):
                return sum(1 for e in jobs[:job + 1] if e == jobs[job])

            def wait_emptied(e, job):
                e.wait_ge(emptied[jobs[job]], emptied_count(job))

            with nc.Block() as block:
                @block.sync
                def _(e):
                    xv = x.rearrange("a (t p) d -> p (a t) d", p=P)
                    for q in range(4):
                        e.dma_start(X[:, 4 * q:4 * q + 4, :], xv[:, 4 * q:4 * q + 4, :]).then_inc(x_landed[q], 16)
                    e.dma_start(WMOD[:, :, :], wmod.rearrange("(a p) n -> p a n", p=P)).then_inc(wmod_landed, 16)
                    e.dma_start(WR[:, :, :], wq_rope.rearrange("(g p) r -> p g r", p=P)).then_inc(wr_landed, 16)
                    e.dma_start(WO[:, :, :], wo.rearrange("(a p) n -> p a n", p=P)).then_inc(wo_landed, 16)
                    e.dma_start(ropeN[:, :, :, :], rope_nat.rearrange("k (t p) r -> p k t r", p=P)).then_inc(rope_landed, 16)

                @block.gpsimd
                def _(e):
                    e.memset(ones[:, :], 1.0).then_inc(ones_set, 1)
                    e.memset(kvw[:, :], 1.0).then_inc(ones_set, 1)
                    e.dma_start(ident[:, :], ident_c).then_inc(const_landed, 16)
                    e.dma_start(masks[:, :, :], masks_c.rearrange("k p n -> p k n")).then_inc(const_landed, 16)
                    e.dma_start(WU[:, :, :], wq_up.rearrange("(h p) r -> p h r", p=P)).then_inc(abs_landed, 16)
                    e.dma_start(WKV[:, :, :], wkv_up.rearrange("(h p) r -> p h r", p=P)).then_inc(abs_landed, 16)

                @block.scalar
                def _(e):
                    e.dma_start(WD[:, 0, :], wq_down).then_inc(wd_landed, 16)
                    e.dma_start(WD[0:KR, 1, :], wkv_down).then_inc(wd_landed, 16)
                    e.dma_start(WD[KR:P, 1, :], wk_rope).then_inc(wd_landed, 16)
                    e.dma_start(cc[:, 0, :], cvec.rearrange("a (k p) -> p (a k)", p=P)).then_inc(small_landed, 16)
                    e.dma_start(qnw[:, :], q_norm_w.rearrange("(p a) -> p a", a=1)).then_inc(small_landed, 16)
                    e.wait_ge(ones_set, 2)
                    for col, row in ((0, 0), (1, KR), (2, 0), (2, KR)):
                        e.dma_start(kvw[row:row + KR, col:col + 1], kv_norm_w.rearrange("(p a) -> p a", a=1)).then_inc(small_landed, 16)
                    e.wait_ge(small_landed, 16 * 6)
                    e.activation(cc[:, 1, :], cc[:, 0, :], ACT.Exp, scale=-1.0).then_inc(silu_exp, 1)
                    e.wait_ge(filled, J_WD + 1)
                    e.activation(WDT[:, :, :], ps[:, J_WD % 8, :].rearrange("p (a n) -> p a n", a=DH), ACT.Copy).then_inc(emptied["A"], 1)
                    e.wait_ge(var_rec, 1)
                    e.activation(rs[:, 1, 0:TT], rs[:, 0, 0:TT], ACT.Sqrt).then_inc(std_ready, 1)
                    e.wait_ge(mod_ready, 1)
                    for k in range(2 * NC):
                        tg, half = k // 2, k % 2
                        e.wait_ge(filled, J_ZT + k + 1)
                        e.activation(hT[:, half, C * tg:C * tg + C], ps[:, (J_ZT + k) % 8, :], ACT.Identity,
                                     bias=modc[:, half:half + 1], scale=scale1[:, half:half + 1]).then_inc(emptied["A"], 1)
                    for k in range(TT // 2):
                        e.wait_ge(filled, J_PROJ + k + 1)
                        e.activation(PJ[:, 2 * k:2 * k + 2, :], ps[:, (J_PROJ + k) % 8, :].rearrange("p (t n) -> p t n", t=2),
                                     ACT.Copy).then_inc(emptied["A"], 1)
                    e.wait_ge(rms_rec, 1)
                    e.activation(rs[:, 1, :], rs[:, 0, :], ACT.Sqrt).then_inc(rms_root, 1)
                    for k in range(3 * NC):
                        e.wait_ge(filled, J_QK + k + 1)
                        if k >= 4:
                            e.wait_ge(tf_free, k - 3)
                        kind = k % 3
                        if kind == 0:
                            e.activation(TF[:, k % 4, :], ps[:, (J_QK + k) % 8, :], ACT.Copy).then_inc(emptied["A"], 1)
                        else:
                            e.activation(TF[:, k % 4, :], ps[:, (J_QK + k) % 8, :], ACT.Identity,
                                         scale=kvw[:, kind - 1:kind]).then_inc(emptied["A"], 1)

                @block.vector
                def _(e):
                    steps = [0]

                    def settle(ins):
                        steps[0] += 1
                        ins.then_inc(dve_step, 1)
                        e.wait_ge(dve_step, steps[0])

                    v = nc.vector
                    for t in range(TT):
                        if t % 4 == 0:
                            e.wait_ge(x_landed[t // 4], 16)
                        last = v.bn_stats(st[:, t, :], X[:, t, :])
                    settle(last)
                    for t in range(TT):
                        last = v.bn_aggr(mv[:, t, :], st[:, t, :])
                    settle(last)
                    settle(v.tensor_scalar(rs[:, 2, 0:TT], mv[:, :, 1], LN_EPS, None, ALU.add))
                    v.reciprocal(rs[:, 0, 0:TT], rs[:, 2, 0:TT]).then_inc(var_rec, 1)
                    e.wait_ge(silu_exp, 1)
                    settle(v.tensor_scalar(cc[:, 2, :], cc[:, 1, :], 1.0, None, ALU.add))
                    settle(v.reciprocal(cc[:, 3, :], cc[:, 2, :]))
                    v.tensor_tensor(cc[:, 4, :], cc[:, 0, :], cc[:, 3, :], ALU.mult).then_inc(silu_ready, 1)
                    e.wait_ge(std_ready, 1)
                    newton = (rs[:, 0, 0:TT], rs[:, 1, 0:TT], rs[:, 2, 0:TT])
                    settle(v.tensor_tensor(newton[0], newton[1], newton[1], ALU.mult))
                    settle(v.tensor_tensor(newton[0], newton[0], newton[2], ALU.mult))
                    settle(v.tensor_scalar(newton[0], newton[0], -0.5, 1.5, ALU.mult, ALU.add))
                    settle(v.tensor_tensor(newton[1], newton[1], newton[0], ALU.mult))
                    for t in range(TT):
                        v.tensor_scalar(Z[:, t, :], X[:, t, :], mv[:, t, 0:1], rs[:, 1, t:t + 1],
                                        ALU.subtract, ALU.mult).then_inc(z_ready, 1)
                    e.wait_ge(const_landed, 32)
                    v.tensor_copy(identb[:, :], ident[:, :])
                    v.tensor_copy(maskb[:, :, :], masks[:, :, :])
                    e.wait_ge(filled, J_MOD + 1)
                    v.tensor_copy(modc[:, :], ps[:, J_MOD % 8, 0:12]).then_inc(emptied["V"], 1)
                    e.wait_ge(emptied["V"], emptied_count(J_MOD))
                    for n, k in enumerate((1, 4)):
                        last = v.tensor_scalar(scale1[:, 2 * n:2 * n + 2], modc[:, 2 * k:2 * k + 2], 1.0, None, ALU.add)
                    last.then_inc(mod_ready, 1)
                    for n, k in enumerate((2, 5)):
                        g = modc[:, 2 * k:2 * k + 2]
                        v.tensor_scalar(small[:, 2 * n:2 * n + 2], g, 0.0, 2.0, ALU.is_ge, ALU.mult)
                        last = v.tensor_scalar(small[:, 4 + 2 * n:6 + 2 * n], g, -1.0, None, ALU.mult)
                    settle(last)
                    for n, k in enumerate((2, 5)):
                        g = modc[:, 2 * k:2 * k + 2]
                        v.tensor_scalar(small[:, 8 + 2 * n:10 + 2 * n], small[:, 2 * n:2 * n + 2], -1.0, None, ALU.add)
                        last = v.tensor_tensor(small[:, 12 + 2 * n:14 + 2 * n], g, small[:, 4 + 2 * n:6 + 2 * n], ALU.max)
                    settle(last)
                    settle(v.tensor_scalar(small[:, 16:20], small[:, 12:16], 0.25, None, ALU.max))
                    settle(v.tensor_tensor(gates[:, :], small[:, 16:20], small[:, 8:12], ALU.mult))
                    e.wait_ge(small_landed, 16 * 6)
                    for k in range(2):
                        e.wait_ge(filled, J_ABS + k + 1)
                        v.tensor_scalar(WQf[:, 4 * k:4 * k + 4, 0, :], ps[:, (J_ABS + k) % 8, :].rearrange("p (g r) -> p g r", g=4),
                                        qnw[:, 0:1], None, ALU.mult).then_inc(emptied["V"], 1)
                    for k in range(2):
                        e.wait_ge(filled, J_ROPE + k + 1)
                        src = ps[:, (J_ROPE + k) % 8, :].rearrange("p (g a t o) -> p g a t o", g=4, a=2, o=2)
                        dst = WQf[:, 4 * k:4 * k + 4, :, :].rearrange("p g m (a t o) -> p g m a t o", a=2, o=2)
                        for a in range(2):
                            for o in range(2):
                                v.tensor_scalar(dst[:, :, 1, a, :, o], src[:, :, 1 - a, :, o], qnw[:, 0:1], None, ALU.mult)
                                last = v.tensor_scalar(dst[:, :, 2, a, :, o], src[:, :, 1 - a, :, 1 - o], qnw[:, 0:1], None, ALU.mult)
                        last.then_inc(emptied["V"], 1)
                    e.wait_ge(emptied["V"], emptied_count(J_ROPE + 1))
                    settle(v.tensor_copy(WQ[:, :, 0, :, :], WQf))
                    v.tensor_tensor(WQ[:, :, 1, :, :], WQf, WQ[:, :, 0, :, :].bitcast(F32), ALU.subtract).then_inc(wq_full, 1)
                    e.wait_ge(wo_landed, 16)
                    for a in range(DH):
                        v.tensor_scalar(WO[:, a, :], WO[:, a, :], gates[:, a:a + 1], None, ALU.mult).then_inc(wo_scaled, 1)
                    wait_emptied(e, J_PROJ + TT // 2 - 1)
                    settle(v.tensor_tensor(SQ, PJ[:, :, 0:192], PJ[:, :, 0:192], ALU.mult))
                    v.reduce_sum(rs[:, 0, 0:TT], SQ[:, :, 0:QR], AX.X)
                    settle(v.reduce_sum(rs[:, 0, TT:2 * TT], SQ[:, :, QR:192], AX.X))
                    v.tensor_scalar(rs[:, 2, 0:TT], rs[:, 0, 0:TT], 1.0 / QR, RMS_EPS, ALU.mult, ALU.add)
                    settle(v.tensor_scalar(rs[:, 2, TT:2 * TT], rs[:, 0, TT:2 * TT], 1.0 / KR, RMS_EPS, ALU.mult, ALU.add))
                    v.reciprocal(rs[:, 0, :], rs[:, 2, :]).then_inc(rms_rec, 1)
                    e.wait_ge(rope_landed, 16)
                    kr = PJ[:, :, 192:256].rearrange("p t (r o) -> p t r o", o=2)
                    kn = KN[:, :, :].rearrange("p t (m r o) -> p t m r o", m=3, o=2)
                    cosn, sinn = ropeN[:, 0, :, :], ropeN[:, 1, :, :]
                    tmp = [hT[:, 1, 1024 + 512 * 0:1024 + 512].rearrange("p (t r) -> p t r", t=TT),
                           hT[:, 1, 1536:2048].rearrange("p (t r) -> p t r", t=TT)]
                    e.wait_ge(wq_full, 1)
                    for o, (f0, f1, op) in enumerate(((cosn, sinn, ALU.subtract), (sinn, cosn, ALU.add))):
                        v.tensor_tensor(tmp[0], kr[:, :, :, 0], f0, ALU.mult)
                        settle(v.tensor_tensor(tmp[1], kr[:, :, :, 1], f1, ALU.mult))
                        for m in (0, 2):
                            last = v.tensor_tensor(kn[:, :, m, :, o], tmp[0], tmp[1], op)
                        settle(last)
                    e.wait_ge(rms_root, 1)
                    settle(v.tensor_tensor(rs[:, 0, :], rs[:, 1, :], rs[:, 1, :], ALU.mult))
                    settle(v.tensor_tensor(rs[:, 0, :], rs[:, 0, :], rs[:, 2, :], ALU.mult))
                    settle(v.tensor_scalar(rs[:, 0, :], rs[:, 0, :], -0.5, 1.5, ALU.mult, ALU.add))
                    settle(v.tensor_tensor(rs[:, 1, :], rs[:, 1, :], rs[:, 0, :], ALU.mult))
                    for t in range(TT):
                        v.tensor_scalar(PJ[:, t, 0:QR], PJ[:, t, 0:QR], rs[:, 1, t:t + 1], None, ALU.mult)
                        v.tensor_scalar(KN[:, t, 64:128], PJ[:, t, QR:192], rs[:, 1, TT + t:TT + t + 1], None,
                                        ALU.mult).then_inc(nat_ready, 1)
                    for k in range(3 * NC):
                        wait_emptied(e, J_QK + k)
                        tg, kind = k // 3, k % 3
                        hi, lo = QT if kind == 0 else K[kind - 1]
                        cols = slice(C * tg, C * tg + C)
                        settle(v.tensor_copy(hi[:, cols], TF[:, k % 4, :]))
                        v.tensor_tensor(lo[:, cols], TF[:, k % 4, :], hi[:, cols].bitcast(F32), ALU.subtract).then_inc(tf_free, 1)
                    for k in range(H // 2):
                        e.wait_ge(filled, J_WOT + k + 1)
                        v.tensor_copy(woT[:, 2 * k:2 * k + 2, :], ps[:, (J_WOT + k) % 8, :].rearrange("p (h d) -> p h d", h=2)).then_inc(emptied["V"], 1)
                    for k in range(PAIRS // 2):
                        e.wait_ge(filled, J_WVO + k + 1)
                        v.tensor_scalar(WVO[:, 2 * k:2 * k + 2, :], ps[:, (J_WVO + k) % 8, :].rearrange("p (g d) -> p g d", g=2),
                                        kvw[:, 2:3], None, ALU.mult).then_inc(emptied["V"], 1)

                @block.tensor
                def _(e):
                    t_ = nc.tensor

                    def bank(job):
                        if job >= 8:
                            wait_emptied(e, job - 8)
                        return ps[:, job % 8, :]

                    e.wait_ge(const_landed, 32)
                    e.wait_ge(wd_landed, 48)
                    b = bank(J_WD)
                    for half in range(DH):
                        for w in range(2):
                            last = t_.transpose(b[:, (2 * half + w) * P:(2 * half + w + 1) * P], WD[:, w, half * P:(half + 1) * P], ident[:, :])
                    last.then_inc(filled, 1)
                    e.wait_ge(silu_ready, 1)
                    e.wait_ge(wmod_landed, 16)
                    b = bank(J_MOD)
                    for n in range(12):
                        for a in range(DH):
                            last = t_.matmul(b[:, n:n + 1], WMOD[:, a, n * P:(n + 1) * P], cc[:, 4, a:a + 1], start=(a == 0), stop=(a == DH - 1))
                    last.then_inc(filled, 1)
                    e.wait_ge(abs_landed, 32)
                    e.wait_ge(wr_landed, 16)
                    for k in range(2):
                        b = bank(J_ABS + k)
                        for n in range(8):
                            h = 8 * k + n
                            last = t_.matmul(b[:, 64 * n:64 * n + 64], WU[:, h, :], WKV[:, 2 * h, :], start=True, stop=True)
                        last.then_inc(filled, 1)
                    for k in range(2):
                        b = bank(J_ROPE + k)
                        for n in range(4):
                            last = t_.transpose(b[:, P * n:P * n + P], WR[:, 4 * k + n, :], ident[:, :])
                        last.then_inc(filled, 1)
                    for k in range(2 * NC):
                        tg, half = k // 2, k % 2
                        b = bank(J_ZT + k)
                        for n in range(CB):
                            e.wait_ge(z_ready, CB * tg + n + 1)
                            last = t_.transpose(b[:, P * n:P * n + P], Z[:, CB * tg + n, half * P:half * P + P], ident[:, :])
                        last.then_inc(filled, 1)
                    wait_emptied(e, J_ZT + 2 * NC - 1)
                    for k in range(TT // 2):
                        b = bank(J_PROJ + k)
                        for n in range(2):
                            t = 2 * k + n
                            for a in range(DH):
                                last = t_.matmul(b[:, D * n:D * n + D], hT[:, a, P * t:P * t + P], WDT[:, a, :], start=(a == 0), stop=(a == DH - 1))
                        last.then_inc(filled, 1)
                    for k in range(3 * NC):
                        tg, kind = k // 3, k % 3
                        b = bank(J_QK + k)
                        for n in range(CB):
                            t = CB * tg + n
                            e.wait_ge(nat_ready, t + 1)
                            src = (PJ[:, t, 0:QR], KN[:, t, 64:192], KN[:, t, 0:128])[kind]
                            last = t_.transpose(b[:, P * n:P * n + P], src, ident[:, :])
                        last.then_inc(filled, 1)
                    e.wait_ge(wo_scaled, DH)
                    for k in range(H // 2):
                        b = bank(J_WOT + k)
                        for n in range(2):
                            for a in range(DH):
                                last = t_.transpose(b[:, D * n + P * a:D * n + P * a + P], WO[:, a, (2 * k + n) * VD:(2 * k + n + 1) * VD], ident[:, :])
                        last.then_inc(filled, 1)
                    wait_emptied(e, J_WOT + H // 2 - 1)
                    for k in range(PAIRS // 2):
                        b = bank(J_WVO + k)
                        for n in range(2):
                            for o in range(2):
                                h = 2 * (2 * k + n) + o
                                last = t_.matmul(b[64 * o:64 * o + 64, D * n:D * n + D], WKV[:, 2 * h + 1, :], woT[:, h, :], start=True, stop=True)
                        last.then_inc(filled, 1)

        with ExitStack() as work:
            WS = sb(work, "WS", [P, 2, 2, 3, P], F32R)
            ropeT = sb(work, "ropeT", [P, 2, 2, C])
            Qf = sb(work, "Qf", [P, 2, C])
            QH = sb(work, "QH", [P, 2, 2, C], F32R)
            QL = sb(work, "QL", [P, 2, 2, C], F32R)
            rp = sb(work, "rp", [P, 2, C])
            mp = sb(work, "mp", [P, 2 * CB, NC])
            mrow = sb(work, "mrow", [P, 2 * CB])
            mhl = sb(work, "mhl", [P, 2, 2 * CB], BF16)
            MB = sb(work, "MB", [P, 2, 2, C])
            PT = sb(work, "PT", [P, 4, 2, C])
            acc = sb(work, "acc", [P, 2, 2, C])
            Osb = sb(work, "Osb", [P, C])
            rl = sb(work, "rl", [P, C])
            ON = sb(work, "ON", [P, PAIRS, C])

            weights_staged, tables_landed = sem("weights_staged"), sem("tables_landed")
            q_projected, q_abs_copied, rope_mul, q_full = sem("q_projected"), sem("q_abs_copied"), sem("rope_mul"), sem("q_full")
            q_high, q_low = sem("q_high"), sem("q_low")
            piece_ready, piece_reduced, row_max, max_split = sem("piece_ready"), sem("piece_reduced"), sem("row_max"), sem("max_split")
            max_spread, shift_ready = sem("max_spread"), sem("shift_ready")
            scores_ready, shifted, probs_ready, probs_summed, probs_used = (
                sem("scores_ready"), sem("shifted"), sem("probs_ready"), sem("probs_summed"), sem("probs_used"))
            out_copied, sums_spread, sums_inverted, normalised = sem("out_copied"), sem("sums_spread"), sem("sums_inverted"), sem("normalised")
            projected, residual_added = sem("projected"), sem("residual_added")

            N0, O_BANK, MISC = 4, 6, 7

            def wait(e, s, value):
                if not isinstance(value, int) or value > 0:
                    e.wait_ge(s, value)

            def first_col(c, j):
                return P * max(0, j - CB * c)

            def piece_steps(c, nk):
                n = PIECES[c]
                a, b = {4: (1, 1), 8: (1, 4), 12: (2, 8), 16: (2, 12)}[nk]
                steps = [[] for _ in range(nk)]
                for i in range(n):
                    steps[a + i * (b - a + 1) // n].append(i)
                return steps, (1 if nk == 4 else nk - 3)

            def piece(c, i):
                hd, r = divmod(i, CB * (c + 1))
                b, pc = divmod(r, c + 1)
                return hd, b, pc, C * pc, min(C, P * (CB * c + b + 1) - C * pc)

            def run_bodies(e, prologue, body):
                prologue()
                for c in range(NC):
                    body(c, 0, PAIRS * c, 0, c, 1)
                    with e.Fori(0, 3) as it:
                        body(c, 1 + 2 * it, PAIRS * c + 1 + 2 * it, 1, c, 2 + 2 * it)
                        body(c, 2 + 2 * it, PAIRS * c + 2 + 2 * it, 0, c, 3 + 2 * it)
                    body(c, PAIRS - 1, PAIRS * c + PAIRS - 1, 1, c + 1, 0)

            def is_first(p):
                return isinstance(p, int) and p == 0

            with nc.Block() as block:
                @block.sync
                def _(e):
                    tabs = rope_q.rearrange("k p (c n) -> p c k n", c=NC)

                    def tables(c):
                        e.dma_start(ropeT[:, c % 2, :, :], tabs[:, c, :, :]).then_inc(tables_landed, 16)

                    def stage(g, p, par):
                        wait(e, q_projected, g - 1)
                        wait(e, weights_staged, 16 * g)
                        e.dma_start(WS[:, par, :, :, :].rearrange("p a m r -> p (a m r)").bitcast(F32),
                                    WQ[:, bass.ds(p, 1) if not isinstance(p, int) else slice(p, p + 1), :, :, :].rearrange("p g a m r -> p (g a m r)").bitcast(F32)).then_inc(weights_staged, 16)

                    def body(c, p, g, par, c2, p2):
                        if is_first(p) and 1 <= c < NC - 1:
                            e.wait_ge(rope_mul, 2 * PAIRS * c)
                            e.wait_ge(tables_landed, 16 * (c + 1))
                            tables(c + 1)
                        if c2 < NC:
                            stage(g + 1, p2, 1 - par)

                    def prologue():
                        tables(0)
                        stage(0, 0, 0)
                        e.wait_ge(tables_landed, 16)
                        tables(1)

                    run_bodies(e, prologue, body)

                @block.tensor
                def _(e):
                    t_ = nc.tensor

                    def project_queries(c, g, par):
                        e.wait_ge(weights_staged, 16 * (g + 1))
                        wait(e, shift_ready, g)
                        wait(e, sums_inverted, g - 1)
                        for m, b in enumerate((N0, N0 + 1, MISC)):
                            for k, (w, q) in enumerate(((0, 0), (0, 1), (1, 0))):
                                last = t_.matmul(ps[:, b, :], WS[:, par, w, m, :], QT[q][:, C * c:C * c + C], start=(k == 0), stop=(k == 2))
                        last.then_inc(q_projected, 1)

                    def max_piece(c, p, par, i):
                        hd, b, pc, key, w = piece(c, i)
                        if i >= 2:
                            wait(e, piece_reduced, pieces_before(c, p) + i - 1)
                        dst = ps[:, N0 + i % 2, 0:w]
                        diag = pc == c
                        last = t_.matmul(dst, QH[:, par, hd, P * b:P * b + P], K[hd][0][:, key:key + w], start=True, stop=not diag)
                        if diag:
                            last = t_.matmul(ps[:, N0 + i % 2, w - P:w], identb[:, :], maskb[:, 0, :], start=False, stop=True)
                        last.then_inc(piece_ready, 1)

                    def spread_maxima(g):
                        e.wait_ge(max_split, 2 * (g + 1))
                        for hd in range(2):
                            for b in range(CB):
                                for part in range(2):
                                    col = mhl[:, part, hd * CB + b:hd * CB + b + 1]
                                    last = t_.matmul(ps[:, N0 + hd, P * b:P * b + P], col.to_broadcast([P, P]), identb[:, :],
                                                     start=(part == 0), stop=(part == 1))
                        last.then_inc(max_spread, 1)

                    def scores(c, n, g, par, j):
                        if j == 0:
                            e.wait_ge(q_low, g + 1)
                        wait(e, shifted, n - 1)
                        x0 = first_col(c, j)
                        masked = j >= CB * c
                        for hd in range(2):
                            b = 2 * (j % 2) + hd
                            for k, (w, q) in enumerate(((0, QH), (0, QL), (1, QH))):
                                last = t_.matmul(ps[:, b, x0:C], K[hd][w][:, P * j:P * j + P], q[:, par, hd, x0:C], start=(k == 0),
                                                 stop=(k == 2 and not masked))
                            if masked:
                                last = t_.matmul(ps[:, b, x0:x0 + P], identb[:, :], maskb[:, 1, :], start=False, stop=True)
                        last.then_inc(scores_ready, 1)

                    def weigh_values(c, n, g, j):
                        e.wait_ge(probs_ready, n + 1)
                        if j == 0:
                            wait(e, out_copied, g)
                        x0 = first_col(c, j)
                        for hd in range(2):
                            last = t_.matmul(ps[64 * hd:64 * hd + 64, O_BANK, x0:C], KN[:, j, 64:128], PT[:, j % 4, hd, x0:C],
                                             start=(j == 0), stop=(j == UNITS[c] - 1))
                        last.then_inc(probs_used, 1)

                    def spread_sums(c, n_end, g, par, g_made):
                        e.wait_ge(probs_summed, n_end)
                        e.wait_ge(rope_mul, 2 * g_made)
                        for hd in range(2):
                            last = t_.matmul(ps[64 * hd:64 * hd + 64, MISC, :], ones[:, :], acc[:, par, hd, :], start=True, stop=True)
                        last.then_inc(sums_spread, 1)

                    def project_out(c, made):
                        e.wait_ge(normalised, PAIRS * (c + 1))
                        e.wait_ge(rope_mul, 2 * made)
                        for half in range(2):
                            if half:
                                e.wait_ge(residual_added, 2 * c + 1)
                            for n in range(2):
                                b = 2 * half + n
                                for g in range(PAIRS):
                                    last = t_.matmul(ps[:, MISC, D * n:D * n + D], ON[:, g, P * b:P * b + P], WVO[:, g, :],
                                                     start=(g == 0), stop=(g == PAIRS - 1))
                            last.then_inc(projected, 1)

                    def body(c, p, g, par, c2, p2):
                        nk, n0 = UNITS[c], units_before(c, p)
                        if c2 < NC:
                            steps, spread = piece_steps(c2, nk)
                        for j in range(nk):
                            if j + 2 < nk:
                                scores(c, n0 + j + 2, g, par, j + 2)
                            elif c2 < NC:
                                scores(c2, n0 + j + 2, g + 1, 1 - par, j + 2 - nk)
                            if c2 < NC:
                                if j == 0:
                                    project_queries(c2, g + 1, 1 - par)
                                for k, i in enumerate(steps[j]):
                                    if i == 0:
                                        e.wait_ge(q_high, g + 2)
                                    max_piece(c2, p2, 1 - par, i)
                                if j == spread:
                                    spread_maxima(g + 1)
                            if is_first(p) and c >= 1 and j == 1:
                                project_out(c - 1, PAIRS * c + 2)
                            weigh_values(c, n0 + j, g, j)
                        if is_first(p) and c >= 1:
                            e.wait_ge(residual_added, 2 * c)
                        spread_sums(c, n0 + nk, g, par, g + 2 if c2 < NC else PAIRS * NC)

                    def prologue():
                        project_queries(0, 0, 0)
                        e.wait_ge(q_high, 1)
                        for i in range(PIECES[0]):
                            max_piece(0, 0, 0, i)
                        spread_maxima(0)
                        scores(0, 0, 0, 0, 0)
                        scores(0, 1, 0, 0, 1)

                    run_bodies(e, prologue, body)
                    e.wait_ge(sums_inverted, PAIRS * NC)
                    project_out(NC - 1, PAIRS * NC)

                @block.vector
                def _(e):
                    v = nc.vector

                    def rope_queries(c, g, par):
                        e.wait_ge(tables_landed, 16 * (c + 1))
                        e.wait_ge(q_projected, g + 1)
                        wait(e, q_full, 2 * g)
                        v.tensor_tensor(rp[:, 0, :], ps[:, N0 + 1, :], ropeT[:, c % 2, 0, :], ALU.mult).then_inc(rope_mul, 1)
                        v.tensor_tensor(rp[:, 1, :], ps[:, MISC, :], ropeT[:, c % 2, 1, :], ALU.mult).then_inc(rope_mul, 1)
                        e.wait_ge(rope_mul, 2 * (g + 1))
                        wait(e, q_low, g)
                        v.tensor_tensor(Qf[64:128, 0, :], rp[64:128, 0, :], rp[64:128, 1, :], ALU.add).then_inc(q_full, 1)
                        v.tensor_tensor(Qf[0:64, 1, :], rp[0:64, 0, :], rp[0:64, 1, :], ALU.add).then_inc(q_full, 1)

                    def reduce_piece(c, p, i):
                        hd, b, pc, key, w = piece(c, i)
                        e.wait_ge(piece_ready, pieces_before(c, p) + i + 1)
                        v.reduce_max(mp[:, hd * CB + b, pc:pc + 1], ps[:, N0 + i % 2, 0:w], AX.X).then_inc(piece_reduced, 1)

                    def split_maxima(c, p, g):
                        e.wait_ge(piece_reduced, pieces_before(c, p) + PIECES[c])
                        v.reduce_max(mrow[:, :], mp[:, :, 0:c + 1], AX.X).then_inc(row_max, 1)
                        e.wait_ge(row_max, g + 1)
                        wait(e, max_spread, g)
                        v.tensor_copy(mhl[:, 0, :], mrow[:, :]).then_inc(max_split, 1)
                        e.wait_ge(max_split, 2 * g + 1)
                        v.tensor_tensor(mhl[:, 1, :], mrow[:, :], mhl[:, 0, :], ALU.subtract).then_inc(max_split, 1)

                    def shift(c, n, g, par, j):
                        if j == 0:
                            e.wait_ge(shift_ready, g + 1)
                        e.wait_ge(scores_ready, n + 1)
                        wait(e, probs_used, n - 3)
                        wait(e, probs_summed, n - 3)
                        x0 = first_col(c, j)
                        b = 2 * (j % 2)
                        v.tensor_tensor(PT[:, j % 4, :, x0:C], ps[:, b:b + 2, x0:C], MB[:, par, :, x0:C], ALU.subtract).then_inc(shifted, 1)

                    def normalise(g, p):
                        e.wait_ge(sums_spread, g + 1)
                        wait(e, normalised, g)
                        v.reciprocal(rl[:, :], ps[:, MISC, :]).then_inc(sums_inverted, 1)
                        e.wait_ge(sums_inverted, g + 1)
                        e.wait_ge(out_copied, g + 1)
                        dst = ON[:, p, :] if isinstance(p, int) else ON[:, bass.ds(p, 1), :].rearrange("p g n -> p (g n)")
                        v.tensor_tensor(dst, Osb[:, :], rl[:, :], ALU.mult).then_inc(normalised, 1)

                    def add_residual(c):
                        for half in range(2):
                            e.wait_ge(projected, 2 * c + half + 1)
                            rows = slice(CB * c + 2 * half, CB * c + 2 * half + 2)
                            v.tensor_tensor(X[:, rows, :], ps[:, MISC, :].rearrange("p (t d) -> p t d", t=2), X[:, rows, :],
                                            ALU.add).then_inc(residual_added, 1)

                    def body(c, p, g, par, c2, p2):
                        nk, n0 = UNITS[c], units_before(c, p)
                        if c2 < NC:
                            steps, spread = piece_steps(c2, nk)
                        for j in range(nk):
                            if j + 2 < nk:
                                shift(c, n0 + j + 2, g, par, j + 2)
                            elif c2 < NC:
                                shift(c2, n0 + j + 2, g + 1, 1 - par, j + 2 - nk)
                            if c2 < NC:
                                if j == 0:
                                    rope_queries(c2, g + 1, 1 - par)
                                for i in steps[j]:
                                    reduce_piece(c2, p2, i)
                                if j == spread:
                                    split_maxima(c2, p2, g + 1)
                            if is_first(p) and c >= 1 and j == 1:
                                add_residual(c - 1)
                        normalise(g, p)

                    def prologue():
                        rope_queries(0, 0, 0)
                        for i in range(PIECES[0]):
                            reduce_piece(0, 0, i)
                        split_maxima(0, 0, 0)
                        shift(0, 0, 0, 0, 0)
                        shift(0, 1, 0, 0, 1)

                    run_bodies(e, prologue, body)
                    add_residual(NC - 1)

                @block.scalar
                def _(e):
                    def copy_queries(g, par):
                        e.wait_ge(q_projected, g + 1)
                        wait(e, q_low, g)
                        e.activation(Qf[0:64, 0, :], ps[0:64, N0, :], ACT.Copy).then_inc(q_abs_copied, 1)
                        e.activation(Qf[64:128, 1, :], ps[64:128, N0, :], ACT.Copy).then_inc(q_abs_copied, 1)
                        e.wait_ge(q_abs_copied, 2 * (g + 1))
                        e.wait_ge(q_full, 2 * (g + 1))
                        e.activation(QH[:, par, :, :], Qf[:, :, :], ACT.Copy).then_inc(q_high, 1)

                    def copy_shift(g, par):
                        e.wait_ge(max_spread, g + 1)
                        e.activation(MB[:, par, :, :], ps[:, N0:N0 + 2, :], ACT.Copy).then_inc(shift_ready, 1)

                    def exponentials(c, n, j):
                        e.wait_ge(shifted, n + 1)
                        x0 = first_col(c, j)
                        e.activation(PT[:, j % 4, :, x0:C], PT[:, j % 4, :, x0:C], ACT.Exp, scale=SCALE).then_inc(probs_ready, 1)

                    def body(c, p, g, par, c2, p2):
                        nk, n0 = UNITS[c], units_before(c, p)
                        spread = piece_steps(c2, nk)[1] if c2 < NC else None
                        for j in range(nk):
                            if j + 2 < nk:
                                exponentials(c, n0 + j + 2, j + 2)
                            elif c2 < NC:
                                exponentials(c2, n0 + j + 2, j + 2 - nk)
                            if c2 < NC:
                                if j == 0:
                                    copy_queries(g + 1, 1 - par)
                                if j == spread:
                                    copy_shift(g + 1, 1 - par)
                        e.wait_ge(probs_used, n0 + nk)
                        wait(e, normalised, g)
                        e.activation(Osb[:, :], ps[:, O_BANK, :], ACT.Copy).then_inc(out_copied, 1)

                    def prologue():
                        copy_queries(0, 0)
                        copy_shift(0, 0)
                        exponentials(0, 0, 0)
                        exponentials(0, 1, 1)

                    run_bodies(e, prologue, body)

                @block.gpsimd
                def _(e):
                    def split_queries(g, par):
                        e.wait_ge(q_high, g + 1)
                        e.tensor_tensor(QL[:, par, :, :], Qf[:, :, :], QH[:, par, :, :].bitcast(F32), ALU.subtract).then_inc(q_low, 1)

                    def sum_probs(c, n, g, par, j):
                        e.wait_ge(probs_ready, n + 1)
                        wait(e, probs_summed, n)
                        x0 = first_col(c, j)
                        a, pt = acc[:, par, :, x0:C], PT[:, j % 4, :, x0:C]
                        if j == 0:
                            wait(e, sums_spread, g - 1)
                            e.tensor_tensor(a, pt, ones[:, 0:1].unsqueeze(2).to_broadcast([P, 2, C]), ALU.mult).then_inc(probs_summed, 1)
                        else:
                            e.tensor_tensor(a, a, pt, ALU.add).then_inc(probs_summed, 1)

                    def body(c, p, g, par, c2, p2):
                        nk, n0 = UNITS[c], units_before(c, p)
                        for j in range(nk):
                            if j + 2 < nk:
                                sum_probs(c, n0 + j + 2, g, par, j + 2)
                            elif c2 < NC:
                                sum_probs(c2, n0 + j + 2, g + 1, 1 - par, j + 2 - nk)
                            if c2 < NC and j == 0:
                                split_queries(g + 1, 1 - par)

                    def prologue():
                        split_queries(0, 0)
                        sum_probs(0, 0, 0, 0, 0)
                        sum_probs(0, 1, 0, 0, 1)

                    run_bodies(e, prologue, body)
        attn_kept.close()

        ffn(nc, base, sb, sem, ps, X, ident, modc, scale1, gates, st, mv, rs,
            wq_gate, s_gate, wq_up_ffn, s_up, wq_down_ffn, s_down, out)


def ffn(nc, base, sb, sem, ps, X, ident, modc, scale1, gates, st, mv, rs,
        wq_gate, s_gate, wq_up_ffn, s_up, wq_down_ffn, s_down, out):
    ZERO_POINT = 128.0
    with ExitStack() as work:
        WI = [sb(work, f"wi_{n}", [P, HB, D], I32) for n in ("gate", "up")]
        WID = sb(work, "wi_down", [P, DH, HID], I32)
        WF = sb(work, "wf", [P, 2, HB, D])
        WFD = sb(work, "wfd", [P, DH, HB * P])
        WT = [sb(work, f"wt_{n}", [P, 2, DH, HB * P], F32R) for n in ("hi", "lo")]
        WTf = sb(work, "wtf", [P, 2, DH, HB * P])
        WDN = sb(work, "wdn", [P, HB, D])
        sc = sb(work, "sc", [P, 2, HB])
        sd = sb(work, "sd", [P, 2, DH])
        Z = sb(work, "Z2", [P, CB, D])
        hF = sb(work, "hF", [P, DH, C])
        hH = sb(work, "hH", [P, DH, C], F32R)
        hL = sb(work, "hL", [P, DH, C], F32R)
        SG = sb(work, "SG", [P, 2, C])
        AT = sb(work, "AT", [P, HB, C])

        scales_landed, wi_landed, scales_cleared = sem("scales_landed"), sem("wi_landed"), sem("scales_cleared")
        f_step, f_filled, f_emptied = sem("ffn_vector_step"), sem("ffn_bank_filled"), sem("ffn_bank_emptied")
        f_rec, f_root, f_z, dequant = sem("ffn_var_rec"), sem("ffn_root"), sem("ffn_z_ready"), sem("dequantised")
        w_ready, h_filled, h_full, h_high, h_low = sem("ffn_weights_ready"), sem("h_filled"), sem("h_full"), sem("h_high"), sem("h_low")
        gu_ready, silu_done, act_ready, down_ready, out_ready, stored = (
            sem("gate_up_ready"), sem("silu_done"), sem("act_ready"), sem("down_ready"), sem("out_ready"), sem("stored"))
        ov = out.rearrange("a (t p) d -> p (a t) d", p=P)
        HLAST = HID - (HB - 1) * P
        F_JOBS = 2 * 2 * 3 // 1

        with nc.Block() as block:
            @block.sync
            def _(e):
                e.wait_ge(scales_cleared, 2)
                for n, (w, s) in enumerate(((wq_gate, s_gate), (wq_up_ffn, s_up))):
                    e.dma_start(WI[n][:, 0:HB - 1, :], w[0:(HB - 1) * P, :].rearrange("(b p) d -> p b d", p=P)).then_inc(wi_landed, 16)
                    e.dma_start(WI[n][0:HLAST, HB - 1, :], w[(HB - 1) * P:HID, :]).then_inc(wi_landed, 16)
                    e.dma_start(sc[:, n, 0:HB - 1], s[0:(HB - 1) * P].rearrange("(b p) -> p b", p=P)).then_inc(scales_landed, 16)
                    e.dma_start(sc[0:HLAST, n, HB - 1:HB], s[(HB - 1) * P:HID].rearrange("(p b) -> p b", b=1)).then_inc(scales_landed, 16)
                e.dma_start(WID[:, :, :], wq_down_ffn.rearrange("(a p) n -> p a n", p=P)).then_inc(wi_landed, 16)
                e.dma_start(sd[:, 0, :], s_down.rearrange("(a p) -> p a", p=P)).then_inc(scales_landed, 16)
                for c in range(NC):
                    e.wait_ge(out_ready, 2 * (c + 1))
                    e.dma_start(ov[:, CB * c:CB * c + CB, :], X[:, CB * c:CB * c + CB, :]).then_inc(stored, 16)
                e.wait_ge(stored, 16 * NC)

            @block.gpsimd
            def _(e):
                e.memset(sc[:, :, :], 0.0).then_inc(scales_cleared, 1)
                e.memset(WI[0][:, HB - 1, :], 0)
                e.memset(WI[1][:, HB - 1, :], 0).then_inc(scales_cleared, 1)
                e.memset(WFD[:, :, HID:HB * P], 0.0).then_inc(dequant, 1)

            @block.scalar
            def _(e):
                e.wait_ge(f_rec, 1)
                e.activation(rs[:, 1, 0:TT], rs[:, 0, 0:TT], ACT.Sqrt).then_inc(f_root, 1)
                with e.Fori(0, NC) as c:
                    for a in range(DH):
                        e.wait_ge(h_filled, DH * c + a + 1)
                        if a == 0:
                            e.wait_ge(h_low, c)
                        e.activation(hF[:, a, :], ps[:, a, :], ACT.Identity, bias=modc[:, 6 + a:7 + a],
                                     scale=scale1[:, 2 + a:3 + a]).then_inc(h_full, 1)
                    e.wait_ge(h_full, DH * c + DH)
                    e.activation(hH[:, :, :], hF[:, :, :], ACT.Copy).then_inc(h_high, 1)
                    for hb in range(HB):
                        e.wait_ge(gu_ready, HB * c + hb + 1)
                        if hb >= 2:
                            e.wait_ge(act_ready, HB * c + hb - 1)
                        else:
                            e.wait_ge(act_ready, HB * c)
                        e.activation(SG[:, hb % 2, :], ps[:, 2 + 2 * (hb % 2), :], ACT.Silu).then_inc(silu_done, 1)

            @block.vector
            def _(e):
                v = nc.vector
                steps = [0]

                def settle(ins):
                    steps[0] += 1
                    ins.then_inc(f_step, 1)
                    e.wait_ge(f_step, steps[0])

                for t in range(TT):
                    last = v.bn_stats(st[:, t, :], X[:, t, :])
                settle(last)
                for t in range(TT):
                    last = v.bn_aggr(mv[:, t, :], st[:, t, :])
                settle(last)
                settle(v.tensor_scalar(rs[:, 2, 0:TT], mv[:, :, 1], LN_EPS, None, ALU.add))
                v.reciprocal(rs[:, 0, 0:TT], rs[:, 2, 0:TT]).then_inc(f_rec, 1)
                e.wait_ge(scales_landed, 16 * 5)
                e.wait_ge(wi_landed, 16 * 5)
                settle(v.tensor_tensor(sd[:, 1, :], sd[:, 0, :], gates[:, 2:4], ALU.mult))
                for n in range(2):
                    for b in range(HB):
                        v.tensor_scalar(WF[:, n, b, :], WI[n][:, b, :], ZERO_POINT, sc[:, n, b:b + 1], ALU.subtract, ALU.mult)
                for a in range(DH):
                    last = v.tensor_scalar(WFD[:, a, 0:HID], WID[:, a, :], ZERO_POINT, sd[:, 1, a:a + 1], ALU.subtract, ALU.mult)
                last.then_inc(dequant, 1)
                e.wait_ge(f_root, 1)
                settle(v.tensor_tensor(rs[:, 0, 0:TT], rs[:, 1, 0:TT], rs[:, 1, 0:TT], ALU.mult))
                settle(v.tensor_tensor(rs[:, 0, 0:TT], rs[:, 0, 0:TT], rs[:, 2, 0:TT], ALU.mult))
                settle(v.tensor_scalar(rs[:, 0, 0:TT], rs[:, 0, 0:TT], -0.5, 1.5, ALU.mult, ALU.add))
                settle(v.tensor_tensor(rs[:, 1, 0:TT], rs[:, 1, 0:TT], rs[:, 0, 0:TT], ALU.mult))
                wtf = WTf[:, :, :, :].rearrange("p n a h -> p (n a h)")
                for k in range(6):
                    e.wait_ge(f_filled, k + 1)
                    v.tensor_copy(wtf[:, C * k:C * k + C], ps[:, k, :]).then_inc(f_emptied, 1)
                e.wait_ge(f_emptied, 6)
                settle(v.tensor_copy(WT[0][:, :, :, :], WTf[:, :, :, :]))
                v.tensor_tensor(WT[1][:, :, :, :], WTf[:, :, :, :], WT[0][:, :, :, :].bitcast(F32), ALU.subtract)
                for k in range(3):
                    e.wait_ge(f_filled, 6 + k + 1)
                    last = v.tensor_copy(WDN[:, 2 * k:2 * k + 2, :], ps[:, (6 + k) % 8, :].rearrange("p (b d) -> p b d", b=2))
                    last.then_inc(f_emptied, 1)
                e.wait_ge(f_emptied, 9)
                v.tensor_copy(sd[:, 0, :], sd[:, 1, :]).then_inc(w_ready, 1)
                with e.Fori(0, NC) as c:
                    e.wait_ge(h_filled, DH * c)
                    for n in range(CB):
                        t = bass.ds(CB * c + n, 1)
                        last = v.tensor_scalar(Z[:, n, :], X[:, t, :].rearrange("p a d -> p (a d)"),
                                               mv[:, t, 0:1].rearrange("p a d -> p (a d)"), rs[:, 1, t], ALU.subtract, ALU.mult)
                    last.then_inc(f_z, 1)
                    e.wait_ge(h_high, c + 1)
                    v.tensor_tensor(hL[:, :, :], hF[:, :, :], hH[:, :, :].bitcast(F32), ALU.subtract).then_inc(h_low, 1)
                    for hb in range(HB):
                        e.wait_ge(silu_done, HB * c + hb + 1)
                        if hb == 0:
                            e.wait_ge(down_ready, 2 * c)
                        v.tensor_tensor(AT[:, hb, :], ps[:, 3 + 2 * (hb % 2), :], SG[:, hb % 2, :], ALU.mult).then_inc(act_ready, 1)
                    for k in range(2):
                        e.wait_ge(down_ready, 2 * c + k + 1)
                        rows = X[:, bass.ds(CB * c + 2 * k, 2), :]
                        v.tensor_tensor(rows, ps[:, 6 + k, :].rearrange("p (t d) -> p t d", t=2), rows, ALU.add).then_inc(out_ready, 1)

            @block.tensor
            def _(e):
                t_ = nc.tensor
                e.wait_ge(dequant, 2)
                blocks = [(n, a, b) for n in range(2) for a in range(DH) for b in range(HB)]
                for k in range(6):
                    for m in range(4):
                        n, a, b = blocks[4 * k + m]
                        last = t_.transpose(ps[:, k, P * m:P * m + P], WF[:, n, b, P * a:P * a + P], ident[:, :])
                    last.then_inc(f_filled, 1)
                for k in range(3):
                    if k == 2:
                        e.wait_ge(f_emptied, 1)
                    for m in range(2):
                        for a in range(DH):
                            last = t_.transpose(ps[:, (6 + k) % 8, D * m + P * a:D * m + P * a + P],
                                                WFD[:, a, P * (2 * k + m):P * (2 * k + m) + P], ident[:, :])
                    last.then_inc(f_filled, 1)
                e.wait_ge(f_emptied, 9)
                e.wait_ge(w_ready, 1)
                with e.Fori(0, NC) as c:
                    e.wait_ge(f_z, c + 1)
                    e.wait_ge(h_full, DH * c)
                    for a in range(DH):
                        for n in range(CB):
                            last = t_.transpose(ps[:, a, P * n:P * n + P], Z[:, n, P * a:P * a + P], ident[:, :])
                        last.then_inc(h_filled, 1)
                    e.wait_ge(h_low, c + 1)
                    for hb in range(HB):
                        if hb >= 2:
                            e.wait_ge(act_ready, HB * c + hb - 1)
                        else:
                            e.wait_ge(act_ready, HB * c)
                        for n in range(2):
                            k = 0
                            for a in range(DH):
                                for w, h in ((0, hH), (0, hL), (1, hH)):
                                    last = t_.matmul(ps[:, 2 + 2 * (hb % 2) + n, :], WT[w][:, n, a, P * hb:P * hb + P], h[:, a, :],
                                                     start=(k == 0), stop=(k == 5))
                                    k += 1
                        last.then_inc(gu_ready, 1)
                    e.wait_ge(act_ready, HB * (c + 1))
                    e.wait_ge(out_ready, 2 * c)
                    for k in range(2):
                        for m in range(2):
                            b = 2 * k + m
                            for hb in range(HB):
                                last = t_.matmul(ps[:, 6 + k, D * m:D * m + D], AT[:, hb, P * b:P * b + P], WDN[:, hb, :],
                                                 start=(hb == 0), stop=(hb == HB - 1))
                        last.then_inc(down_ready, 1)


_INS = ["L0_attn_x", "L0_attn_wq_down", "L0_attn_q_norm_w", "L0_attn_wq_up", "L0_attn_wq_rope", "L0_attn_wkv_down",
        "L0_attn_kv_norm_w", "L0_attn_wkv_up", "L0_attn_wk_rope", "L0_attn_wo", "L0_ffn_wq_gate", "L0_ffn_s_gate",
        "L0_ffn_wq_up", "L0_ffn_s_up", "L0_ffn_wq_down", "L0_ffn_s_down", "L0_c", "L0_wmod"]


def shape_constants():
    inv = np.float32(1.0) / np.power(np.float32(10000.0), np.arange(0, ROPE, 2, dtype=np.float32) / np.float32(ROPE))
    angle = np.outer(np.arange(S, dtype=np.float32), inv.astype(np.float32)).astype(np.float32)
    cos, sin = np.cos(angle).astype(np.float32), np.sin(angle).astype(np.float32)
    row = np.arange(P)
    masks = np.stack([np.where(row[None, :] > row[:, None], NEG, 0.0), np.where(row[:, None] > row[None, :], NEG, 0.0)]).astype(np.float32)
    cosq = np.repeat(cos.T, 2, axis=0)
    sinq = np.repeat(sin.T, 2, axis=0) * np.tile([-1.0, 1.0], ROPE // 2)[:, None]
    rope_q = np.stack([np.concatenate([cosq, cosq]), np.concatenate([sinq, sinq])]).astype(np.float32)
    return {"ident": np.eye(P, dtype=np.float32), "masks": masks, "rope_nat": np.stack([cos, sin]), "rope_q": rope_q}


def kernel(**inputs):
    import concourse.bacc as _bacc
    from concourse import mybir as _mybir
    from concourse.bass_utils import run_bass_kernel_spmd as _run

    nc = _bacc.Bacc("TRN2", target_bir_lowering=False, num_devices=1)
    arrays, args = {}, []
    given = [(n, inputs[n]) for n in _INS] + list(shape_constants().items())
    for name, value in given:
        a = np.ascontiguousarray(value)
        arrays[f"in_{name}_dram"] = a
        args.append(nc.dram_tensor(f"in_{name}_dram", a.shape, _mybir.dt.from_np(a.dtype), kind="ExternalInput").ap())
    out = nc.dram_tensor("out_0_dram", (1, S, D), _mybir.dt.float32, kind="ExternalOutput").ap()
    build(nc, *args, out)
    r = _run(nc, [arrays], core_ids=[0])
    return r.results[0]["out_0_dram"]
```

```python
from contextlib import ExitStack

import numpy as np

import concourse.bass as bass
from concourse import mybir

F32 = mybir.dt.float32
F32R = mybir.dt.float32r
BF16 = mybir.dt.bfloat16
I32 = mybir.dt.int32
ALU = mybir.AluOpType
ACT = mybir.ActivationFunctionType
AX = mybir.AxisListType

P = 128
S = 2048
D = 256
DH = D // P
H = 16
PAIRS = H // 2
NOPE, ROPE, VD = 128, 64, 128
QR, KR = 128, 64
HID = 704
HB = 6
TT = S // P
C = 512
NC = S // C
CB = C // P
NEG = -1.0e30
SCALE = float(1.0 / np.sqrt(NOPE + ROPE))
LN_EPS, RMS_EPS = 1e-5, 1e-6

UNITS = [CB * (c + 1) for c in range(NC)]
U0 = [sum(UNITS[:c]) for c in range(NC + 1)]
STEPS = U0[NC]
PIECES = 2 * STEPS
LEAD = 22


def build(nc, x, wq_down, q_norm_w, wq_up, wq_rope, wkv_down, kv_norm_w, wkv_up, wk_rope, wo,
          wq_gate, s_gate, wq_up_ffn, s_up, wq_down_ffn, s_down, cvec, wmod,
          ident_c, masks_c, rope_nat, rope_q, out):
    with ExitStack() as base:
        base.enter_context(nc.allow_non_contiguous_dma(reason="vectors of a few hundred elements laid over the partitions"))
        def sb(stack, name, shape, dt=F32):
            return stack.enter_context(nc.sbuf_tensor(name, shape, dt))

        def sem(name):
            return base.enter_context(nc.semaphore(name))

        ps = base.enter_context(nc.psum_tensor("ps", [P, 8, C], F32))
        wq_d = nc.dram_tensor("wq_scratch", (PAIRS, P, 2 * 3 * P), F32, kind="Internal").ap()
        o_d = nc.dram_tensor("o_scratch", (PAIRS, P, S), F32, kind="Internal").ap()
        l_d = nc.dram_tensor("l_scratch", (H, S), F32, kind="Internal").ap()
        r_d = nc.dram_tensor("r_scratch", (H, S), F32, kind="Internal").ap()
        X = sb(base, "X", [P, TT, D])
        ident = sb(base, "ident", [P, P])
        identb = sb(base, "identb", [P, P], BF16)
        masks = sb(base, "masks", [P, 2, P])
        maskb = sb(base, "maskb", [P, 2, P], BF16)
        ones = sb(base, "ones", [P, 64])
        WVO = sb(base, "WVO", [P, PAIRS, D])
        modc = sb(base, "modc", [P, 12])
        scale1 = sb(base, "scale1", [P, 4])
        gates = sb(base, "gates", [P, 4])
        small = sb(base, "small", [P, 64])
        st = sb(base, "st", [P, TT, 6])
        mv = sb(base, "mv", [P, TT, 2])
        rs = sb(base, "rs", [P, 3, 2 * TT])

        attn_kept = base.enter_context(ExitStack())
        QT = [sb(attn_kept, n, [P, S], F32R) for n in ("qt_hi", "qt_lo")]
        K = [[sb(attn_kept, f"k{v}_{n}", [P, S], F32R) for n in ("hi", "lo")] for v in range(2)]
        KN = sb(attn_kept, "KN", [P, TT, 192])

        with ExitStack() as scratch:
            Z = sb(scratch, "Z", [P, TT, D])
            hT = sb(scratch, "hT", [P, DH, S])
            WU = sb(scratch, "WU", [P, H, QR])
            WKV = sb(scratch, "WKV", [P, 2 * H, KR])
            WR = sb(scratch, "WR", [P, PAIRS, QR])
            WO = sb(scratch, "WO", [P, DH, H * VD])
            WMOD = sb(scratch, "WMOD", [P, DH, 6 * D])
            WD = sb(scratch, "WD", [P, 2, D])
            WDT = sb(scratch, "WDT", [P, DH, D])
            ropeN = sb(scratch, "ropeN", [P, 2, TT, ROPE // 2])
            cc = sb(scratch, "cc", [P, 6, DH])
            qnw = sb(scratch, "qnw", [P, 1])
            kvw = sb(scratch, "kvw", [P, 3])
            WQ = sb(scratch, "WQ", [P, PAIRS, 2, 3, P], F32R)
            PJ = Z
            SQ = hT[:, :, :].rearrange("p a b -> p (a b)")[:, 0:TT * 192].rearrange("p (t c) -> p t c", t=TT)
            woT = hT[:, :, :].rearrange("p a (h d) -> p (a h) d", d=D)
            WQf = KN[:, :, :].rearrange("p t c -> p (t c)").rearrange("p (g m r) -> p g m r", g=PAIRS, m=3)
            TF = WMOD[:, :, :].rearrange("p a b -> p (a b)")[:, 0:4 * C].rearrange("p (s c) -> p s c", s=4)

            jobs = (["A"] + ["V"] + ["V"] * 4 + ["A"] * 8 + ["A"] * 8 + ["A"] * 12 + ["V"] * 8 + ["V"] * 4)
            J_WD, J_MOD, J_ABS, J_ROPE, J_ZT, J_PROJ, J_QK, J_WOT, J_WVO = 0, 1, 2, 4, 6, 14, 22, 34, 42

            x_landed, small_landed, wd_landed, abs_landed = [sem(f"x_landed_{q}") for q in range(4)], sem("small_landed"), sem("wd_landed"), sem("abs_landed")
            wr_landed = sem("wr_landed")
            const_landed, rope_landed, wmod_landed, wo_landed = sem("const_landed"), sem("rope_landed"), sem("wmod_landed"), sem("wo_landed")
            filled = sem("prep_bank_filled")
            emptied = {"A": sem("prep_emptied_by_scalar"), "V": sem("prep_emptied_by_vector")}
            dve_step, act_step = sem("prep_vector_step"), sem("prep_scalar_step")
            z_ready, silu_exp, var_rec, std_ready = sem("z_ready"), sem("silu_exp"), sem("var_rec"), sem("std_ready")
            silu_ready, mod_ready, rms_rec, rms_root = sem("silu_ready"), sem("mod_ready"), sem("rms_rec"), sem("rms_root")
            wq_stored = sem("wq_stored")
            ones_set, wq_full, nat_ready, wo_scaled, tf_free = sem("ones_set"), sem("wq_full"), sem("nat_ready"), sem("wo_scaled"), sem("tf_free")

            def emptied_count(job):
                return sum(1 for e in jobs[:job + 1] if e == jobs[job])

            def wait_emptied(e, job):
                e.wait_ge(emptied[jobs[job]], emptied_count(job))

            with nc.Block() as block:
                @block.sync
                def _(e):
                    xv = x.rearrange("a (t p) d -> p (a t) d", p=P)
                    for q in range(4):
                        e.dma_start(X[:, 4 * q:4 * q + 4, :], xv[:, 4 * q:4 * q + 4, :]).then_inc(x_landed[q], 16)
                    e.dma_start(WMOD[:, :, :], wmod.rearrange("(a p) n -> p a n", p=P)).then_inc(wmod_landed, 16)
                    e.dma_start(WR[:, :, :], wq_rope.rearrange("(g p) r -> p g r", p=P)).then_inc(wr_landed, 16)
                    e.dma_start(WO[:, :, :], wo.rearrange("(a p) n -> p a n", p=P)).then_inc(wo_landed, 16)
                    e.dma_start(ropeN[:, :, :, :], rope_nat.rearrange("k (t p) r -> p k t r", p=P)).then_inc(rope_landed, 16)
                    e.wait_ge(wq_full, 1)
                    e.dma_start(wq_d.rearrange("g p n -> p g n"), WQ[:, :, :, :, :].rearrange("p g a m r -> p g (a m r)").bitcast(F32)).then_inc(wq_stored, 16)
                    e.wait_ge(wq_stored, 16)

                @block.gpsimd
                def _(e):
                    e.memset(ones[:, :], 1.0).then_inc(ones_set, 1)
                    e.memset(kvw[:, :], 1.0).then_inc(ones_set, 1)
                    e.dma_start(ident[:, :], ident_c).then_inc(const_landed, 16)
                    e.dma_start(masks[:, :, :], masks_c.rearrange("k p n -> p k n")).then_inc(const_landed, 16)
                    e.dma_start(WU[:, :, :], wq_up.rearrange("(h p) r -> p h r", p=P)).then_inc(abs_landed, 16)
                    e.dma_start(WKV[:, :, :], wkv_up.rearrange("(h p) r -> p h r", p=P)).then_inc(abs_landed, 16)

                @block.scalar
                def _(e):
                    e.dma_start(WD[:, 0, :], wq_down).then_inc(wd_landed, 16)
                    e.dma_start(WD[0:KR, 1, :], wkv_down).then_inc(wd_landed, 16)
                    e.dma_start(WD[KR:P, 1, :], wk_rope).then_inc(wd_landed, 16)
                    e.dma_start(cc[:, 0, :], cvec.rearrange("a (k p) -> p (a k)", p=P)).then_inc(small_landed, 16)
                    e.dma_start(qnw[:, :], q_norm_w.rearrange("(p a) -> p a", a=1)).then_inc(small_landed, 16)
                    e.wait_ge(ones_set, 2)
                    for col, row in ((0, 0), (1, KR), (2, 0), (2, KR)):
                        e.dma_start(kvw[row:row + KR, col:col + 1], kv_norm_w.rearrange("(p a) -> p a", a=1)).then_inc(small_landed, 16)
                    e.wait_ge(small_landed, 16 * 6)
                    e.activation(cc[:, 1, :], cc[:, 0, :], ACT.Exp, scale=-1.0).then_inc(silu_exp, 1)
                    e.wait_ge(filled, J_WD + 1)
                    e.activation(WDT[:, :, :], ps[:, J_WD % 8, :].rearrange("p (a n) -> p a n", a=DH), ACT.Copy).then_inc(emptied["A"], 1)
                    e.wait_ge(var_rec, 1)
                    e.activation(rs[:, 1, 0:TT], rs[:, 0, 0:TT], ACT.Sqrt).then_inc(std_ready, 1)
                    e.wait_ge(mod_ready, 1)
                    for k in range(2 * NC):
                        tg, half = k // 2, k % 2
                        e.wait_ge(filled, J_ZT + k + 1)
                        e.activation(hT[:, half, C * tg:C * tg + C], ps[:, (J_ZT + k) % 8, :], ACT.Identity,
                                     bias=modc[:, half:half + 1], scale=scale1[:, half:half + 1]).then_inc(emptied["A"], 1)
                    for k in range(TT // 2):
                        e.wait_ge(filled, J_PROJ + k + 1)
                        e.activation(PJ[:, 2 * k:2 * k + 2, :], ps[:, (J_PROJ + k) % 8, :].rearrange("p (t n) -> p t n", t=2),
                                     ACT.Copy).then_inc(emptied["A"], 1)
                    e.wait_ge(rms_rec, 1)
                    e.activation(rs[:, 1, :], rs[:, 0, :], ACT.Sqrt).then_inc(rms_root, 1)
                    for k in range(3 * NC):
                        e.wait_ge(filled, J_QK + k + 1)
                        if k >= 4:
                            e.wait_ge(tf_free, k - 3)
                        kind = k % 3
                        if kind == 0:
                            e.activation(TF[:, k % 4, :], ps[:, (J_QK + k) % 8, :], ACT.Copy).then_inc(emptied["A"], 1)
                        else:
                            e.activation(TF[:, k % 4, :], ps[:, (J_QK + k) % 8, :], ACT.Identity,
                                         scale=kvw[:, kind - 1:kind]).then_inc(emptied["A"], 1)

                @block.vector
                def _(e):
                    steps = [0]

                    def settle(ins):
                        steps[0] += 1
                        ins.then_inc(dve_step, 1)
                        e.wait_ge(dve_step, steps[0])

                    v = nc.vector
                    for t in range(TT):
                        if t % 4 == 0:
                            e.wait_ge(x_landed[t // 4], 16)
                        last = v.bn_stats(st[:, t, :], X[:, t, :])
                    settle(last)
                    for t in range(TT):
                        last = v.bn_aggr(mv[:, t, :], st[:, t, :])
                    settle(last)
                    settle(v.tensor_scalar(rs[:, 2, 0:TT], mv[:, :, 1], LN_EPS, None, ALU.add))
                    v.reciprocal(rs[:, 0, 0:TT], rs[:, 2, 0:TT]).then_inc(var_rec, 1)
                    e.wait_ge(silu_exp, 1)
                    settle(v.tensor_scalar(cc[:, 2, :], cc[:, 1, :], 1.0, None, ALU.add))
                    settle(v.reciprocal(cc[:, 3, :], cc[:, 2, :]))
                    v.tensor_tensor(cc[:, 4, :], cc[:, 0, :], cc[:, 3, :], ALU.mult).then_inc(silu_ready, 1)
                    e.wait_ge(std_ready, 1)
                    newton = (rs[:, 0, 0:TT], rs[:, 1, 0:TT], rs[:, 2, 0:TT])
                    settle(v.tensor_tensor(newton[0], newton[1], newton[1], ALU.mult))
                    settle(v.tensor_tensor(newton[0], newton[0], newton[2], ALU.mult))
                    settle(v.tensor_scalar(newton[0], newton[0], -0.5, 1.5, ALU.mult, ALU.add))
                    settle(v.tensor_tensor(newton[1], newton[1], newton[0], ALU.mult))
                    for t in range(TT):
                        v.tensor_scalar(Z[:, t, :], X[:, t, :], mv[:, t, 0:1], rs[:, 1, t:t + 1],
                                        ALU.subtract, ALU.mult).then_inc(z_ready, 1)
                    e.wait_ge(const_landed, 32)
                    v.tensor_copy(identb[:, :], ident[:, :])
                    v.tensor_copy(maskb[:, :, :], masks[:, :, :])
                    e.wait_ge(filled, J_MOD + 1)
                    v.tensor_copy(modc[:, :], ps[:, J_MOD % 8, 0:12]).then_inc(emptied["V"], 1)
                    e.wait_ge(emptied["V"], emptied_count(J_MOD))
                    for n, k in enumerate((1, 4)):
                        last = v.tensor_scalar(scale1[:, 2 * n:2 * n + 2], modc[:, 2 * k:2 * k + 2], 1.0, None, ALU.add)
                    last.then_inc(mod_ready, 1)
                    for n, k in enumerate((2, 5)):
                        g = modc[:, 2 * k:2 * k + 2]
                        v.tensor_scalar(small[:, 2 * n:2 * n + 2], g, 0.0, 2.0, ALU.is_ge, ALU.mult)
                        last = v.tensor_scalar(small[:, 4 + 2 * n:6 + 2 * n], g, -1.0, None, ALU.mult)
                    settle(last)
                    for n, k in enumerate((2, 5)):
                        g = modc[:, 2 * k:2 * k + 2]
                        v.tensor_scalar(small[:, 8 + 2 * n:10 + 2 * n], small[:, 2 * n:2 * n + 2], -1.0, None, ALU.add)
                        last = v.tensor_tensor(small[:, 12 + 2 * n:14 + 2 * n], g, small[:, 4 + 2 * n:6 + 2 * n], ALU.max)
                    settle(last)
                    settle(v.tensor_scalar(small[:, 16:20], small[:, 12:16], 0.25, None, ALU.max))
                    settle(v.tensor_tensor(gates[:, :], small[:, 16:20], small[:, 8:12], ALU.mult))
                    e.wait_ge(small_landed, 16 * 6)
                    for k in range(2):
                        e.wait_ge(filled, J_ABS + k + 1)
                        v.tensor_scalar(WQf[:, 4 * k:4 * k + 4, 0, :], ps[:, (J_ABS + k) % 8, :].rearrange("p (g r) -> p g r", g=4),
                                        qnw[:, 0:1], None, ALU.mult).then_inc(emptied["V"], 1)
                    for k in range(2):
                        e.wait_ge(filled, J_ROPE + k + 1)
                        src = ps[:, (J_ROPE + k) % 8, :].rearrange("p (g a t o) -> p g a t o", g=4, a=2, o=2)
                        dst = WQf[:, 4 * k:4 * k + 4, :, :].rearrange("p g m (a t o) -> p g m a t o", a=2, o=2)
                        for a in range(2):
                            for o in range(2):
                                v.tensor_scalar(dst[:, :, 1, a, :, o], src[:, :, 1 - a, :, o], qnw[:, 0:1], None, ALU.mult)
                                last = v.tensor_scalar(dst[:, :, 2, a, :, o], src[:, :, 1 - a, :, 1 - o], qnw[:, 0:1], None, ALU.mult)
                        last.then_inc(emptied["V"], 1)
                    e.wait_ge(emptied["V"], emptied_count(J_ROPE + 1))
                    settle(v.tensor_copy(WQ[:, :, 0, :, :], WQf))
                    v.tensor_tensor(WQ[:, :, 1, :, :], WQf, WQ[:, :, 0, :, :].bitcast(F32), ALU.subtract).then_inc(wq_full, 1)
                    e.wait_ge(wo_landed, 16)
                    for a in range(DH):
                        v.tensor_scalar(WO[:, a, :], WO[:, a, :], gates[:, a:a + 1], None, ALU.mult).then_inc(wo_scaled, 1)
                    wait_emptied(e, J_PROJ + TT // 2 - 1)
                    settle(v.tensor_tensor(SQ, PJ[:, :, 0:192], PJ[:, :, 0:192], ALU.mult))
                    v.reduce_sum(rs[:, 0, 0:TT], SQ[:, :, 0:QR], AX.X)
                    settle(v.reduce_sum(rs[:, 0, TT:2 * TT], SQ[:, :, QR:192], AX.X))
                    v.tensor_scalar(rs[:, 2, 0:TT], rs[:, 0, 0:TT], 1.0 / QR, RMS_EPS, ALU.mult, ALU.add)
                    settle(v.tensor_scalar(rs[:, 2, TT:2 * TT], rs[:, 0, TT:2 * TT], 1.0 / KR, RMS_EPS, ALU.mult, ALU.add))
                    v.reciprocal(rs[:, 0, :], rs[:, 2, :]).then_inc(rms_rec, 1)
                    e.wait_ge(rope_landed, 16)
                    kr = PJ[:, :, 192:256].rearrange("p t (r o) -> p t r o", o=2)
                    kn = KN[:, :, :].rearrange("p t (m r o) -> p t m r o", m=3, o=2)
                    cosn, sinn = ropeN[:, 0, :, :], ropeN[:, 1, :, :]
                    tmp = [hT[:, 1, 1024 + 512 * 0:1024 + 512].rearrange("p (t r) -> p t r", t=TT),
                           hT[:, 1, 1536:2048].rearrange("p (t r) -> p t r", t=TT)]
                    e.wait_ge(wq_full, 1)
                    for o, (f0, f1, op) in enumerate(((cosn, sinn, ALU.subtract), (sinn, cosn, ALU.add))):
                        v.tensor_tensor(tmp[0], kr[:, :, :, 0], f0, ALU.mult)
                        settle(v.tensor_tensor(tmp[1], kr[:, :, :, 1], f1, ALU.mult))
                        for m in (0, 2):
                            last = v.tensor_tensor(kn[:, :, m, :, o], tmp[0], tmp[1], op)
                        settle(last)
                    e.wait_ge(rms_root, 1)
                    settle(v.tensor_tensor(rs[:, 0, :], rs[:, 1, :], rs[:, 1, :], ALU.mult))
                    settle(v.tensor_tensor(rs[:, 0, :], rs[:, 0, :], rs[:, 2, :], ALU.mult))
                    settle(v.tensor_scalar(rs[:, 0, :], rs[:, 0, :], -0.5, 1.5, ALU.mult, ALU.add))
                    settle(v.tensor_tensor(rs[:, 1, :], rs[:, 1, :], rs[:, 0, :], ALU.mult))
                    for t in range(TT):
                        v.tensor_scalar(PJ[:, t, 0:QR], PJ[:, t, 0:QR], rs[:, 1, t:t + 1], None, ALU.mult)
                        v.tensor_scalar(KN[:, t, 64:128], PJ[:, t, QR:192], rs[:, 1, TT + t:TT + t + 1], None,
                                        ALU.mult).then_inc(nat_ready, 1)
                    for k in range(3 * NC):
                        wait_emptied(e, J_QK + k)
                        tg, kind = k // 3, k % 3
                        hi, lo = QT if kind == 0 else K[kind - 1]
                        cols = slice(C * tg, C * tg + C)
                        settle(v.tensor_copy(hi[:, cols], TF[:, k % 4, :]))
                        v.tensor_tensor(lo[:, cols], TF[:, k % 4, :], hi[:, cols].bitcast(F32), ALU.subtract).then_inc(tf_free, 1)
                    for k in range(H // 2):
                        e.wait_ge(filled, J_WOT + k + 1)
                        v.tensor_copy(woT[:, 2 * k:2 * k + 2, :], ps[:, (J_WOT + k) % 8, :].rearrange("p (h d) -> p h d", h=2)).then_inc(emptied["V"], 1)
                    for k in range(PAIRS // 2):
                        e.wait_ge(filled, J_WVO + k + 1)
                        v.tensor_scalar(WVO[:, 2 * k:2 * k + 2, :], ps[:, (J_WVO + k) % 8, :].rearrange("p (g d) -> p g d", g=2),
                                        kvw[:, 2:3], None, ALU.mult).then_inc(emptied["V"], 1)

                @block.tensor
                def _(e):
                    t_ = nc.tensor

                    def bank(job):
                        if job >= 8:
                            wait_emptied(e, job - 8)
                        return ps[:, job % 8, :]

                    e.wait_ge(const_landed, 32)
                    e.wait_ge(wd_landed, 48)
                    b = bank(J_WD)
                    for half in range(DH):
                        for w in range(2):
                            last = t_.transpose(b[:, (2 * half + w) * P:(2 * half + w + 1) * P], WD[:, w, half * P:(half + 1) * P], ident[:, :])
                    last.then_inc(filled, 1)
                    e.wait_ge(silu_ready, 1)
                    e.wait_ge(wmod_landed, 16)
                    b = bank(J_MOD)
                    for n in range(12):
                        for a in range(DH):
                            last = t_.matmul(b[:, n:n + 1], WMOD[:, a, n * P:(n + 1) * P], cc[:, 4, a:a + 1], start=(a == 0), stop=(a == DH - 1))
                    last.then_inc(filled, 1)
                    e.wait_ge(abs_landed, 32)
                    e.wait_ge(wr_landed, 16)
                    for k in range(2):
                        b = bank(J_ABS + k)
                        for n in range(8):
                            h = 8 * k + n
                            last = t_.matmul(b[:, 64 * n:64 * n + 64], WU[:, h, :], WKV[:, 2 * h, :], start=True, stop=True)
                        last.then_inc(filled, 1)
                    for k in range(2):
                        b = bank(J_ROPE + k)
                        for n in range(4):
                            last = t_.transpose(b[:, P * n:P * n + P], WR[:, 4 * k + n, :], ident[:, :])
                        last.then_inc(filled, 1)
                    for k in range(2 * NC):
                        tg, half = k // 2, k % 2
                        b = bank(J_ZT + k)
                        for n in range(CB):
                            e.wait_ge(z_ready, CB * tg + n + 1)
                            last = t_.transpose(b[:, P * n:P * n + P], Z[:, CB * tg + n, half * P:half * P + P], ident[:, :])
                        last.then_inc(filled, 1)
                    wait_emptied(e, J_ZT + 2 * NC - 1)
                    for k in range(TT // 2):
                        b = bank(J_PROJ + k)
                        for n in range(2):
                            t = 2 * k + n
                            for a in range(DH):
                                last = t_.matmul(b[:, D * n:D * n + D], hT[:, a, P * t:P * t + P], WDT[:, a, :], start=(a == 0), stop=(a == DH - 1))
                        last.then_inc(filled, 1)
                    for k in range(3 * NC):
                        tg, kind = k // 3, k % 3
                        b = bank(J_QK + k)
                        for n in range(CB):
                            t = CB * tg + n
                            e.wait_ge(nat_ready, t + 1)
                            src = (PJ[:, t, 0:QR], KN[:, t, 64:192], KN[:, t, 0:128])[kind]
                            last = t_.transpose(b[:, P * n:P * n + P], src, ident[:, :])
                        last.then_inc(filled, 1)
                    e.wait_ge(wo_scaled, DH)
                    for k in range(H // 2):
                        b = bank(J_WOT + k)
                        for n in range(2):
                            for a in range(DH):
                                last = t_.transpose(b[:, D * n + P * a:D * n + P * a + P], WO[:, a, (2 * k + n) * VD:(2 * k + n + 1) * VD], ident[:, :])
                        last.then_inc(filled, 1)
                    wait_emptied(e, J_WOT + H // 2 - 1)
                    for k in range(PAIRS // 2):
                        b = bank(J_WVO + k)
                        for n in range(2):
                            for o in range(2):
                                h = 2 * (2 * k + n) + o
                                last = t_.matmul(b[64 * o:64 * o + 64, D * n:D * n + D], WKV[:, 2 * h + 1, :], woT[:, h, :], start=True, stop=True)
                        last.then_inc(filled, 1)

        with ExitStack() as work:
            WS = sb(work, "WS", [P, 2, 3, P], F32R)
            ropeT = sb(work, "ropeT", [P, 2, S])
            Qf = sb(work, "Qf", [P, 2, C])
            QH = sb(work, "QH", [P, NC, 2, C], F32R)
            QL = sb(work, "QL", [P, NC, 2, C], F32R)
            rp = sb(work, "rp", [P, 2, C])
            mp = sb(work, "mp", [P, 2, 2 * CB, NC])
            mrow = sb(work, "mrow", [P, 2 * CB])
            mhl = sb(work, "mhl", [P, 2, 2 * CB], BF16)
            MB = sb(work, "MB", [P, 3, 2, C])
            PT = sb(work, "PT", [P, 4, 2, C])
            acc = sb(work, "acc", [P, 2, 2, C])
            Osb = sb(work, "Osb", [P, 2, C])
            Lsb = sb(work, "Lsb", [64, 2, C])

            weights_staged, tables_landed = sem("weights_staged"), sem("tables_landed")
            q_abs, q_rope, q_swap = sem("q_abs_projected"), sem("q_rope_projected"), sem("q_swap_projected")
            q_abs_copied, rope_mul, q_full = sem("q_abs_copied"), sem("rope_mul"), sem("q_full")
            q_high, q_low = sem("q_high"), sem("q_low")
            piece_ready, piece_reduced, row_max, max_split = sem("piece_ready"), sem("piece_reduced"), sem("row_max"), sem("max_split")
            max_spread, shift_ready = sem("max_spread"), sem("shift_ready")
            scores_ready, shifted, probs_ready, probs_summed, probs_used = (
                sem("scores_ready"), sem("shifted"), sem("probs_ready"), sem("probs_summed"), sem("probs_used"))
            out_copied, sums_ready, sums_copied, results_stored = sem("out_copied"), sem("sums_ready"), sem("sums_copied"), [sem(f"results_stored_{c}") for c in range(NC)]

            N0, O_BANK, MISC = 4, 6, 7
            MB_SLOT = [1, 2, 1, 0]

            MISC_AT = {
                2: [("max", 2, 0, 0)], 3: [("max", 2, 1, 0)], 4: [("sum", 0)],
                10: [("abs", 0)], 11: [("rope", 0)], 12: [("swap", 0)], 13: [("sum", 1)],
                14: [("abs", 1)], 15: [("rope", 1)], 16: [("swap", 1)],
                18: [("max", 3, 0, 0)], 19: [("max", 3, 1, 0)],
                22: [("max", 0, 0, 1)], 23: [("max", 0, 1, 1)], 24: [("sum", 2)],
                25: [("abs", 2)], 26: [("rope", 2)], 27: [("swap", 2)],
                30: [("max", 1, 0, 1)], 31: [("max", 1, 1, 1)],
                37: [("abs", 3)], 38: [("rope", 3)], 39: [("swap", 3), ("sum", 3)],
            }

            def step_of(u):
                d, u = divmod(u, STEPS)
                c = max(k for k in range(NC) if U0[k] <= u)
                return d, c, u - U0[c]

            def piece(w, k):
                d, c, j = step_of(w)
                i = 2 * j + k
                hd, r = divmod(i, CB * (c + 1))
                b, pc = divmod(r, c + 1)
                return d, c, i, hd, b, pc, C * pc, min(C, P * (CB * c + b + 1) - C * pc)

            def first_col(c, j):
                return P * max(0, j - CB * c)

            def wait(e, s, value):
                if not isinstance(value, int) or value > 0:
                    e.wait_ge(s, value)

            def job(p, c):
                return NC * p + c

            order = [ev for u in sorted(MISC_AT) for ev in MISC_AT[u]]

            order_last = [ev for ev in order if ev[0] == "sum" or (ev[0] == "max" and not ev[3])]

            def wait_misc(e, p, ev, last_pair):
                evs = order_last if last_pair else order
                k = evs.index(ev)
                prev, q = (evs[k - 1], p) if k else (order[-1], p - 1)
                if k == 0 and isinstance(p, int) and p == 0:
                    e.wait_ge(shift_ready, 4)
                    return
                if prev[0] == "max":
                    wait(e, shift_ready, 2 * job(q + prev[3], prev[1]) + prev[2] + 1)
                elif prev[0] == "sum":
                    wait(e, sums_copied, job(q, prev[1]) + 1)
                elif prev[0] == "abs":
                    wait(e, q_abs_copied, 2 * job(q + 1, prev[1]) + 2)
                else:
                    wait(e, rope_mul, 2 * job(q + 1, prev[1]) + (1 if prev[0] == "rope" else 2))

            def run_pairs(e, prologue, body):
                prologue()
                body(0, False)
                with e.Fori(1, PAIRS - 1) as p:
                    body(p, False)
                body(PAIRS - 1, True)

            with nc.Block() as block:
                @block.sync
                def _(e):
                    def stage(p):
                        src = wq_d[p, :, :] if isinstance(p, int) else wq_d[bass.ds(p, 1), :, :].rearrange("g p n -> p (g n)")
                        e.dma_start(WS[:, :, :, :].rearrange("p a m r -> p (a m r)").bitcast(F32), src).then_inc(weights_staged, 16)

                    def store(p, c):
                        e.wait_ge(out_copied, job(p, c) + 1)
                        cols = slice(C * c, C * c + C)
                        if isinstance(p, int):
                            o_dst, l_dst = o_d[p, :, cols], l_d[2 * p:2 * p + 2, cols]
                        else:
                            o_dst = o_d[bass.ds(p, 1), :, cols].rearrange("g p n -> p (g n)")
                            l_dst = l_d[bass.ds(2 * p, 2), cols]
                        e.dma_start(o_dst, Osb[:, c % 2, :]).then_inc(results_stored[c], 16)
                        e.wait_ge(sums_copied, job(p, c) + 1)
                        e.dma_start(l_dst, Lsb[0:64:32, c % 2, :]).then_inc(results_stored[c], 16)

                    def body(p, last):
                        if not last:
                            e.wait_ge(q_swap, job(p, NC - 1) + 1)
                            stage(p + 1)
                        for c in range(NC):
                            store(p, c)

                    def prologue():
                        stage(0)
                        e.dma_start(ropeT[:, :, :], rope_q.rearrange("k p n -> p k n")).then_inc(tables_landed, 16)

                    run_pairs(e, prologue, body)
                    for c in range(NC):
                        e.wait_ge(results_stored[c], 32 * PAIRS)

                @block.tensor
                def _(e):
                    t_ = nc.tensor

                    def project(c, m, done):
                        for k, (w, q) in enumerate(((0, 0), (0, 1), (1, 0))):
                            last = t_.matmul(ps[:, MISC, :], WS[:, w, m, :], QT[q][:, C * c:C * c + C], start=(k == 0), stop=(k == 2))
                        last.then_inc(done, 1)

                    def spread_maxima(c, hd, g):
                        e.wait_ge(max_split, 2 * (g + 1))
                        for b in range(CB):
                            for part in range(2):
                                col = mhl[:, part, hd * CB + b:hd * CB + b + 1]
                                last = t_.matmul(ps[:, MISC, P * b:P * b + P], col.to_broadcast([P, P]), identb[:, :],
                                                 start=(part == 0), stop=(part == 1))
                        last.then_inc(max_spread, 1)

                    def sum_columns(p, c):
                        e.wait_ge(probs_summed, STEPS * p + U0[c + 1])
                        for hd in range(2):
                            last = t_.matmul(ps[32 * hd:32 * hd + 32, MISC, :], ones[:, 0:32], acc[:, c % 2, hd, :], start=True, stop=True)
                        last.then_inc(sums_ready, 1)

                    def misc(p, ev, last_pair):
                        kind, c = ev[0], ev[1]
                        if last_pair and ev not in order_last:
                            return
                        wait_misc(e, p, ev, last_pair)
                        if kind == "max":
                            spread_maxima(c, ev[2], job(p + ev[3], c))
                        elif kind == "sum":
                            sum_columns(p, c)
                        else:
                            if kind == "abs":
                                e.wait_ge(weights_staged, 16 * (p + 2))
                            project(c, ("abs", "rope", "swap").index(kind), {"abs": q_abs, "rope": q_rope, "swap": q_swap}[kind])

                    def max_pieces(p, w, last_pair):
                        for k in range(2):
                            d, c, i, hd, b, pc, key, width = piece(w, k)
                            if d and last_pair:
                                return
                            if i == 0:
                                e.wait_ge(q_high, job(p + d, c) + 1)
                            wait(e, piece_reduced, PIECES * p + 2 * w + k - 1)
                            diag = pc == c
                            last = t_.matmul(ps[:, N0 + k, 0:max(width, 2 * P)], QH[:, c, hd, P * b:P * b + P],
                                             K[hd][0][:, key:key + max(width, 2 * P)], start=True, stop=not diag)
                            if diag:
                                last = t_.matmul(ps[:, N0 + k, width - P:width], identb[:, :], maskb[:, 0, :], start=False, stop=True)
                            last.then_inc(piece_ready, 1)

                    def scores(p, u, last_pair):
                        d, c, j = step_of(u)
                        if d and last_pair:
                            return
                        if j == 0:
                            e.wait_ge(q_low, job(p + d, c) + 1)
                        wait(e, shifted, STEPS * p + u - 1)
                        x0 = first_col(c, j)
                        xm = min(x0, C - 2 * P)
                        masked = j >= CB * c
                        for hd in range(2):
                            b = 2 * (u % 2) + hd
                            for k, (w, q) in enumerate(((0, QH), (0, QL), (1, QH))):
                                last = t_.matmul(ps[:, b, xm:C], K[hd][w][:, P * j:P * j + P], q[:, c, hd, xm:C], start=(k == 0),
                                                 stop=(k == 2 and not masked))
                            if masked:
                                last = t_.matmul(ps[:, b, x0:x0 + P], identb[:, :], maskb[:, 1, :], start=False, stop=True)
                        last.then_inc(scores_ready, 1)

                    def weigh_values(p, u):
                        _, c, j = step_of(u)
                        e.wait_ge(probs_ready, STEPS * p + u + 1)
                        if j == 0:
                            wait(e, out_copied, job(p, c))
                        x0 = first_col(c, j)
                        for hd in range(2):
                            last = t_.matmul(ps[64 * hd:64 * hd + 64, O_BANK, x0:C], KN[:, j, 64:128], PT[:, u % 4, hd, x0:C],
                                             start=(j == 0), stop=(j == UNITS[c] - 1))
                        last.then_inc(probs_used, 1)

                    def body(p, last_pair):
                        for u in range(STEPS):
                            scores(p, u + 2, last_pair)
                            late = [ev for ev in MISC_AT.get(u, []) if ev == ("sum", 3)]
                            for ev in MISC_AT.get(u, []):
                                if ev not in late:
                                    misc(p, ev, last_pair)
                            max_pieces(p, u + LEAD, last_pair)
                            weigh_values(p, u)
                            for ev in late:
                                misc(p, ev, last_pair)

                    def prologue():
                        e.wait_ge(weights_staged, 16)
                        for c in range(NC):
                            wait(e, rope_mul, 2 * c)
                            project(c, 0, q_abs)
                            e.wait_ge(q_abs_copied, 2 * c + 2)
                            project(c, 1, q_rope)
                            e.wait_ge(rope_mul, 2 * c + 1)
                            project(c, 2, q_swap)
                        e.wait_ge(rope_mul, 2 * NC)
                        for w in range(LEAD):
                            max_pieces(0, w, False)
                            for c in range(2):
                                if w == U0[c + 1] + 1:
                                    for hd in range(2):
                                        wait(e, shift_ready, 2 * c + hd)
                                        spread_maxima(c, hd, c)
                        scores(0, 0, False)
                        scores(0, 1, False)

                    run_pairs(e, prologue, body)

                @block.vector
                def _(e):
                    v = nc.vector

                    def rope_cos(c, g):
                        e.wait_ge(q_rope, g + 1)
                        wait(e, q_full, 2 * g)
                        v.tensor_tensor(rp[:, 0, :], ps[:, MISC, :], ropeT[:, 0, C * c:C * c + C], ALU.mult).then_inc(rope_mul, 1)

                    def rope_sin(c, g):
                        e.wait_ge(q_swap, g + 1)
                        v.tensor_tensor(rp[:, 1, :], ps[:, MISC, :], ropeT[:, 1, C * c:C * c + C], ALU.mult).then_inc(rope_mul, 1)
                        e.wait_ge(rope_mul, 2 * (g + 1))
                        wait(e, q_low, g)
                        v.tensor_tensor(Qf[64:128, 0, :], rp[64:128, 0, :], rp[64:128, 1, :], ALU.add).then_inc(q_full, 1)
                        v.tensor_tensor(Qf[0:64, 1, :], rp[0:64, 0, :], rp[0:64, 1, :], ALU.add).then_inc(q_full, 1)

                    def reduce_pieces(p, w, last_pair):
                        for k in range(2):
                            d, c, i, hd, b, pc, key, width = piece(w, k)
                            if d and last_pair:
                                return
                            e.wait_ge(piece_ready, PIECES * p + 2 * w + k + 1)
                            v.reduce_max(mp[:, c % 2, hd * CB + b, pc:pc + 1], ps[:, N0 + k, 0:width], AX.X).then_inc(piece_reduced, 1)
                        if i == 2 * UNITS[c] - 1:
                            split_maxima(PIECES * p + 2 * w + 2, c, job(p + d, c))

                    def split_maxima(pieces_done, c, g):
                        e.wait_ge(piece_reduced, pieces_done)
                        v.reduce_max(mrow[:, :], mp[:, c % 2, :, 0:c + 1], AX.X).then_inc(row_max, 1)
                        e.wait_ge(row_max, g + 1)
                        wait(e, max_spread, 2 * g)
                        v.tensor_copy(mhl[:, 0, :], mrow[:, :]).then_inc(max_split, 1)
                        e.wait_ge(max_split, 2 * g + 1)
                        v.tensor_tensor(mhl[:, 1, :], mrow[:, :], mhl[:, 0, :], ALU.subtract).then_inc(max_split, 1)

                    def shift(p, u, last_pair):
                        d, c, j = step_of(u)
                        if d and last_pair:
                            return
                        if j == 0:
                            e.wait_ge(shift_ready, 2 * job(p + d, c) + 2)
                        e.wait_ge(scores_ready, STEPS * p + u + 1)
                        wait(e, probs_used, STEPS * p + u - 3)
                        wait(e, probs_summed, STEPS * p + u - 3)
                        x0 = first_col(c, j)
                        b = 2 * (u % 2)
                        v.tensor_tensor(PT[:, u % 4, :, x0:C], ps[:, b:b + 2, x0:C], MB[:, MB_SLOT[c], :, x0:C], ALU.subtract).then_inc(shifted, 1)

                    def body(p, last_pair):
                        for u in range(STEPS):
                            shift(p, u + 2, last_pair)
                            for ev in MISC_AT.get(u, []):
                                if ev[0] == "rope" and not last_pair:
                                    rope_cos(ev[1], job(p + 1, ev[1]))
                                if ev[0] == "swap" and not last_pair:
                                    rope_sin(ev[1], job(p + 1, ev[1]))
                            reduce_pieces(p, u + LEAD, last_pair)

                    def prologue():
                        e.wait_ge(tables_landed, 16)
                        for c in range(NC):
                            rope_cos(c, c)
                            rope_sin(c, c)
                        for w in range(LEAD):
                            reduce_pieces(0, w, False)
                        shift(0, 0, False)
                        shift(0, 1, False)

                    run_pairs(e, prologue, body)

                @block.scalar
                def _(e):
                    def copy_abs(g):
                        e.wait_ge(q_abs, g + 1)
                        wait(e, q_low, g)
                        e.activation(Qf[0:64, 0, :], ps[0:64, MISC, :], ACT.Copy).then_inc(q_abs_copied, 1)
                        e.activation(Qf[64:128, 1, :], ps[64:128, MISC, :], ACT.Copy).then_inc(q_abs_copied, 1)

                    def high_part(c, g):
                        e.wait_ge(q_abs_copied, 2 * (g + 1))
                        e.wait_ge(q_full, 2 * (g + 1))
                        e.activation(QH[:, c, :, :], Qf[:, :, :], ACT.Copy).then_inc(q_high, 1)

                    def copy_shift(c, hd, g):
                        e.wait_ge(max_spread, 2 * g + hd + 1)
                        e.activation(MB[:, MB_SLOT[c], hd, :], ps[:, MISC, :], ACT.Copy).then_inc(shift_ready, 1)

                    def wait_stored(p, c):
                        wait(e, results_stored[(c + 2) % NC], 32 * (p + c // 2))

                    def copy_sums(p, c):
                        g = job(p, c)
                        e.wait_ge(sums_ready, g + 1)
                        wait_stored(p, c)
                        e.activation(Lsb[:, c % 2, :], ps[0:64, MISC, :], ACT.Copy).then_inc(sums_copied, 1)

                    def copy_output(p, c):
                        g = job(p, c)
                        e.wait_ge(probs_used, STEPS * p + U0[c + 1])
                        wait_stored(p, c)
                        e.activation(Osb[:, c % 2, :], ps[:, O_BANK, :], ACT.Copy).then_inc(out_copied, 1)

                    def exponentials(p, u, last_pair):
                        d, c, j = step_of(u)
                        if d and last_pair:
                            return
                        e.wait_ge(shifted, STEPS * p + u + 1)
                        x0 = first_col(c, j)
                        e.activation(PT[:, u % 4, :, x0:C], PT[:, u % 4, :, x0:C], ACT.Exp, scale=SCALE).then_inc(probs_ready, 1)

                    def body(p, last_pair):
                        for u in range(STEPS):
                            exponentials(p, u + 2, last_pair)
                            for ev in MISC_AT.get(u, []):
                                if ev[0] == "abs" and not last_pair:
                                    copy_abs(job(p + 1, ev[1]))
                                if ev[0] == "swap" and not last_pair:
                                    high_part(ev[1], job(p + 1, ev[1]))
                                if ev[0] == "max" and not (last_pair and ev[3]):
                                    copy_shift(ev[1], ev[2], job(p + ev[3], ev[1]))
                                if ev[0] == "sum" and ev[1] < NC - 1:
                                    copy_sums(p, ev[1])
                            if u + 1 in U0:
                                c = U0.index(u + 1) - 1
                                copy_output(p, c)
                                if c == NC - 1:
                                    copy_sums(p, c)

                    def prologue():
                        for c in range(NC):
                            copy_abs(c)
                            high_part(c, c)
                        for c in range(2):
                            for hd in range(2):
                                copy_shift(c, hd, c)
                        exponentials(0, 0, False)
                        exponentials(0, 1, False)

                    run_pairs(e, prologue, body)

                @block.gpsimd
                def _(e):
                    def low_part(c, g):
                        e.wait_ge(q_high, g + 1)
                        e.tensor_tensor(QL[:, c, :, :], Qf[:, :, :], QH[:, c, :, :].bitcast(F32), ALU.subtract).then_inc(q_low, 1)

                    def sum_probs(p, u, last_pair):
                        d, c, j = step_of(u)
                        if d and last_pair:
                            return
                        e.wait_ge(probs_ready, STEPS * p + u + 1)
                        wait(e, probs_summed, STEPS * p + u)
                        x0 = first_col(c, j)
                        a, pt = acc[:, c % 2, :, x0:C], PT[:, u % 4, :, x0:C]
                        if j == 0:
                            wait(e, sums_ready, job(p + d, c) - 1)
                            e.tensor_tensor(a, pt, ones[:, 0:1].unsqueeze(2).to_broadcast([P, 2, C]), ALU.mult).then_inc(probs_summed, 1)
                        else:
                            e.tensor_tensor(a, a, pt, ALU.add).then_inc(probs_summed, 1)

                    def body(p, last_pair):
                        for u in range(STEPS):
                            sum_probs(p, u + 2, last_pair)
                            for ev in MISC_AT.get(u, []):
                                if ev[0] == "swap" and not last_pair:
                                    low_part(ev[1], job(p + 1, ev[1]))

                    def prologue():
                        for c in range(NC):
                            low_part(c, c)
                        sum_probs(0, 0, False)
                        sum_probs(0, 1, False)

                    run_pairs(e, prologue, body)
        attn_kept.close()

        project_and_feed(nc, base, sb, sem, ps, X, ident, modc, scale1, gates, st, mv, rs, WVO, o_d, l_d, r_d,
                         wq_gate, s_gate, wq_up_ffn, s_up, wq_down_ffn, s_down, out)


def project_and_feed(nc, base, sb, sem, ps, X, ident, modc, scale1, gates, st, mv, rs, WVO, o_d, l_d, r_d,
                     wq_gate, s_gate, wq_up_ffn, s_up, wq_down_ffn, s_down, out):
    ZERO_POINT = 128.0
    with ExitStack() as work:
        WI = [sb(work, f"wi_{n}", [P, HB, D], I32) for n in ("gate", "up")]
        WID = sb(work, "wi_down", [P, DH, HID], I32)
        WF = sb(work, "wf", [P, 2, HB, D])
        WFD = sb(work, "wfd", [P, DH, HB * P])
        WT = [sb(work, f"wt_{n}", [P, 2, DH, HB * P], F32R) for n in ("hi", "lo")]
        WTf = sb(work, "wtf", [P, 2, DH, HB * P])
        WDN = sb(work, "wdn", [P, HB, D])
        sc = sb(work, "sc", [P, 2, HB])
        sd = sb(work, "sd", [P, 2, DH])
        Z = sb(work, "Z2", [P, 2, CB, D])
        hF = sb(work, "hF", [P, DH, C])
        hH = sb(work, "hH", [P, DH, C], F32R)
        hL = sb(work, "hL", [P, DH, C], F32R)
        SG = sb(work, "SG", [P, 2, C])
        AT = sb(work, "AT", [P, HB, C])
        sums = sb(work, "sums", [P, 2, H * S // P])
        OT = sb(work, "OT", [P, 1, PAIRS, C])
        RB = sb(work, "RB", [P, 1, PAIRS, C])

        scales_landed, wi_landed, scales_cleared = sem("scales_landed"), sem("wi_landed"), sem("scales_cleared")
        f_step, f_filled, f_emptied = sem("ffn_vector_step"), sem("ffn_bank_filled"), sem("ffn_bank_emptied")
        f_rec, f_root, f_z, dequant = sem("ffn_var_rec"), sem("ffn_root"), sem("ffn_z_ready"), sem("dequantised")
        w_ready, h_filled, h_full, h_high, h_low = sem("ffn_weights_ready"), sem("h_filled"), sem("h_full"), sem("h_high"), sem("h_low")
        gu_ready, silu_done, act_ready, down_ready, out_ready, stored = (
            sem("gate_up_ready"), sem("silu_done"), sem("act_ready"), sem("down_ready"), sem("out_ready"), sem("stored"))
        sums_landed, sums_inverted, inverses_stored = sem("sums_landed"), sem("sums_inverted"), sem("inverses_stored")
        outputs_landed, inverses_landed, normalised = sem("outputs_landed"), sem("inverses_landed"), sem("outputs_normalised")
        projected, residual_added = sem("projected"), sem("residual_added")
        ov = out.rearrange("a (t p) d -> p (a t) d", p=P)
        HLAST = HID - (HB - 1) * P

        with nc.Block() as block:
            @block.sync
            def _(e):
                e.dma_start(sums[:, 0, :], l_d.rearrange("h (a n) -> (h a) n", n=H * S // P)).then_inc(sums_landed, 16)
                e.dma_start(OT[:, 0, :, :], o_d[:, :, 0:C].rearrange("g p n -> p g n")).then_inc(outputs_landed, 16)
                e.wait_ge(sums_inverted, 1)
                e.dma_start(r_d.rearrange("h (a n) -> (h a) n", n=H * S // P), sums[:, 1, :]).then_inc(inverses_stored, 16)
                e.wait_ge(inverses_stored, 16)

                def load(c):
                    cols = slice(C * c, C * c + C)
                    if c:
                        e.wait_ge(projected, 2 * c)
                        e.wait_ge(outputs_landed, 16 * c)
                        e.wait_ge(inverses_landed, 32 * c)
                        e.dma_start(OT[:, 0, :, :], o_d[:, :, cols].rearrange("g p n -> p g n")).then_inc(outputs_landed, 16)
                    for o in range(2):
                        src = r_d.rearrange("(g o) s -> o g s", o=2)[o, :, cols].partition_broadcast(64)
                        e.dma_start(RB[64 * o:64 * o + 64, 0, :, :], src).then_inc(inverses_landed, 16)

                load(0)
                e.wait_ge(scales_cleared, 2)
                for n, (w, s) in enumerate(((wq_gate, s_gate), (wq_up_ffn, s_up))):
                    e.dma_start(WI[n][:, 0:HB - 1, :], w[0:(HB - 1) * P, :].rearrange("(b p) d -> p b d", p=P)).then_inc(wi_landed, 16)
                    e.dma_start(WI[n][0:HLAST, HB - 1, :], w[(HB - 1) * P:HID, :]).then_inc(wi_landed, 16)
                    e.dma_start(sc[:, n, 0:HB - 1], s[0:(HB - 1) * P].rearrange("(b p) -> p b", p=P)).then_inc(scales_landed, 16)
                    e.dma_start(sc[0:HLAST, n, HB - 1:HB], s[(HB - 1) * P:HID].rearrange("(p b) -> p b", b=1)).then_inc(scales_landed, 16)
                e.dma_start(WID[:, :, :], wq_down_ffn.rearrange("(a p) n -> p a n", p=P)).then_inc(wi_landed, 16)
                e.dma_start(sd[:, 0, :], s_down.rearrange("(a p) -> p a", p=P)).then_inc(scales_landed, 16)
                load(1)
                for c in range(NC):
                    if c + 2 < NC:
                        load(c + 2)
                    e.wait_ge(out_ready, 2 * (c + 1))
                    e.dma_start(ov[:, CB * c:CB * c + CB, :], X[:, CB * c:CB * c + CB, :]).then_inc(stored, 16)
                e.wait_ge(stored, 16 * NC)

            @block.gpsimd
            def _(e):
                e.memset(sc[:, :, :], 0.0).then_inc(scales_cleared, 1)
                e.memset(WI[0][:, HB - 1, :], 0)
                e.memset(WI[1][:, HB - 1, :], 0).then_inc(scales_cleared, 1)
                e.memset(WFD[:, :, HID:HB * P], 0.0).then_inc(dequant, 1)
                for c in range(NC):
                    e.wait_ge(outputs_landed, 16 * (c + 1))
                    e.wait_ge(inverses_landed, 32 * (c + 1))
                    for g in range(PAIRS):
                        e.tensor_tensor(OT[:, 0, g, :], OT[:, 0, g, :], RB[:, 0, g, :], ALU.mult).then_inc(normalised, 1)

            @block.scalar
            def _(e):
                def root(c):
                    e.wait_ge(f_rec, c + 1)
                    e.activation(rs[:, 1, CB * c:CB * c + CB], rs[:, 0, CB * c:CB * c + CB], ACT.Sqrt).then_inc(f_root, 1)

                root(0)
                for c in range(NC):
                    if c + 1 < NC:
                        root(c + 1)
                    for a in range(DH):
                        e.wait_ge(h_filled, DH * c + a + 1)
                        if a == 0 and c:
                            e.wait_ge(h_low, c)
                        e.activation(hF[:, a, :], ps[:, a, :], ACT.Identity, bias=modc[:, 6 + a:7 + a],
                                     scale=scale1[:, 2 + a:3 + a]).then_inc(h_full, 1)
                    e.wait_ge(h_full, DH * c + DH)
                    if c:
                        e.wait_ge(gu_ready, HB * c)
                    e.activation(hH[:, :, :], hF[:, :, :], ACT.Copy).then_inc(h_high, 1)
                    for hb in range(HB):
                        e.wait_ge(gu_ready, HB * c + hb + 1)
                        if HB * c + hb >= 2:
                            e.wait_ge(act_ready, HB * c + hb - 1)
                        e.activation(SG[:, hb % 2, :], ps[:, 2 + 2 * (hb % 2), :], ACT.Silu).then_inc(silu_done, 1)

            @block.vector
            def _(e):
                v = nc.vector
                steps = [0]

                def settle(ins):
                    steps[0] += 1
                    ins.then_inc(f_step, 1)
                    e.wait_ge(f_step, steps[0])

                def attend_and_norm(c):
                    for k in range(2):
                        e.wait_ge(projected, 2 * c + k + 1)
                        rows = X[:, CB * c + 2 * k:CB * c + 2 * k + 2, :]
                        v.tensor_tensor(rows, ps[:, 6 + k, :].rearrange("p (t d) -> p t d", t=2), rows, ALU.add).then_inc(residual_added, 1)
                    e.wait_ge(residual_added, 2 * c + 2)
                    tiles = range(CB * c, CB * c + CB)
                    for t in tiles:
                        last = v.bn_stats(st[:, t, :], X[:, t, :])
                    settle(last)
                    for t in tiles:
                        last = v.bn_aggr(mv[:, t, :], st[:, t, :])
                    settle(last)
                    b, r, a = (rs[:, k, CB * c:CB * c + CB] for k in range(3))
                    settle(v.tensor_scalar(a, mv[:, CB * c:CB * c + CB, 1], LN_EPS, None, ALU.add))
                    v.reciprocal(b, a).then_inc(f_rec, 1)
                    e.wait_ge(f_root, c + 1)
                    settle(v.tensor_tensor(b, r, r, ALU.mult))
                    settle(v.tensor_tensor(b, b, a, ALU.mult))
                    settle(v.tensor_scalar(b, b, -0.5, 1.5, ALU.mult, ALU.add))
                    settle(v.tensor_tensor(r, r, b, ALU.mult))
                    if c >= 2:
                        e.wait_ge(h_filled, DH * (c - 1))
                    for n, t in enumerate(tiles):
                        last = v.tensor_scalar(Z[:, c % 2, n, :], X[:, t, :], mv[:, t, 0:1], rs[:, 1, t:t + 1], ALU.subtract, ALU.mult)
                    last.then_inc(f_z, 1)

                e.wait_ge(sums_landed, 16)
                v.reciprocal(sums[:, 1, :], sums[:, 0, :]).then_inc(sums_inverted, 1)
                e.wait_ge(scales_landed, 16 * 5)
                e.wait_ge(wi_landed, 16 * 5)
                settle(v.tensor_tensor(sd[:, 1, :], sd[:, 0, :], gates[:, 2:4], ALU.mult))
                for n in range(2):
                    for b in range(HB):
                        v.tensor_scalar(WF[:, n, b, :], WI[n][:, b, :], ZERO_POINT, sc[:, n, b:b + 1], ALU.subtract, ALU.mult)
                for a in range(DH):
                    last = v.tensor_scalar(WFD[:, a, 0:HID], WID[:, a, :], ZERO_POINT, sd[:, 1, a:a + 1], ALU.subtract, ALU.mult)
                last.then_inc(dequant, 1)
                wtf = WTf[:, :, :, :].rearrange("p n a h -> p (n a h)")
                for k in range(6):
                    e.wait_ge(f_filled, k + 1)
                    v.tensor_copy(wtf[:, C * k:C * k + C], ps[:, k, :]).then_inc(f_emptied, 1)
                for k in range(3):
                    e.wait_ge(f_filled, 6 + k + 1)
                    last = v.tensor_copy(WDN[:, 2 * k:2 * k + 2, :], ps[:, (0, 1, 2)[k], :].rearrange("p (b d) -> p b d", b=2))
                    last.then_inc(f_emptied, 1)
                attend_and_norm(0)
                e.wait_ge(f_emptied, 9)
                settle(v.tensor_copy(WT[0][:, :, :, :], WTf[:, :, :, :]))
                v.tensor_tensor(WT[1][:, :, :, :], WTf[:, :, :, :], WT[0][:, :, :, :].bitcast(F32), ALU.subtract).then_inc(w_ready, 1)
                for c in range(NC):
                    if c + 1 < NC:
                        attend_and_norm(c + 1)
                    e.wait_ge(h_high, c + 1)
                    if c:
                        e.wait_ge(gu_ready, HB * c)
                    v.tensor_tensor(hL[:, :, :], hF[:, :, :], hH[:, :, :].bitcast(F32), ALU.subtract).then_inc(h_low, 1)
                    for hb in range(HB):
                        e.wait_ge(silu_done, HB * c + hb + 1)
                        if hb == 0 and c:
                            e.wait_ge(down_ready, 2 * c)
                        v.tensor_tensor(AT[:, hb, :], ps[:, 3 + 2 * (hb % 2), :], SG[:, hb % 2, :], ALU.mult).then_inc(act_ready, 1)
                    for k in range(2):
                        e.wait_ge(down_ready, 2 * c + k + 1)
                        rows = X[:, CB * c + 2 * k:CB * c + 2 * k + 2, :]
                        v.tensor_tensor(rows, ps[:, 6 + k, :].rearrange("p (t d) -> p t d", t=2), rows, ALU.add).then_inc(out_ready, 1)

            @block.tensor
            def _(e):
                t_ = nc.tensor

                def project(c):
                    e.wait_ge(normalised, PAIRS * (c + 1))
                    if c >= 2:
                        e.wait_ge(out_ready, 2 * (c - 1))
                    for k in range(2):
                        for m in range(2):
                            b = 2 * k + m
                            for g in range(PAIRS):
                                last = t_.matmul(ps[:, 6 + k, D * m:D * m + D], OT[:, 0, g, P * b:P * b + P], WVO[:, g, :],
                                                 start=(g == 0), stop=(g == PAIRS - 1))
                        last.then_inc(projected, 1)

                e.wait_ge(dequant, 2)
                blocks = [(n, a, b) for n in range(2) for a in range(DH) for b in range(HB)]
                for k in range(6):
                    for m in range(4):
                        n, a, b = blocks[4 * k + m]
                        last = t_.transpose(ps[:, k, P * m:P * m + P], WF[:, n, b, P * a:P * a + P], ident[:, :])
                    last.then_inc(f_filled, 1)
                for k in range(3):
                    e.wait_ge(f_emptied, k + 1)
                    for m in range(2):
                        for a in range(DH):
                            last = t_.transpose(ps[:, k, D * m + P * a:D * m + P * a + P],
                                                WFD[:, a, P * (2 * k + m):P * (2 * k + m) + P], ident[:, :])
                    last.then_inc(f_filled, 1)
                project(0)
                for c in range(NC):
                    if c + 1 < NC:
                        e.wait_ge(residual_added, 2 * c + 2)
                        if c:
                            e.wait_ge(out_ready, 2 * c)
                        project(c + 1)
                    e.wait_ge(f_emptied, 9)
                    e.wait_ge(f_z, c + 1)
                    if c:
                        e.wait_ge(h_full, DH * c)
                    for a in range(DH):
                        for n in range(CB):
                            last = t_.transpose(ps[:, a, P * n:P * n + P], Z[:, c % 2, n, P * a:P * a + P], ident[:, :])
                        last.then_inc(h_filled, 1)
                    e.wait_ge(w_ready, 1)
                    e.wait_ge(h_low, c + 1)
                    for hb in range(HB):
                        if HB * c + hb >= 2:
                            e.wait_ge(act_ready, HB * c + hb - 1)
                        for n in range(2):
                            k = 0
                            for a in range(DH):
                                for w, h in ((0, hH), (0, hL), (1, hH)):
                                    last = t_.matmul(ps[:, 2 + 2 * (hb % 2) + n, :], WT[w][:, n, a, P * hb:P * hb + P], h[:, a, :],
                                                     start=(k == 0), stop=(k == 5))
                                    k += 1
                        last.then_inc(gu_ready, 1)
                    e.wait_ge(act_ready, HB * (c + 1))
                    if c + 1 < NC:
                        e.wait_ge(residual_added, 2 * c + 4)
                    for k in range(2):
                        for m in range(2):
                            b = 2 * k + m
                            for hb in range(HB):
                                last = t_.matmul(ps[:, 6 + k, D * m:D * m + D], AT[:, hb, P * b:P * b + P], WDN[:, hb, :],
                                                 start=(hb == 0), stop=(hb == HB - 1))
                        last.then_inc(down_ready, 1)


_INS = ["L0_attn_x", "L0_attn_wq_down", "L0_attn_q_norm_w", "L0_attn_wq_up", "L0_attn_wq_rope", "L0_attn_wkv_down",
        "L0_attn_kv_norm_w", "L0_attn_wkv_up", "L0_attn_wk_rope", "L0_attn_wo", "L0_ffn_wq_gate", "L0_ffn_s_gate",
        "L0_ffn_wq_up", "L0_ffn_s_up", "L0_ffn_wq_down", "L0_ffn_s_down", "L0_c", "L0_wmod"]


def shape_constants():
    inv = np.float32(1.0) / np.power(np.float32(10000.0), np.arange(0, ROPE, 2, dtype=np.float32) / np.float32(ROPE))
    angle = np.outer(np.arange(S, dtype=np.float32), inv.astype(np.float32)).astype(np.float32)
    cos, sin = np.cos(angle).astype(np.float32), np.sin(angle).astype(np.float32)
    row = np.arange(P)
    masks = np.stack([np.where(row[None, :] > row[:, None], NEG, 0.0), np.where(row[:, None] > row[None, :], NEG, 0.0)]).astype(np.float32)
    cosq = np.repeat(cos.T, 2, axis=0)
    sinq = np.repeat(sin.T, 2, axis=0) * np.tile([-1.0, 1.0], ROPE // 2)[:, None]
    rope_q = np.stack([np.concatenate([cosq, cosq]), np.concatenate([sinq, sinq])]).astype(np.float32)
    return {"ident": np.eye(P, dtype=np.float32), "masks": masks, "rope_nat": np.stack([cos, sin]), "rope_q": rope_q}


def kernel(**inputs):
    import concourse.bacc as _bacc
    from concourse import mybir as _mybir
    from concourse.bass_utils import run_bass_kernel_spmd as _run

    nc = _bacc.Bacc("TRN2", target_bir_lowering=False, num_devices=1)
    arrays, args = {}, []
    given = [(n, inputs[n]) for n in _INS] + list(shape_constants().items())
    for name, value in given:
        a = np.ascontiguousarray(value)
        arrays[f"in_{name}_dram"] = a
        args.append(nc.dram_tensor(f"in_{name}_dram", a.shape, _mybir.dt.from_np(a.dtype), kind="ExternalInput").ap())
    out = nc.dram_tensor("out_0_dram", (1, S, D), _mybir.dt.float32, kind="ExternalOutput").ap()
    build(nc, *args, out)
    r = _run(nc, [arrays], core_ids=[0])
    return r.results[0]["out_0_dram"]
```

```python
from contextlib import ExitStack

import numpy as np

import concourse.bass as bass
from concourse import mybir

F32 = mybir.dt.float32
F32R = mybir.dt.float32r
BF16 = mybir.dt.bfloat16
I32 = mybir.dt.int32
ALU = mybir.AluOpType
ACT = mybir.ActivationFunctionType
AX = mybir.AxisListType

P = 128
S = 2048
D = 256
DH = D // P
H = 16
PAIRS = H // 2
NOPE, ROPE, VD = 128, 64, 128
QR, KR = 128, 64
HID = 704
HB = 6
TT = S // P
C = 512
NC = S // C
CB = C // P
HLAST = HID - (HB - 1) * P
ZERO_POINT = 128.0
NEG = -1.0e30
SCALE = float(1.0 / np.sqrt(NOPE + ROPE))
LN_EPS, RMS_EPS = 1e-5, 1e-6

UNITS = [CB * (c + 1) for c in range(NC)]
U0 = [sum(UNITS[:c]) for c in range(NC + 1)]
STEPS = U0[NC]
PIECES = 2 * STEPS
G = 2
NG = PAIRS // G
LEAD = 23


def in_place(nc, stack, name, shape, dt, dt_after):
    with nc.sbuf_tensor(f"{name}_first", shape, dt) as first:
        pass
    return first, stack.enter_context(nc.sbuf_tensor(name, shape, dt_after))


def build(nc, x, wq_down, q_norm_w, wq_up, wq_rope, wkv_down, kv_norm_w, wkv_up, wk_rope, wo,
          wq_gate, s_gate, wq_up_ffn, s_up, wq_down_ffn, s_down, cvec, wmod,
          ident_c, masks_c, rope_nat, rope_q, out):
    with ExitStack() as base:
        base.enter_context(nc.allow_non_contiguous_dma(reason="vectors of a few hundred elements laid over the partitions"))
        def sb(stack, name, shape, dt=F32):
            return stack.enter_context(nc.sbuf_tensor(name, shape, dt))

        def sem(name):
            return base.enter_context(nc.semaphore(name))

        ps = base.enter_context(nc.psum_tensor("ps", [P, 8, C], F32))
        wq_d = nc.dram_tensor("wq_scratch", (PAIRS, P, 2 * 2 * P), F32, kind="Internal").ap()
        o_d = nc.dram_tensor("o_scratch", (PAIRS, P, S), F32, kind="Internal").ap()
        l_d = nc.dram_tensor("l_scratch", (H, S), F32, kind="Internal").ap()
        ffn_d = nc.dram_tensor("ffn_scratch", (P, 3, DH * HB * P), F32, kind="Internal").ap()
        r_d = nc.dram_tensor("r_scratch", (H, S), F32, kind="Internal").ap()
        X = sb(base, "X", [P, TT, D])
        ident = sb(base, "ident", [P, P])
        identb = sb(base, "identb", [P, P], BF16)
        masks = sb(base, "masks", [P, 2, P])
        maskb = sb(base, "maskb", [P, 2, P], BF16)
        ones = sb(base, "ones", [P, 64])
        WVO, WVL = in_place(nc, base, "WVO", [P, PAIRS, D], F32, F32R)
        modc = sb(base, "modc", [P, 12])
        scale1 = sb(base, "scale1", [P, 4])
        gates = sb(base, "gates", [P, 4])
        small = sb(base, "small", [P, 64])
        Osb = sb(base, "Osb", [P, 2, C])
        Lsb = sb(base, "Lsb", [64, 2, C])
        LP = sb(base, "LP", [P, 2, 2 * S // P])
        results_stored = [sem(f"results_stored_{c}") for c in range(NC)]

        def pair_rows(d, p):
            rows = d[2 * p:2 * p + 2, :] if isinstance(p, int) else d[bass.ds(2 * p, 2), :]
            return rows.rearrange("h (a n) -> (h a) n", n=2 * S // P)

        st = sb(base, "st", [P, TT, 6])
        mv = sb(base, "mv", [P, TT, 2])
        rs = sb(base, "rs", [P, 3, 2 * TT])

        with ExitStack() as early:
            FI, FW = [], []
            for n, name in enumerate(("gate", "up", "down")):
                shape = [P, HB, D] if n < 2 else [P, DH, HB * P]
                whole, same = in_place(nc, early, f"ffn_{name}", shape, I32, F32)
                FI.append(whole)
                FW.append(same)
            FTD = sb(early, "ffn_down_t", [P, HB * D])
        with ExitStack() as later:
            OF, OL = in_place(nc, later, "outputs", [P, 2, PAIRS, C], F32, F32R)
            WTH = sb(later, "wt_hi", [P, 2, DH, HB * P], F32R)
            WTF, WTL = in_place(nc, later, "wt_lo", [P, 2, DH, HB * P], F32, F32R)
            hH = sb(later, "hH", [P, DH, C], F32R)
            RB = sb(later, "RB", [P, PAIRS, C])
        outputs_landed = [[sem(f"outputs_landed_{k}_{g}") for g in range(NG)] for k in range(2)]
        inverses_landed = [sem(f"inverses_landed_{g}") for g in range(NG)]

        def load_outputs(e, c, g):
            e.dma_start(OF[:, c % 2, G * g:G * g + G, :],
                        o_d[G * g:G * g + G, :, C * c:C * c + C].rearrange("g p n -> p g n")).then_inc(outputs_landed[c % 2][g], 16)

        def load_inverses(e, c, g):
            for o in range(2):
                src = r_d.rearrange("(g o) s -> o g s", o=2)[o, G * g:G * g + G, C * c:C * c + C].partition_broadcast(64)
                e.dma_start(RB[64 * o:64 * o + 64, G * g:G * g + G, :], src).then_inc(inverses_landed[g], 16)

        attn_kept = base.enter_context(ExitStack())
        QT = [sb(attn_kept, n, [P, S], F32R) for n in ("qt_hi", "qt_lo")]
        K = [[sb(attn_kept, f"k{v}_{n}", [P, S], F32R) for n in ("hi", "lo")] for v in range(2)]
        KN = sb(attn_kept, "KN", [P, TT, 192])

        with ExitStack() as scratch:
            Z = sb(scratch, "Z", [P, TT, D])
            hT = sb(scratch, "hT", [P, DH, S])
            WU = sb(scratch, "WU", [P, H, QR])
            WKV = sb(scratch, "WKV", [P, 2 * H, KR])
            WR = sb(scratch, "WR", [P, PAIRS, QR])
            WO = sb(scratch, "WO", [P, DH, H * VD])
            WMOD = sb(scratch, "WMOD", [P, DH, 6 * D])
            WD = WVO
            WDT = sb(scratch, "WDT", [P, DH, D])
            ropeN = sb(scratch, "ropeN", [P, 2, TT, ROPE // 2])
            cc = sb(scratch, "cc", [P, 6, DH])
            qnw = sb(scratch, "qnw", [P, 1])
            kvw = sb(scratch, "kvw", [P, 3])
            WQ = sb(scratch, "WQ", [P, PAIRS, 2, 2, P], F32R)
            fsc = sb(scratch, "fsc", [P, 2, HB])
            fsd = sb(scratch, "fsd", [P, 2, DH])
            PJ = Z
            SQ = WU[:, :, :].rearrange("p h r -> p (h r)")[:, 0:TT // 2 * 192].rearrange("p (t c) -> p t c", c=192)
            woT = hT[:, :, :].rearrange("p a (h d) -> p (a h) d", d=D)
            WQf = WMOD[:, :, :].rearrange("p a n -> p (a n)")[:, 0:PAIRS * 2 * P].rearrange("p (g m r) -> p g m r", g=PAIRS, m=2)
            FTh = hT[:, :, :].rearrange("p a b -> p (a b)")
            FT = [FTD[:, :], FTh[:, 0:DH * HB * P], FTh[:, DH * HB * P:2 * DH * HB * P]]
            rope_tmp = WR[:, :, :].rearrange("p g r -> p (g r)")[:, 0:TT * ROPE // 2].rearrange("p (k t r) -> p k t r", k=2, r=ROPE // 2)

            groups = (("WD", "A"), ("MOD", "V"), ("ZT", "A" * (2 * NC)), ("MOD2", "V"), ("PROJ", "A" * (TT // 4)), ("ABS", "VV"), ("ROPE", "VV"),
                      ("PROJ2", "A" * (TT // 4)), ("FFN", "A" * 9), ("QK", "V" * (3 * NC)), ("WOT", "AV" * (H // 4)), ("WVO", "VA" * (PAIRS // 4)))
            jobs, first_job = "", {}
            for name, readers in groups:
                first_job[name] = len(jobs)
                jobs += readers
            J_WD, J_MOD, J_MOD2, J_ZT, J_ABS, J_ROPE, J_FFN, J_QK, J_WOT, J_WVO = (
                first_job[n] for n in ("WD", "MOD", "MOD2", "ZT", "ABS", "ROPE", "FFN", "QK", "WOT", "WVO"))

            def j_proj(k):
                return first_job["PROJ"] + k if k < TT // 4 else first_job["PROJ2"] + k - TT // 4

            x_landed, c_landed, small_landed, wd_landed, abs_landed = [sem(f"x_landed_{q}") for q in range(4)], sem("c_landed"), sem("small_landed"), sem("wd_landed"), sem("abs_landed")
            wr_landed, ident_landed = sem("wr_landed"), sem("ident_landed")
            masks_landed, rope_landed, wmod_landed, wo_landed = sem("masks_landed"), sem("rope_landed"), [sem("wmod_landed_0"), sem("wmod_landed_1")], sem("wo_landed")
            filled = sem("prep_bank_filled")
            emptied = {"A": sem("prep_emptied_by_scalar"), "V": sem("prep_emptied_by_vector")}
            dve_step, pool_step = sem("prep_vector_step"), sem("prep_pool_step")
            z_ready, silu_exp, var_rec, std_ready = sem("z_ready"), sem("silu_exp"), sem("var_rec"), sem("std_ready")
            silu_ready, mod_ready, rms_rec, rms_root, rms_ready = sem("silu_ready"), sem("mod_ready"), sem("rms_rec"), sem("rms_root"), sem("rms_ready")
            wq_stored, ffn_stored, ffn_down_stored = sem("wq_stored"), sem("ffn_stored"), sem("ffn_down_stored")
            ffn_landed, ffn_scales_landed, ffn_cleared = sem("ffn_landed"), sem("ffn_scales_landed"), sem("ffn_cleared")
            ffn_dequant = sem("ffn_dequantised")
            ones_set, wq_high, wq_low = sem("ones_set"), sem("wq_high"), sem("wq_low")
            q_nat_ready, kv_nat_ready, rope_nat_ready, wo_scaled = [sem("q_nat_ready_0"), sem("q_nat_ready_1")], sem("kv_nat_ready"), sem("rope_nat_ready"), sem("wo_scaled")
            qk_high = sem("qk_high")
            HT = TT // 2

            def emptied_count(job):
                return sum(1 for e in jobs[:job + 1] if e == jobs[job])

            def wait_emptied(e, job):
                e.wait_ge(emptied[jobs[job]], emptied_count(job))

            def by_half(k, hf):
                return rs[:, k, :].rearrange("p (s t) -> p s t", s=2)[:, :, HT * hf:HT * hf + HT]

            with nc.Block() as block:
                @block.sync
                def _(e):
                    xv = x.rearrange("a (t p) d -> p (a t) d", p=P)
                    for q in range(4):
                        e.dma_start(X[:, 4 * q:4 * q + 4, :], xv[:, 4 * q:4 * q + 4, :]).then_inc(x_landed[q], 16)
                    e.dma_start(WU[:, :, :], wq_up.rearrange("(h p) r -> p h r", p=P)).then_inc(abs_landed, 16)
                    e.dma_start(WKV[:, :, :], wkv_up.rearrange("(h p) r -> p h r", p=P)).then_inc(abs_landed, 16)
                    e.dma_start(WR[:, :, :], wq_rope.rearrange("(g p) r -> p g r", p=P)).then_inc(wr_landed, 16)
                    e.wait_ge(ffn_cleared, 4)
                    for n, (w, sc) in enumerate(((wq_gate, s_gate), (wq_up_ffn, s_up))):
                        e.dma_start(FI[n][:, 0:HB - 1, :], w[0:(HB - 1) * P, :].rearrange("(b p) d -> p b d", p=P)).then_inc(ffn_landed, 16)
                        e.dma_start(FI[n][0:HLAST, HB - 1, :], w[(HB - 1) * P:HID, :]).then_inc(ffn_landed, 16)
                    e.dma_start(FI[2][:, :, 0:HID], wq_down_ffn.rearrange("(a p) n -> p a n", p=P)).then_inc(ffn_landed, 16)
                    e.dma_start(ropeN[:, :, :, :], rope_nat.rearrange("k (t p) r -> p k t r", p=P)).then_inc(rope_landed, 16)
                    e.dma_start(WO[:, :, :], wo.rearrange("(a p) n -> p a n", p=P)).then_inc(wo_landed, 16)
                    wait_emptied(e, J_FFN + 2)
                    e.dma_start(ffn_d[:, 2, :], FT[0]).then_inc(ffn_down_stored, 16)
                    wait_emptied(e, J_FFN + 8)
                    for n in range(2):
                        e.dma_start(ffn_d[:, n, :], FT[1 + n]).then_inc(ffn_stored, 16)
                    e.wait_ge(wq_high, 1)
                    e.wait_ge(wq_low, 1)
                    e.dma_start(wq_d.rearrange("g p n -> p g n"), WQ[:, :, :, :, :].rearrange("p g a m r -> p g (a m r)").bitcast(F32)).then_inc(wq_stored, 16)
                    e.wait_ge(wq_stored, 16)
                    e.wait_ge(ffn_down_stored, 16)
                    e.wait_ge(ffn_stored, 32)

                @block.gpsimd
                def _(e):
                    e.dma_start(ident[:, :], ident_c).then_inc(ident_landed, 16)
                    e.memset(kvw[:, :], 1.0).then_inc(ones_set, 1)
                    e.memset(ones[:, :], 1.0)
                    e.memset(fsc[:, :, :], 0.0).then_inc(ffn_cleared, 1)
                    for n in range(2):
                        e.memset(FI[n][:, HB - 1, :], 0).then_inc(ffn_cleared, 1)
                    e.memset(FW[2][:, :, HID:HB * P], 0.0).then_inc(ffn_cleared, 1)
                    e.dma_start(qnw[:, :], q_norm_w.rearrange("(p a) -> p a", a=1)).then_inc(small_landed, 16)
                    e.wait_ge(ones_set, 1)
                    for col, row in ((0, 0), (1, KR), (2, 0), (2, KR)):
                        e.dma_start(kvw[row:row + KR, col:col + 1], kv_norm_w.rearrange("(p a) -> p a", a=1)).then_inc(small_landed, 16)
                    e.dma_start(masks[:, :, :], masks_c.rearrange("k p n -> p k n")).then_inc(masks_landed, 16)
                    e.wait_ge(ffn_cleared, 4)
                    for n, sc in enumerate((s_gate, s_up)):
                        e.dma_start(fsc[:, n, 0:HB - 1], sc[0:(HB - 1) * P].rearrange("(b p) -> p b", p=P)).then_inc(ffn_scales_landed, 16)
                        e.dma_start(fsc[0:HLAST, n, HB - 1:HB], sc[(HB - 1) * P:HID].rearrange("(p b) -> p b", b=1)).then_inc(ffn_scales_landed, 16)
                    e.dma_start(fsd[:, 0, :], s_down.rearrange("(a p) -> p a", p=P)).then_inc(ffn_scales_landed, 16)
                    e.wait_ge(rope_landed, 16)
                    e.wait_ge(filled, J_ROPE + 2)
                    done = 0
                    for hf in range(2):
                        wait_emptied(e, j_proj(4 * hf + 3))
                        ts = slice(HT * hf, HT * hf + HT)
                        kr = PJ[:, ts, 192:256].rearrange("p t (r o) -> p t r o", o=2)
                        kn = KN[:, ts, :].rearrange("p t (m r o) -> p t m r o", m=3, o=2)
                        cosn, sinn = ropeN[:, 0, ts, :], ropeN[:, 1, ts, :]
                        for o, (f0, f1, op) in enumerate(((cosn, sinn, ALU.subtract), (sinn, cosn, ALU.add))):
                            e.tensor_tensor(rope_tmp[:, 0, :, :], kr[:, :, :, 0], f0, ALU.mult).then_inc(pool_step, 1)
                            e.tensor_tensor(rope_tmp[:, 1, :, :], kr[:, :, :, 1], f1, ALU.mult).then_inc(pool_step, 1)
                            done += 2
                            e.wait_ge(pool_step, done)
                            for m in (0, 2):
                                last = e.tensor_tensor(kn[:, :, m, :, o], rope_tmp[:, 0, :, :], rope_tmp[:, 1, :, :], op)
                            last.then_inc(rope_nat_ready, 1)
                            e.wait_ge(rope_nat_ready, 2 * hf + o + 1)
                    e.wait_ge(wq_high, 1)
                    e.tensor_tensor(WQ[:, :, 1, :, :], WQf, WQ[:, :, 0, :, :].bitcast(F32), ALU.subtract).then_inc(wq_low, 1)

                @block.scalar
                def _(e):
                    e.dma_start(cc[:, 0, :], cvec.rearrange("a (k p) -> p (a k)", p=P)).then_inc(c_landed, 16)
                    e.dma_start(WD[:, 0, :], wq_down).then_inc(wd_landed, 16)
                    e.dma_start(WD[0:KR, 1, :], wkv_down).then_inc(wd_landed, 16)
                    e.dma_start(WD[KR:P, 1, :], wk_rope).then_inc(wd_landed, 16)
                    for n, cols in enumerate((slice(0, 2 * D), slice(2 * D, 6 * D))):
                        e.dma_start(WMOD[:, :, cols], wmod[:, cols].rearrange("(a p) n -> p a n", p=P)).then_inc(wmod_landed[n], 16)
                    e.wait_ge(c_landed, 16)
                    e.activation(cc[:, 1, :], cc[:, 0, :], ACT.Exp, scale=-1.0).then_inc(silu_exp, 1)
                    for hf in range(2):
                        ts = slice(HT * hf, HT * hf + HT)
                        e.wait_ge(var_rec, hf + 1)
                        e.activation(rs[:, 1, ts], rs[:, 0, ts], ACT.Sqrt).then_inc(std_ready, 1)
                    e.wait_ge(filled, J_WD + 1)
                    e.activation(WDT[:, :, :], ps[:, J_WD % 8, :].rearrange("p (a n) -> p a n", a=DH), ACT.Copy).then_inc(emptied["A"], 1)
                    e.wait_ge(mod_ready, 1)
                    for k in range(2 * NC):
                        tg, half = k // 2, k % 2
                        e.wait_ge(filled, J_ZT + k + 1)
                        e.activation(hT[:, half, C * tg:C * tg + C], ps[:, (J_ZT + k) % 8, :], ACT.Identity,
                                     bias=modc[:, half:half + 1], scale=scale1[:, half:half + 1]).then_inc(emptied["A"], 1)
                    for k in range(TT // 2):
                        e.wait_ge(filled, j_proj(k) + 1)
                        e.activation(PJ[:, 2 * k:2 * k + 2, :], ps[:, j_proj(k) % 8, :].rearrange("p (t n) -> p t n", t=2),
                                     ACT.Copy).then_inc(emptied["A"], 1)
                    wait_emptied(e, J_ROPE + 1)
                    e.activation(WQ[:, :, 0, :, :], WQf, ACT.Copy).then_inc(wq_high, 1)
                    for k in range(9):
                        e.wait_ge(filled, J_FFN + k + 1)
                        e.activation(FT[k // 3][:, C * (k % 3):C * (k % 3) + C], ps[:, (J_FFN + k) % 8, :], ACT.Copy).then_inc(emptied["A"], 1)
                    for hf in range(2):
                        e.wait_ge(rms_rec, hf + 1)
                        e.activation(by_half(1, hf), by_half(0, hf), ACT.Sqrt).then_inc(rms_root, 1)
                    e.wait_ge(rms_ready, 1)
                    for t in range(HT):
                        e.activation(PJ[:, t, 0:QR], PJ[:, t, 0:QR], ACT.Identity, scale=rs[:, 1, t:t + 1]).then_inc(q_nat_ready[0], 1)
                    e.wait_ge(small_landed, 16 * 5)
                    e.wait_ge(ffn_down_stored, 16)
                    for k in range(3 * NC):
                        tg, kind = k // 3, k % 3
                        hi = (QT if kind == 0 else K[kind - 1])[0][:, C * tg:C * tg + C]
                        e.wait_ge(filled, J_QK + k + 1)
                        if kind == 0:
                            e.activation(hi, ps[:, (J_QK + k) % 8, :], ACT.Copy).then_inc(qk_high, 1)
                        else:
                            e.activation(hi, ps[:, (J_QK + k) % 8, :], ACT.Identity, scale=kvw[:, kind - 1:kind]).then_inc(qk_high, 1)
                    e.wait_ge(ffn_stored, 32)
                    for k in range(0, H // 2, 2):
                        e.wait_ge(filled, J_WOT + k + 1)
                        e.activation(woT[:, 2 * k:2 * k + 2, :], ps[:, (J_WOT + k) % 8, :].rearrange("p (h d) -> p h d", h=2), ACT.Copy).then_inc(emptied["A"], 1)
                    for k in range(1, PAIRS // 2, 2):
                        e.wait_ge(filled, J_WVO + k + 1)
                        e.activation(WVO[:, 2 * k:2 * k + 2, :], ps[:, (J_WVO + k) % 8, :].rearrange("p (g d) -> p g d", g=2),
                                     ACT.Identity, scale=kvw[:, 2:3]).then_inc(emptied["A"], 1)

                @block.vector
                def _(e):
                    steps = [0]

                    def settle(ins):
                        steps[0] += 1
                        ins.then_inc(dve_step, 1)
                        e.wait_ge(dve_step, steps[0])

                    v = nc.vector

                    def measure(hf):
                        for t in range(HT * hf, HT * hf + HT):
                            if t % 4 == 0:
                                e.wait_ge(x_landed[t // 4], 16)
                            last = v.bn_stats(st[:, t, :], X[:, t, :])
                        settle(last)
                        for t in range(HT * hf, HT * hf + HT):
                            last = v.bn_aggr(mv[:, t, :], st[:, t, :])
                        settle(last)
                        ts = slice(HT * hf, HT * hf + HT)
                        settle(v.tensor_scalar(rs[:, 2, ts], mv[:, ts, 1], LN_EPS, None, ALU.add))
                        v.reciprocal(rs[:, 0, ts], rs[:, 2, ts]).then_inc(var_rec, 1)

                    def refine(tmp, root, a):
                        settle(v.tensor_tensor(tmp, root, root, ALU.mult))
                        settle(v.tensor_tensor(tmp, tmp, a, ALU.mult))
                        settle(v.tensor_scalar(tmp, tmp, -0.5, 1.5, ALU.mult, ALU.add))
                        return v.tensor_tensor(root, root, tmp, ALU.mult)

                    def norm(hf):
                        e.wait_ge(std_ready, hf + 1)
                        ts = slice(HT * hf, HT * hf + HT)
                        settle(refine(rs[:, 0, ts], rs[:, 1, ts], rs[:, 2, ts]))
                        for t in range(HT * hf, HT * hf + HT):
                            v.tensor_scalar(Z[:, t, :], X[:, t, :], mv[:, t, 0:1], rs[:, 1, t:t + 1],
                                            ALU.subtract, ALU.mult).then_inc(z_ready, 1)

                    measure(0)
                    e.wait_ge(silu_exp, 1)
                    settle(v.tensor_scalar(cc[:, 2, :], cc[:, 1, :], 1.0, None, ALU.add))
                    settle(v.reciprocal(cc[:, 3, :], cc[:, 2, :]))
                    v.tensor_tensor(cc[:, 4, :], cc[:, 0, :], cc[:, 3, :], ALU.mult).then_inc(silu_ready, 1)
                    norm(0)
                    measure(1)
                    e.wait_ge(filled, J_MOD + 1)
                    v.tensor_copy(modc[:, 0:4], ps[:, J_MOD % 8, 0:4]).then_inc(emptied["V"], 1)
                    e.wait_ge(emptied["V"], emptied_count(J_MOD))
                    v.tensor_scalar(scale1[:, 0:2], modc[:, 2:4], 1.0, None, ALU.add).then_inc(mod_ready, 1)
                    norm(1)
                    e.wait_ge(filled, J_MOD2 + 1)
                    v.tensor_copy(modc[:, 4:12], ps[:, J_MOD2 % 8, 4:12]).then_inc(emptied["V"], 1)
                    e.wait_ge(emptied["V"], emptied_count(J_MOD2))
                    v.tensor_scalar(scale1[:, 2:4], modc[:, 8:10], 1.0, None, ALU.add)
                    for n, k in enumerate((2, 5)):
                        g = modc[:, 2 * k:2 * k + 2]
                        v.tensor_scalar(small[:, 2 * n:2 * n + 2], g, 0.0, 2.0, ALU.is_ge, ALU.mult)
                        last = v.tensor_scalar(small[:, 4 + 2 * n:6 + 2 * n], g, -1.0, None, ALU.mult)
                    settle(last)
                    for n, k in enumerate((2, 5)):
                        g = modc[:, 2 * k:2 * k + 2]
                        v.tensor_scalar(small[:, 8 + 2 * n:10 + 2 * n], small[:, 2 * n:2 * n + 2], -1.0, None, ALU.add)
                        last = v.tensor_tensor(small[:, 12 + 2 * n:14 + 2 * n], g, small[:, 4 + 2 * n:6 + 2 * n], ALU.max)
                    settle(last)
                    settle(v.tensor_scalar(small[:, 16:20], small[:, 12:16], 0.25, None, ALU.max))
                    settle(v.tensor_tensor(gates[:, :], small[:, 16:20], small[:, 8:12], ALU.mult))
                    e.wait_ge(ident_landed, 16)
                    e.wait_ge(masks_landed, 16)
                    v.tensor_copy(identb[:, :], ident[:, :])
                    v.tensor_copy(maskb[:, :, :], masks[:, :, :])
                    e.wait_ge(small_landed, 16 * 5)
                    for k in range(2):
                        e.wait_ge(filled, J_ABS + k + 1)
                        v.tensor_scalar(WQf[:, 4 * k:4 * k + 4, 0, :], ps[:, (J_ABS + k) % 8, :].rearrange("p (g r) -> p g r", g=4),
                                        qnw[:, 0:1], None, ALU.mult).then_inc(emptied["V"], 1)
                    for k in range(2):
                        e.wait_ge(filled, J_ROPE + k + 1)
                        src = ps[:, (J_ROPE + k) % 8, :].rearrange("p (g a t) -> p g a t", g=4, a=2)
                        dst = WQf[:, 4 * k:4 * k + 4, 1, :].rearrange("p g (a t) -> p g a t", a=2)
                        for a in range(2):
                            last = v.tensor_scalar(dst[:, :, a, :], src[:, :, 1 - a, :], qnw[:, 0:1], None, ALU.mult)
                        last.then_inc(emptied["V"], 1)
                    e.wait_ge(ffn_scales_landed, 16 * 5)
                    e.wait_ge(ffn_landed, 16 * 5)
                    settle(v.tensor_tensor(fsd[:, 1, :], fsd[:, 0, :], gates[:, 2:4], ALU.mult))
                    for a in range(DH):
                        v.tensor_scalar(FW[2][:, a, 0:HID], FI[2][:, a, 0:HID], ZERO_POINT, fsd[:, 1, a:a + 1], ALU.subtract, ALU.mult).then_inc(ffn_dequant, 1)
                    for n in range(2):
                        for b in range(HB):
                            v.tensor_scalar(FW[n][:, b, :], FI[n][:, b, :], ZERO_POINT, fsc[:, n, b:b + 1], ALU.subtract, ALU.mult).then_inc(ffn_dequant, 1)
                    for hf in range(2):
                        wait_emptied(e, j_proj(4 * hf + 3))
                        ts = slice(HT * hf, HT * hf + HT)
                        settle(v.tensor_tensor(SQ, PJ[:, ts, 0:192], PJ[:, ts, 0:192], ALU.mult))
                        v.reduce_sum(rs[:, 0, HT * hf:HT * hf + HT], SQ[:, :, 0:QR], AX.X)
                        settle(v.reduce_sum(rs[:, 0, TT + HT * hf:TT + HT * hf + HT], SQ[:, :, QR:192], AX.X))
                        v.tensor_scalar(by_half(2, hf)[:, 0, :], by_half(0, hf)[:, 0, :], 1.0 / QR, RMS_EPS, ALU.mult, ALU.add)
                        settle(v.tensor_scalar(by_half(2, hf)[:, 1, :], by_half(0, hf)[:, 1, :], 1.0 / KR, RMS_EPS, ALU.mult, ALU.add))
                        v.reciprocal(by_half(0, hf), by_half(2, hf)).then_inc(rms_rec, 1)
                    for hf in range(2):
                        e.wait_ge(rms_root, hf + 1)
                        refine(by_half(0, hf), by_half(1, hf), by_half(2, hf)).then_inc(rms_ready, 1)
                        e.wait_ge(rms_ready, hf + 1)
                        for t in range(HT * hf, HT * hf + HT):
                            v.tensor_scalar(KN[:, t, 64:128], PJ[:, t, QR:192], rs[:, 1, TT + t:TT + t + 1], None,
                                            ALU.mult).then_inc(kv_nat_ready, 1)
                            if hf:
                                v.tensor_scalar(PJ[:, t, 0:QR], PJ[:, t, 0:QR], rs[:, 1, t:t + 1], None, ALU.mult).then_inc(q_nat_ready[1], 1)
                    e.wait_ge(wo_landed, 16)
                    for a in range(DH):
                        v.tensor_scalar(WO[:, a, :], WO[:, a, :], gates[:, a:a + 1], None, ALU.mult).then_inc(wo_scaled, 1)
                    for k in range(3 * NC):
                        e.wait_ge(qk_high, k + 1)
                        tg, kind = k // 3, k % 3
                        hi, lo = (t[:, C * tg:C * tg + C] for t in (QT if kind == 0 else K[kind - 1]))
                        full = ps[:, (J_QK + k) % 8, :]
                        if kind == 0:
                            v.tensor_tensor(lo, full, hi.bitcast(F32), ALU.subtract).then_inc(emptied["V"], 1)
                        else:
                            v.scalar_tensor_tensor(lo, full, kvw[:, kind - 1:kind], hi.bitcast(F32), ALU.mult, ALU.subtract).then_inc(emptied["V"], 1)
                    e.wait_ge(ffn_stored, 32)
                    for k in range(1, H // 2, 2):
                        e.wait_ge(filled, J_WOT + k + 1)
                        v.tensor_copy(woT[:, 2 * k:2 * k + 2, :], ps[:, (J_WOT + k) % 8, :].rearrange("p (h d) -> p h d", h=2)).then_inc(emptied["V"], 1)
                    for k in range(0, PAIRS // 2, 2):
                        e.wait_ge(filled, J_WVO + k + 1)
                        v.tensor_scalar(WVO[:, 2 * k:2 * k + 2, :], ps[:, (J_WVO + k) % 8, :].rearrange("p (g d) -> p g d", g=2),
                                        kvw[:, 2:3], None, ALU.mult).then_inc(emptied["V"], 1)

                @block.tensor
                def _(e):
                    t_ = nc.tensor

                    def bank(job):
                        if job >= 8:
                            wait_emptied(e, job - 8)
                        return ps[:, job % 8, :]

                    def project_tokens(ks):
                        for k in ks:
                            b = bank(j_proj(k))
                            if k % 2 == 0:
                                wait_emptied(e, J_ZT + 2 * (k // 2) + 1)
                            for n in range(2):
                                t = 2 * k + n
                                for a in range(DH):
                                    last = t_.matmul(b[:, D * n:D * n + D], hT[:, a, P * t:P * t + P], WDT[:, a, :], start=(a == 0), stop=(a == DH - 1))
                            last.then_inc(filled, 1)

                    e.wait_ge(ident_landed, 16)
                    e.wait_ge(wd_landed, 48)
                    b = bank(J_WD)
                    for half in range(DH):
                        for w in range(2):
                            last = t_.transpose(b[:, (2 * half + w) * P:(2 * half + w + 1) * P], WD[:, w, half * P:(half + 1) * P], ident[:, :])
                    last.then_inc(filled, 1)
                    def modulation(b, columns):
                        for n in columns:
                            for a in range(DH):
                                last = t_.matmul(b[:, n:n + 1], WMOD[:, a, n * P:(n + 1) * P], cc[:, 4, a:a + 1], start=(a == 0), stop=(a == DH - 1))
                        last.then_inc(filled, 1)

                    e.wait_ge(silu_ready, 1)
                    e.wait_ge(wmod_landed[0], 16)
                    modulation(bank(J_MOD), range(4))
                    for k in range(2 * NC):
                        tg, half = k // 2, k % 2
                        b = bank(J_ZT + k)
                        for n in range(CB):
                            e.wait_ge(z_ready, CB * tg + n + 1)
                            last = t_.transpose(b[:, P * n:P * n + P], Z[:, CB * tg + n, half * P:half * P + P], ident[:, :])
                        last.then_inc(filled, 1)
                    e.wait_ge(wmod_landed[1], 16)
                    modulation(bank(J_MOD2), range(4, 12))
                    project_tokens(range(TT // 4))
                    e.wait_ge(abs_landed, 32)
                    e.wait_ge(wr_landed, 16)
                    for k in range(2):
                        b = bank(J_ABS + k)
                        for n in range(8):
                            h = 8 * k + n
                            last = t_.matmul(b[:, 64 * n:64 * n + 64], WU[:, h, :], WKV[:, 2 * h, :], start=True, stop=True)
                        last.then_inc(filled, 1)
                    for k in range(2):
                        b = bank(J_ROPE + k)
                        for n in range(4):
                            last = t_.transpose(b[:, P * n:P * n + P], WR[:, 4 * k + n, :], ident[:, :])
                        last.then_inc(filled, 1)
                    project_tokens(range(TT // 4, TT // 2))
                    e.wait_ge(ffn_dequant, DH)
                    for k in range(3):
                        bk = bank(J_FFN + k)
                        for m in range(2):
                            for a in range(DH):
                                last = t_.transpose(bk[:, D * m + P * a:D * m + P * a + P], FW[2][:, a, P * (2 * k + m):P * (2 * k + m) + P], ident[:, :])
                        last.then_inc(filled, 1)
                    blocks = [(n, a, b) for n in range(2) for a in range(DH) for b in range(HB)]
                    for k in range(6):
                        bk = bank(J_FFN + 3 + k)
                        for m in range(4):
                            n, a, b = blocks[4 * k + m]
                            e.wait_ge(ffn_dequant, DH + HB * n + b + 1)
                            last = t_.transpose(bk[:, P * m:P * m + P], FW[n][:, b, P * a:P * a + P], ident[:, :])
                        last.then_inc(filled, 1)
                    for k in range(3 * NC):
                        tg, kind = k // 3, k % 3
                        b = bank(J_QK + k)
                        for n in range(CB):
                            t = CB * tg + n
                            if kind == 0:
                                e.wait_ge(q_nat_ready[t // HT], t % HT + 1)
                            else:
                                e.wait_ge(kv_nat_ready, t + 1)
                                e.wait_ge(rope_nat_ready, 2 * (t // HT) + 2)
                            src = (PJ[:, t, 0:QR], KN[:, t, 64:192], KN[:, t, 0:128])[kind]
                            last = t_.transpose(b[:, P * n:P * n + P], src, ident[:, :])
                        last.then_inc(filled, 1)
                    e.wait_ge(wo_scaled, DH)
                    for k in range(H // 2):
                        b = bank(J_WOT + k)
                        for n in range(2):
                            for a in range(DH):
                                last = t_.transpose(b[:, D * n + P * a:D * n + P * a + P], WO[:, a, (2 * k + n) * VD:(2 * k + n + 1) * VD], ident[:, :])
                        last.then_inc(filled, 1)
                    wait_emptied(e, J_WOT + H // 2 - 1)
                    wait_emptied(e, J_WOT + H // 2 - 2)
                    for k in range(PAIRS // 2):
                        b = bank(J_WVO + k)
                        for n in range(2):
                            for o in range(2):
                                h = 2 * (2 * k + n) + o
                                last = t_.matmul(b[64 * o:64 * o + 64, D * n:D * n + D], WKV[:, 2 * h + 1, :], woT[:, h, :], start=True, stop=True)
                        last.then_inc(filled, 1)

        with ExitStack() as work:
            ropeT = sb(work, "ropeT", [P, 2, S])
            WS = sb(work, "WS", [P, 2, 2, P], F32R)
            Qf = sb(work, "Qf", [P, 2, C])
            QH = sb(work, "QH", [P, NC, 2, C], F32R)
            QL = sb(work, "QL", [P, NC, 2, C], F32R)
            RF = sb(work, "RF", [P, C])
            RS = sb(work, "RS", [P, C])
            RC = sb(work, "RC", [P, C])
            mp = sb(work, "mp", [P, 2, 2 * CB, NC])
            mrow = sb(work, "mrow", [P, 2 * CB])
            mhl = sb(work, "mhl", [P, 2, 2 * CB], BF16)
            MB = sb(work, "MB", [P, 3, 2, C])
            PT = sb(work, "PT", [P, 4, 2, C])
            acc = sb(work, "acc", [P, 2, 2, C])

            weights_staged, tables_landed = sem("weights_staged"), [sem(f"tables_landed_{c}") for c in range(NC)]
            q_abs, q_rope = sem("q_abs_projected"), sem("q_rope_projected")
            q_abs_copied, rope_copied, rope_swapped, rope_mul, q_full = (
                sem("q_abs_copied"), sem("rope_copied"), sem("rope_swapped"), sem("rope_mul"), sem("q_full"))
            q_high, q_low = sem("q_high"), sem("q_low")
            piece_ready, piece_reduced, row_max, max_split = sem("piece_ready"), sem("piece_reduced"), sem("row_max"), sem("max_split")
            max_spread, shift_ready = sem("max_spread"), sem("shift_ready")
            scores_ready, shifted, probs_ready, probs_summed, probs_used = (
                sem("scores_ready"), sem("shifted"), sem("probs_ready"), sem("probs_summed"), sem("probs_used"))
            out_copied, sums_ready, sums_copied = sem("out_copied"), sem("sums_ready"), sem("sums_copied")

            pair_sums_landed, pair_inverted, inverses_stored = sem("pair_sums_landed"), sem("pair_inverted"), sem("inverses_stored")

            N0, O_BANK, MISC = 4, 6, 7
            MB_SLOT = [1, 2, 1, 0]

            FIRST_PROJECTED, FIRST_ROTATED = [0, 0, 4, 8], [0, 3, 7, 11]
            SPARE = [0, 1, 2, 3, O_BANK]

            def spare_bank(c, m):
                return SPARE[(2 * c + 1 - m) % len(SPARE)]

            MISC_AT = {
                3: [("max", 2, 0, 0)], 4: [("max", 2, 1, 0)], 5: [("sum", 0)],
                6: [("rope", 0)], 7: [("abs", 0)], 8: [("cos", 0)], 9: [("sin", 0)], 10: [("turn", 0)], 12: [("split", 0)],
                13: [("sum", 1)], 14: [("rope", 1)], 15: [("abs", 1)], 16: [("cos", 1)], 17: [("sin", 1)], 18: [("turn", 1)],
                19: [("max", 3, 0, 0)], 20: [("max", 3, 1, 0), ("split", 1)],
                21: [("rope", 2)], 22: [("abs", 2), ("cos", 2)], 23: [("max", 0, 0, 1)], 24: [("max", 0, 1, 1), ("sin", 2)],
                25: [("turn", 2)], 26: [("sum", 2)], 27: [("split", 2)],
                31: [("max", 1, 0, 1)], 32: [("max", 1, 1, 1)],
                33: [("rope", 3)], 34: [("abs", 3), ("cos", 3)], 35: [("sin", 3)], 36: [("turn", 3)], 38: [("split", 3)], 39: [("sum", 3)],
            }
            FIRST_LEAD = 12
            MISC_FIRST = {**MISC_AT, 3: [], 4: [("sum", 0)], 5: [("rope", 0)], 6: [("abs", 0)], 7: [("max", 2, 0, 0)], 8: [("max", 2, 1, 0), ("cos", 0)]}

            def is_first(p):
                return isinstance(p, int) and p == 0

            def misc_at(p, u):
                return (MISC_FIRST if is_first(p) else MISC_AT).get(u, [])

            def lead_steps(p, u):
                if not is_first(p):
                    return [u + LEAD]
                return range(min(u + LEAD, FIRST_LEAD + 2 * u), min(u + 1 + LEAD, FIRST_LEAD + 2 * (u + 1)))

            TURN = ("cos", "sin", "turn")

            def step_of(u):
                d, u = divmod(u, STEPS)
                c = max(k for k in range(NC) if U0[k] <= u)
                return d, c, u - U0[c]

            def piece(w, k):
                d, c, j = step_of(w)
                i = 2 * j + k
                hd, r = divmod(i, CB * (c + 1))
                b, pc = divmod(r, c + 1)
                return d, c, i, hd, b, pc, C * pc, min(C, P * (CB * c + b + 1) - C * pc)

            def first_col(c, j):
                return P * max(0, j - CB * c)

            def wait(e, s, value):
                if not isinstance(value, int) or value > 0:
                    e.wait_ge(s, value)

            def job(p, c):
                return NC * p + c

            order, order_first = ([ev for u in sorted(table) for ev in table[u] if ev[0] in ("max", "sum", "abs", "rope")]
                                  for table in (MISC_AT, MISC_FIRST))

            order_last = [ev for ev in order if ev[0] == "sum" or (ev[0] == "max" and not ev[3])]

            def wait_misc(e, p, ev, last_pair):
                evs = order_last if last_pair else order_first if is_first(p) else order
                k = evs.index(ev)
                prev, q = (evs[k - 1], p) if k else (order[-1], p - 1)
                if k == 0 and is_first(p):
                    e.wait_ge(shift_ready, 4)
                    return
                if prev[0] == "max":
                    wait(e, shift_ready, 2 * job(q + prev[3], prev[1]) + prev[2] + 1)
                elif prev[0] == "sum":
                    wait(e, sums_copied, job(q, prev[1]) + 1)
                elif prev[0] == "abs":
                    wait(e, q_abs_copied, 2 * job(q + 1, prev[1]) + 2)
                else:
                    wait(e, rope_copied, job(q + 1, prev[1]) + 1)

            def run_pairs(e, prologue, body):
                prologue()
                body(0, False)
                with e.Fori(1, PAIRS - 1) as p:
                    body(p, False)
                body(PAIRS - 1, True)

            with nc.Block() as block:
                @block.sync
                def _(e):
                    def stage(p):
                        src = wq_d[p, :, :] if isinstance(p, int) else wq_d[bass.ds(p, 1), :, :].rearrange("g p n -> p (g n)")
                        e.dma_start(WS[:, :, :, :].rearrange("p a m r -> p (a m r)").bitcast(F32), src).then_inc(weights_staged, 16)

                    def store(p, c):
                        e.wait_ge(out_copied, job(p, c) + 1)
                        cols = slice(C * c, C * c + C)
                        if isinstance(p, int):
                            o_dst, l_dst = o_d[p, :, cols], l_d[2 * p:2 * p + 2, cols]
                        else:
                            o_dst = o_d[bass.ds(p, 1), :, cols].rearrange("g p n -> p (g n)")
                            l_dst = l_d[bass.ds(2 * p, 2), cols]
                        e.dma_start(o_dst, Osb[:, c % 2, :]).then_inc(results_stored[c], 16)
                        e.wait_ge(sums_copied, job(p, c) + 1)
                        e.dma_start(l_dst, Lsb[0:64:32, c % 2, :]).then_inc(results_stored[c], 16)

                    def body(p, last):
                        if not last:
                            e.wait_ge(q_abs, job(p, NC - 1) + 1)
                            stage(p + 1)
                        first = is_first(p)
                        if not first:
                            load_sums(p)
                        for c in range(NC):
                            if c >= 2 and not last:
                                exchange(job(p + 1, c))
                            store(p, c)
                            if c == 0 and not first:
                                store_inverses(p)
                            if c < 2 and not last:
                                exchange(job(p + 1, c))
                            if c == 0 and last:
                                prefetch()

                    def prefetch():
                        e.wait_ge(inverses_stored, 16 * (PAIRS - 1))
                        e.wait_ge(q_abs, NC * PAIRS)
                        e.wait_ge(q_full, 2 * NC * PAIRS)
                        for g in range(NG - 1):
                            load_outputs(e, 0, g)
                            load_inverses(e, 0, g)

                    def exchange(g):
                        e.wait_ge(rope_copied, g + 1)
                        for o in range(2):
                            e.dma_start(RS[o:P:2, :], RF[1 - o:P:2, :]).then_inc(rope_swapped, 16)

                    def load_sums(p):
                        for c in range(NC):
                            e.wait_ge(results_stored[c], 32 * p)
                        e.dma_start(LP[:, 0, :], pair_rows(l_d, p - 1)).then_inc(pair_sums_landed, 16)

                    def store_inverses(p):
                        e.wait_ge(pair_inverted, p)
                        e.dma_start(pair_rows(r_d, p - 1), LP[:, 1, :]).then_inc(inverses_stored, 16)

                    def prologue():
                        stage(0)
                        for c in range(NC):
                            cols = slice(C * c, C * c + C)
                            e.dma_start(ropeT[:, :, cols], rope_q[:, :, cols].rearrange("k p n -> p k n")).then_inc(tables_landed[c], 16)
                        for c in range(NC):
                            exchange(c)

                    run_pairs(e, prologue, body)
                    e.wait_ge(inverses_stored, 16 * (PAIRS - 1))

                @block.tensor
                def _(e):
                    t_ = nc.tensor

                    def project(c, m, done, bank=MISC):
                        for k, (w, q) in enumerate(((0, 0), (0, 1), (1, 0))):
                            last = t_.matmul(ps[:, bank, :], WS[:, w, m, :], QT[q][:, C * c:C * c + C], start=(k == 0), stop=(k == 2))
                        last.then_inc(done, 1)

                    def spread_maxima(c, hd, g):
                        e.wait_ge(max_split, 2 * (g + 1))
                        for b in range(CB):
                            for part in range(2):
                                col = mhl[:, part, hd * CB + b:hd * CB + b + 1]
                                last = t_.matmul(ps[:, MISC, P * b:P * b + P], col.to_broadcast([P, P]), identb[:, :],
                                                 start=(part == 0), stop=(part == 1))
                        last.then_inc(max_spread, 1)

                    def sum_columns(p, c):
                        e.wait_ge(probs_summed, STEPS * p + U0[c + 1])
                        for hd in range(2):
                            last = t_.matmul(ps[32 * hd:32 * hd + 32, MISC, :], ones[:, 0:32], acc[:, c % 2, hd, :], start=True, stop=True)
                        last.then_inc(sums_ready, 1)

                    def misc(p, ev, last_pair):
                        kind, c = ev[0], ev[1]
                        if kind in TURN + ("split",) or last_pair and ev not in order_last:
                            return
                        wait_misc(e, p, ev, last_pair)
                        if kind == "max":
                            spread_maxima(c, ev[2], job(p + ev[3], c))
                        elif kind == "sum":
                            sum_columns(p, c)
                        else:
                            if kind == "rope":
                                e.wait_ge(weights_staged, 16 * (p + 2))
                            project(c, ("abs", "rope").index(kind), {"abs": q_abs, "rope": q_rope}[kind])

                    def max_pieces(p, w, last_pair):
                        for k in range(2):
                            d, c, i, hd, b, pc, key, width = piece(w, k)
                            if d and last_pair:
                                return
                            if i == 0:
                                e.wait_ge(q_high, job(p + d, c) + 1)
                            wait(e, piece_reduced, PIECES * p + 2 * w + k - 1)
                            diag = pc == c
                            last = t_.matmul(ps[:, N0 + k, 0:max(width, 2 * P)], QH[:, c, hd, P * b:P * b + P],
                                             K[hd][0][:, key:key + max(width, 2 * P)], start=True, stop=not diag)
                            if diag:
                                last = t_.matmul(ps[:, N0 + k, width - P:width], identb[:, :], maskb[:, 0, :], start=False, stop=True)
                            last.then_inc(piece_ready, 1)

                    def scores(p, u, last_pair):
                        d, c, j = step_of(u)
                        if d and last_pair:
                            return
                        if j == 0:
                            e.wait_ge(q_low, job(p + d, c) + 1)
                        wait(e, shifted, STEPS * p + u - 1)
                        x0 = first_col(c, j)
                        xm = min(x0, C - 2 * P)
                        masked = j >= CB * c
                        for hd in range(2):
                            b = 2 * (u % 2) + hd
                            for k, (w, q) in enumerate(((0, QH), (0, QL), (1, QH))):
                                last = t_.matmul(ps[:, b, xm:C], K[hd][w][:, P * j:P * j + P], q[:, c, hd, xm:C], start=(k == 0),
                                                 stop=(k == 2 and not masked))
                            if masked:
                                last = t_.matmul(ps[:, b, x0:x0 + P], identb[:, :], maskb[:, 1, :], start=False, stop=True)
                        last.then_inc(scores_ready, 1)

                    def weigh_values(p, u):
                        _, c, j = step_of(u)
                        e.wait_ge(probs_ready, STEPS * p + u + 1)
                        if j == 0:
                            wait(e, out_copied, job(p, c))
                        x0 = first_col(c, j)
                        for hd in range(2):
                            last = t_.matmul(ps[64 * hd:64 * hd + 64, O_BANK, x0:C], KN[:, j, 64:128], PT[:, u % 4, hd, x0:C],
                                             start=(j == 0), stop=(j == UNITS[c] - 1))
                        last.then_inc(probs_used, 1)

                    def body(p, last_pair):
                        for u in range(STEPS):
                            scores(p, u + 2, last_pair)
                            late = [ev for ev in misc_at(p, u) if ev == ("sum", 3)]
                            for ev in misc_at(p, u):
                                if ev not in late:
                                    misc(p, ev, last_pair)
                            lead = list(lead_steps(p, u))
                            max_pieces(p, lead[0], last_pair)
                            weigh_values(p, u)
                            for w in lead[1:]:
                                max_pieces(p, w, last_pair)
                            for ev in late:
                                misc(p, ev, last_pair)

                    def project_first(c):
                        for k, (m, done) in enumerate(((1, q_rope), (0, q_abs))):
                            n = 2 * c + k - len(SPARE)
                            if n >= 0:
                                if n % 2 == 0:
                                    e.wait_ge(rope_copied, n // 2 + 1)
                                else:
                                    e.wait_ge(q_abs_copied, 2 * (n // 2) + 2)
                            project(c, m, done, spare_bank(c, m))

                    def prologue():
                        e.wait_ge(weights_staged, 16)
                        for w in range(FIRST_LEAD):
                            for c in range(NC):
                                if w == FIRST_PROJECTED[c]:
                                    project_first(c)
                            max_pieces(0, w, False)
                            for hd in range(2):
                                if w == U0[1] + 1 + 2 * hd:
                                    wait(e, shift_ready, hd)
                                    spread_maxima(0, hd, 0)
                        e.wait_ge(q_abs_copied, 2 * NC)
                        e.wait_ge(rope_copied, NC)
                        scores(0, 0, False)
                        for hd in range(2):
                            e.wait_ge(shift_ready, 2 + hd)
                            spread_maxima(1, hd, 1)
                            if hd == 0:
                                scores(0, 1, False)

                    run_pairs(e, prologue, body)

                @block.vector
                def _(e):
                    v = nc.vector

                    def turn(part, c, g):
                        if part == "cos":
                            e.wait_ge(rope_copied, g + 1)
                            wait(e, q_full, 2 * g)
                            v.tensor_tensor(RC[:, :], RF[:, :], ropeT[:, 0, C * c:C * c + C], ALU.mult).then_inc(rope_mul, 1)
                        elif part == "sin":
                            e.wait_ge(rope_swapped, 32 * (g + 1))
                            v.tensor_tensor(RS[:, :], RS[:, :], ropeT[:, 1, C * c:C * c + C], ALU.mult).then_inc(rope_mul, 1)
                        else:
                            e.wait_ge(rope_mul, 2 * (g + 1))
                            wait(e, q_low, g)
                            v.tensor_tensor(Qf[64:128, 0, :], RC[64:128, :], RS[64:128, :], ALU.add).then_inc(q_full, 1)
                            v.tensor_tensor(Qf[0:64, 1, :], RC[0:64, :], RS[0:64, :], ALU.add).then_inc(q_full, 1)

                    def reduce_pieces(p, w, last_pair):
                        for k in range(2):
                            d, c, i, hd, b, pc, key, width = piece(w, k)
                            if d and last_pair:
                                return
                            e.wait_ge(piece_ready, PIECES * p + 2 * w + k + 1)
                            v.reduce_max(mp[:, c % 2, hd * CB + b, pc:pc + 1], ps[:, N0 + k, 0:width], AX.X).then_inc(piece_reduced, 1)
                        if i == 2 * UNITS[c] - 1:
                            split_maxima(PIECES * p + 2 * w + 2, c, job(p + d, c))

                    def split_maxima(pieces_done, c, g):
                        e.wait_ge(piece_reduced, pieces_done)
                        v.reduce_max(mrow[:, :], mp[:, c % 2, :, 0:c + 1], AX.X).then_inc(row_max, 1)
                        e.wait_ge(row_max, g + 1)
                        wait(e, max_spread, 2 * g)
                        v.tensor_copy(mhl[:, 0, :], mrow[:, :]).then_inc(max_split, 1)
                        e.wait_ge(max_split, 2 * g + 1)
                        v.tensor_tensor(mhl[:, 1, :], mrow[:, :], mhl[:, 0, :], ALU.subtract).then_inc(max_split, 1)

                    def shift(p, u, last_pair):
                        d, c, j = step_of(u)
                        if d and last_pair:
                            return
                        if j == 0:
                            e.wait_ge(shift_ready, 2 * job(p + d, c) + 2)
                        e.wait_ge(scores_ready, STEPS * p + u + 1)
                        wait(e, probs_used, STEPS * p + u - 3)
                        wait(e, probs_summed, STEPS * p + u - 3)
                        x0 = first_col(c, j)
                        b = 2 * (u % 2)
                        v.tensor_tensor(PT[:, u % 4, :, x0:C], ps[:, b:b + 2, x0:C], MB[:, MB_SLOT[c], :, x0:C], ALU.subtract).then_inc(shifted, 1)

                    def invert_sums(p):
                        e.wait_ge(pair_sums_landed, 16 * p)
                        v.reciprocal(LP[:, 1, :], LP[:, 0, :]).then_inc(pair_inverted, 1)

                    def body(p, last_pair):
                        for u in range(STEPS):
                            if u == 3 and not is_first(p):
                                invert_sums(p)
                            if u == STEPS - 1 and not is_first(p):
                                e.wait_ge(inverses_stored, 16 * p)
                            shift(p, u + 2, last_pair)
                            for w in lead_steps(p, u):
                                reduce_pieces(p, w, last_pair)
                            for ev in misc_at(p, u):
                                if ev[0] in TURN and not last_pair:
                                    turn(ev[0], ev[1], job(p + 1, ev[1]))

                    def prologue():
                        for w in range(FIRST_LEAD):
                            if w in FIRST_ROTATED:
                                c = FIRST_ROTATED.index(w)
                                e.wait_ge(tables_landed[c], 16)
                                for part in TURN:
                                    turn(part, c, c)
                            reduce_pieces(0, w, False)
                        shift(0, 0, False)
                        shift(0, 1, False)

                    run_pairs(e, prologue, body)

                @block.scalar
                def _(e):
                    def copy_abs(g, bank=MISC):
                        e.wait_ge(q_abs, g + 1)
                        wait(e, q_low, g)
                        e.activation(Qf[0:64, 0, :], ps[0:64, bank, :], ACT.Copy).then_inc(q_abs_copied, 1)
                        e.activation(Qf[64:128, 1, :], ps[64:128, bank, :], ACT.Copy).then_inc(q_abs_copied, 1)

                    def copy_rope(g, bank=MISC):
                        e.wait_ge(q_rope, g + 1)
                        wait(e, q_full, 2 * g)
                        e.activation(RF[:, :], ps[:, bank, :], ACT.Copy).then_inc(rope_copied, 1)

                    def high_part(c, g):
                        e.wait_ge(q_abs_copied, 2 * (g + 1))
                        e.wait_ge(q_full, 2 * (g + 1))
                        e.activation(QH[:, c, :, :], Qf[:, :, :], ACT.Copy).then_inc(q_high, 1)

                    def copy_shift(c, hd, g):
                        e.wait_ge(max_spread, 2 * g + hd + 1)
                        e.activation(MB[:, MB_SLOT[c], hd, :], ps[:, MISC, :], ACT.Copy).then_inc(shift_ready, 1)

                    def wait_stored(p, c):
                        wait(e, results_stored[(c + 2) % NC], 32 * (p + c // 2))

                    def copy_sums(p, c):
                        g = job(p, c)
                        e.wait_ge(sums_ready, g + 1)
                        wait_stored(p, c)
                        e.activation(Lsb[:, c % 2, :], ps[0:64, MISC, :], ACT.Copy).then_inc(sums_copied, 1)

                    def copy_output(p, c):
                        g = job(p, c)
                        e.wait_ge(probs_used, STEPS * p + U0[c + 1])
                        wait_stored(p, c)
                        e.activation(Osb[:, c % 2, :], ps[:, O_BANK, :], ACT.Copy).then_inc(out_copied, 1)

                    def exponentials(p, u, last_pair):
                        d, c, j = step_of(u)
                        if d and last_pair:
                            return
                        e.wait_ge(shifted, STEPS * p + u + 1)
                        x0 = first_col(c, j)
                        e.activation(PT[:, u % 4, :, x0:C], PT[:, u % 4, :, x0:C], ACT.Exp, scale=SCALE).then_inc(probs_ready, 1)

                    def body(p, last_pair):
                        for u in range(STEPS):
                            for ev in misc_at(p, u):
                                if ev[0] == "abs" and not last_pair:
                                    copy_abs(job(p + 1, ev[1]))
                                if ev[0] == "rope" and not last_pair:
                                    copy_rope(job(p + 1, ev[1]))
                                if ev[0] == "max" and not (last_pair and ev[3]):
                                    copy_shift(ev[1], ev[2], job(p + ev[3], ev[1]))
                                if ev[0] == "sum" and ev[1] < NC - 1:
                                    copy_sums(p, ev[1])
                            exponentials(p, u + 2, last_pair)
                            for ev in misc_at(p, u):
                                if ev[0] == "split" and not last_pair:
                                    high_part(ev[1], job(p + 1, ev[1]))
                            if u + 1 in U0:
                                c = U0.index(u + 1) - 1
                                copy_output(p, c)
                                if c == NC - 1:
                                    copy_sums(p, c)

                    def prologue():
                        for c in range(NC):
                            copy_rope(c, spare_bank(c, 1))
                            copy_abs(c, spare_bank(c, 0))
                            if c == 2:
                                copy_shift(0, 0, 0)
                                copy_shift(0, 1, 0)
                            high_part(c, c)
                        copy_shift(1, 0, 1)
                        copy_shift(1, 1, 1)
                        exponentials(0, 0, False)
                        exponentials(0, 1, False)

                    run_pairs(e, prologue, body)

                @block.gpsimd
                def _(e):
                    def low_part(c, g):
                        e.wait_ge(q_high, g + 1)
                        e.tensor_tensor(QL[:, c, :, :], Qf[:, :, :], QH[:, c, :, :].bitcast(F32), ALU.subtract).then_inc(q_low, 1)

                    def sum_probs(p, u, last_pair):
                        d, c, j = step_of(u)
                        if d and last_pair:
                            return
                        e.wait_ge(probs_ready, STEPS * p + u + 1)
                        wait(e, probs_summed, STEPS * p + u)
                        x0 = first_col(c, j)
                        a, pt = acc[:, c % 2, :, x0:C], PT[:, u % 4, :, x0:C]
                        if j == 0:
                            wait(e, sums_ready, job(p + d, c) - 1)
                            e.tensor_tensor(a, pt, ones[:, 0:1].unsqueeze(2).to_broadcast([P, 2, C]), ALU.mult).then_inc(probs_summed, 1)
                        else:
                            e.tensor_tensor(a, a, pt, ALU.add).then_inc(probs_summed, 1)

                    def body(p, last_pair):
                        for u in range(STEPS):
                            sum_probs(p, u + 2, last_pair)
                            for ev in misc_at(p, u):
                                if ev[0] == "split" and not last_pair:
                                    low_part(ev[1], job(p + 1, ev[1]))

                    def prologue():
                        for c in range(NC):
                            low_part(c, c)
                        sum_probs(0, 0, False)
                        sum_probs(0, 1, False)

                    run_pairs(e, prologue, body)
        attn_kept.close()

        project_and_feed(nc, sb, sem, ps, X, ident, modc, scale1, st, mv, rs, WVO, WVL, LP, results_stored, pair_rows,
                         (OF, OL, WTH, WTF, WTL, hH, RB), outputs_landed, inverses_landed, load_outputs, load_inverses,
                         l_d, r_d, ffn_d, out)


def project_and_feed(nc, sb, sem, ps, X, ident, modc, scale1, st, mv, rs, WVO, WVL, LP, results_stored, pair_rows,
                     first_tensors, outputs_landed, inverses_landed, load_outputs, load_inverses,
                     l_d, r_d, ffn_d, out):
    OF, OL, WTH, WTF, WTL, hH, RB = first_tensors
    with ExitStack() as work:
        sb(work, "first_tensors", [P, 2 * PAIRS * C + 2 * (2 * DH * HB * P) + DH * C + PAIRS * C])

        def full_then_low(name, shape):
            return in_place(nc, work, name, shape, F32, F32R)

        WVH = sb(work, "wvo_hi", [P, PAIRS, D], F32R)
        WDH = sb(work, "wdn_hi", [P, HB, D], F32R)
        WDF, WDL = full_then_low("wdn_lo", [P, HB, D])
        Z = sb(work, "Z2", [P, 2, CB, D])
        hF, hL = full_then_low("h_lo", [P, DH, C])
        SG = sb(work, "SG", [P, 2, C])
        AH = sb(work, "act_hi", [P, HB, C], F32R)
        AF, AL = full_then_low("act_lo", [P, HB, C])
        OH = sb(work, "out_hi", [P, 2, PAIRS, C], F32R)

        f_step = sem("ffn_vector_step")
        f_rec, f_root, f_z = sem("ffn_var_rec"), sem("ffn_root"), sem("ffn_z_ready")
        weights_landed = sem("weights_landed")
        wvo_high, wvo_low, w_high, w_low = sem("wvo_high"), sem("wvo_low"), sem("ffn_weights_high"), sem("ffn_weights_low")
        h_filled, h_full, h_high, h_low = sem("h_filled"), sem("h_full"), sem("h_high"), sem("h_low")
        gu_ready, silu_done, act_ready, down_ready, out_ready, stored = (
            sem("gate_up_ready"), sem("silu_done"), sem("act_ready"), sem("down_ready"), sem("out_ready"), sem("stored"))
        act_high, act_low = sem("act_high"), sem("act_low")
        last_sums_landed, last_inverted, last_stored = sem("last_sums_landed"), sem("last_inverted"), sem("last_inverses_stored")
        normalised, out_high, out_low, out_low_odd = sem("outputs_normalised"), sem("outputs_high"), sem("outputs_low"), sem("outputs_low_odd")
        projected, residual_added = sem("projected"), sem("residual_added")
        ov = out.rearrange("a (t p) d -> p (a t) d", p=P)

        ORDER = [(0, g) for g in range(NG - 1)] + [(1, 0), (1, 1), (0, NG - 1)] + [(1, g) for g in range(2, NG)]
        ORDER += [(c, g) for c in range(2, NC) for g in range(NG)]
        BY_POOL = [cg for cg in ORDER if cg[0] or cg[1] % 2 == 0]

        def nth(c, g):
            return ORDER.index((c, g)) + 1

        with nc.Block() as block:
            @block.sync
            def _(e):
                def load(c, g):
                    if c >= 2:
                        e.wait_ge(projected, 2 * (c - 1))
                    load_outputs(e, c, g)
                    e.wait_ge(normalised, nth(c - 1, g))
                    load_inverses(e, c, g)

                for k in results_stored:
                    e.wait_ge(k, 32 * PAIRS)
                e.dma_start(LP[:, 0, :], pair_rows(l_d, PAIRS - 1)).then_inc(last_sums_landed, 16)
                load_outputs(e, 0, NG - 1)
                load(1, 0)
                load(1, 1)
                e.wait_ge(last_inverted, 1)
                e.dma_start(pair_rows(r_d, PAIRS - 1), LP[:, 1, :]).then_inc(last_stored, 16)
                load(1, 2)
                e.wait_ge(last_stored, 16)
                load_inverses(e, 0, NG - 1)
                for c in range(1, NC):
                    for g in range(NG):
                        if c > 1 or g == NG - 1:
                            load(c, g)
                    if c == 1:
                        for n in range(2):
                            e.dma_start(WTF[:, n, :, :].rearrange("p a h -> p (a h)"), ffn_d[:, n, :]).then_inc(weights_landed, 16)
                        e.dma_start(WDF[:, :, :].rearrange("p a h -> p (a h)"), ffn_d[:, 2, :]).then_inc(weights_landed, 16)
                for c in range(NC):
                    for k in range(2):
                        e.wait_ge(out_ready, 2 * c + k + 1)
                        rows = slice(CB * c + 2 * k, CB * c + 2 * k + 2)
                        e.dma_start(ov[:, rows, :], X[:, rows, :]).then_inc(stored, 16)
                e.wait_ge(stored, 32 * NC)

            @block.gpsimd
            def _(e):
                def low_outputs(c, g):
                    part = slice(G * g, G * g + G)
                    e.wait_ge(out_high, nth(c, g))
                    e.tensor_tensor(OL[:, c % 2, part, :], OF[:, c % 2, part, :], OH[:, c % 2, part, :].bitcast(F32),
                                    ALU.subtract).then_inc(out_low, 1)

                for c, g in BY_POOL[:2 * NG - 2]:
                    low_outputs(c, g)
                for c in range(NC):
                    e.wait_ge(h_high, c + 1)
                    e.tensor_tensor(hL[:, :, :], hF[:, :, :], hH[:, :, :].bitcast(F32), ALU.subtract).then_inc(h_low, 1)
                    if c + 2 < NC:
                        for g in range(NG):
                            low_outputs(c + 2, g)

            @block.scalar
            def _(e):
                def root(c):
                    e.wait_ge(f_rec, c + 1)
                    e.activation(rs[:, 1, CB * c:CB * c + CB], rs[:, 0, CB * c:CB * c + CB], ACT.Sqrt).then_inc(f_root, 1)

                def high_outputs(c, g):
                    part = slice(G * g, G * g + G)
                    if c >= 2:
                        e.wait_ge(projected, 2 * (c - 1))
                    e.wait_ge(normalised, nth(c, g))
                    e.activation(OH[:, c % 2, part, :], OF[:, c % 2, part, :], ACT.Copy).then_inc(out_high, 1)

                def high_act(c, hb):
                    e.wait_ge(act_ready, HB * c + hb + 1)
                    e.activation(AH[:, hb, :], AF[:, hb, :], ACT.Copy).then_inc(act_high, 1)

                e.activation(WVH[:, :, :], WVO[:, :, :], ACT.Copy).then_inc(wvo_high, 1)
                for c, g in ORDER[:2 * NG]:
                    high_outputs(c, g)
                root(0)
                e.wait_ge(weights_landed, 48)
                e.activation(WTH[:, :, :, :], WTF[:, :, :, :], ACT.Copy).then_inc(w_high, 1)
                e.activation(WDH[:, :, :], WDF[:, :, :], ACT.Copy).then_inc(w_high, 1)
                for c in range(NC):
                    for a in range(DH):
                        e.wait_ge(h_filled, DH * c + a + 1)
                        e.activation(hF[:, a, :], ps[:, a, :], ACT.Identity, bias=modc[:, 6 + a:7 + a],
                                     scale=scale1[:, 2 + a:3 + a]).then_inc(h_full, 1)
                    e.wait_ge(h_full, DH * c + DH)
                    e.activation(hH[:, :, :], hF[:, :, :], ACT.Copy).then_inc(h_high, 1)
                    for hb in range(HB):
                        e.wait_ge(gu_ready, HB * c + hb + 1)
                        if HB * c + hb >= 2:
                            e.wait_ge(act_ready, HB * c + hb - 1)
                        e.activation(SG[:, hb % 2, :], ps[:, 2 + 2 * (hb % 2), :], ACT.Silu).then_inc(silu_done, 1)
                        if hb == 0 and c + 1 < NC:
                            root(c + 1)
                        if hb:
                            high_act(c, hb - 1)
                        if hb >= 3 and c + 2 < NC:
                            high_outputs(c + 2, hb - 3)
                    high_act(c, HB - 1)
                    if c + 2 < NC:
                        high_outputs(c + 2, NG - 1)

            @block.vector
            def _(e):
                v = nc.vector
                steps = [0]

                def settle(ins):
                    steps[0] += 1
                    ins.then_inc(f_step, 1)
                    e.wait_ge(f_step, steps[0])

                def normalise(c, g):
                    part = slice(G * g, G * g + G)
                    e.wait_ge(outputs_landed[c % 2][g], 16 * (c // 2 + 1))
                    e.wait_ge(inverses_landed[g], 32 * (c + 1))
                    ot = OF[:, c % 2, part, :]
                    v.tensor_tensor(ot, ot, RB[:, part, :], ALU.mult).then_inc(normalised, 1)

                def add_and_measure(c):
                    tiles = range(CB * c, CB * c + CB)
                    for k in range(2):
                        e.wait_ge(projected, 2 * c + k + 1)
                        rows = X[:, CB * c + 2 * k:CB * c + 2 * k + 2, :]
                        sums = ps[:, 6 + k, :].rearrange("p (t d) -> p t d", t=2) if c else ps[:, 2 + 2 * k:4 + 2 * k, 0:D]
                        v.tensor_tensor(rows, sums, rows, ALU.add).then_inc(residual_added, 1)
                        e.wait_ge(residual_added, 2 * c + k + 1)
                        for t in tiles[2 * k:2 * k + 2]:
                            last = v.bn_stats(st[:, t, :], X[:, t, :])
                    settle(last)
                    for t in tiles:
                        last = v.bn_aggr(mv[:, t, :], st[:, t, :])
                    settle(last)
                    settle(v.tensor_scalar(rs[:, 2, CB * c:CB * c + CB], mv[:, CB * c:CB * c + CB, 1], LN_EPS, None, ALU.add))
                    v.reciprocal(rs[:, 0, CB * c:CB * c + CB], rs[:, 2, CB * c:CB * c + CB]).then_inc(f_rec, 1)

                def norm_tokens(c):
                    b, r, a = (rs[:, k, CB * c:CB * c + CB] for k in range(3))
                    e.wait_ge(f_root, c + 1)
                    settle(v.tensor_tensor(b, r, r, ALU.mult))
                    settle(v.tensor_tensor(b, b, a, ALU.mult))
                    settle(v.tensor_scalar(b, b, -0.5, 1.5, ALU.mult, ALU.add))
                    settle(v.tensor_tensor(r, r, b, ALU.mult))
                    if c >= 2:
                        e.wait_ge(h_filled, DH * (c - 1))
                    for n in range(CB):
                        t = CB * c + n
                        last = v.tensor_scalar(Z[:, c % 2, n, :], X[:, t, :], mv[:, t, 0:1], rs[:, 1, t:t + 1], ALU.subtract, ALU.mult)
                    last.then_inc(f_z, 1)

                def low_act(c, hb):
                    e.wait_ge(act_high, HB * c + hb + 1)
                    v.tensor_tensor(AL[:, hb, :], AF[:, hb, :], AH[:, hb, :].bitcast(F32), ALU.subtract).then_inc(act_low, 1)

                def low_odd(g):
                    part = slice(G * g, G * g + G)
                    e.wait_ge(out_high, nth(0, g))
                    v.tensor_tensor(OL[:, 0, part, :], OF[:, 0, part, :], OH[:, 0, part, :].bitcast(F32), ALU.subtract).then_inc(out_low_odd, 1)

                for g in range(NG - 1):
                    normalise(0, g)
                e.wait_ge(wvo_high, 1)
                v.tensor_tensor(WVL[:, :, :], WVO[:, :, :], WVH[:, :, :].bitcast(F32), ALU.subtract).then_inc(wvo_low, 1)
                e.wait_ge(last_sums_landed, 16)
                v.reciprocal(LP[:, 1, :], LP[:, 0, :]).then_inc(last_inverted, 1)
                low_odd(1)
                normalise(1, 0)
                normalise(1, 1)
                normalise(0, NG - 1)
                low_odd(NG - 1)
                for g in range(2, NG):
                    normalise(1, g)
                add_and_measure(0)
                norm_tokens(0)
                e.wait_ge(w_high, 1)
                v.tensor_tensor(WTL[:, :, :, :], WTF[:, :, :, :], WTH[:, :, :, :].bitcast(F32), ALU.subtract).then_inc(w_low, 1)
                e.wait_ge(w_high, 2)
                v.tensor_tensor(WDL[:, :, :], WDF[:, :, :], WDH[:, :, :].bitcast(F32), ALU.subtract).then_inc(w_low, 1)
                for c in range(NC):
                    if c + 1 < NC:
                        add_and_measure(c + 1)
                    for hb in range(HB):
                        e.wait_ge(silu_done, HB * c + hb + 1)
                        if hb == 0 and c:
                            e.wait_ge(down_ready, 2 * c)
                        v.tensor_tensor(AF[:, hb, :], ps[:, 3 + 2 * (hb % 2), :], SG[:, hb % 2, :], ALU.mult).then_inc(act_ready, 1)
                        if hb:
                            low_act(c, hb - 1)
                        if hb == 1 and c + 1 < NC:
                            norm_tokens(c + 1)
                        if hb >= 2 and c + 2 < NC:
                            normalise(c + 2, hb - 2)
                    low_act(c, HB - 1)
                    for k in range(2):
                        e.wait_ge(down_ready, 2 * c + k + 1)
                        rows = X[:, CB * c + 2 * k:CB * c + 2 * k + 2, :]
                        v.tensor_tensor(rows, ps[:, 6 + k, :].rearrange("p (t d) -> p t d", t=2), rows, ALU.add).then_inc(out_ready, 1)

            @block.tensor
            def _(e):
                t_ = nc.tensor

                def project_pair(out, c, b, g):
                    cols = slice(P * b, P * b + P)
                    for n, (o, w) in enumerate(((OH, WVH), (OH, WVL), (OL, WVH))):
                        last = t_.matmul(out, o[:, c % 2, g, cols], w[:, g, :], start=(g == 0 and n == 0), stop=(g == PAIRS - 1 and n == 2))
                    return last

                def project_first():
                    for g in range(PAIRS):
                        if g % G == 0:
                            k = g // G
                            if k % 2:
                                e.wait_ge(out_low_odd, k // 2 + 1)
                            else:
                                e.wait_ge(out_low, BY_POOL.index((0, k)) + 1)
                        for b in range(CB):
                            last = project_pair(ps[:, 2 + b, 0:D], 0, b, g)
                            if g == PAIRS - 1 and b % 2:
                                last.then_inc(projected, 1)

                def project(c, halves=range(2)):
                    for k in halves:
                        if c >= 2:
                            e.wait_ge(out_ready, 2 * (c - 2) + k + 1)
                        for m in range(2):
                            b = 2 * k + m
                            for g in range(PAIRS):
                                if b == 0 and g % G == 0:
                                    e.wait_ge(out_low, BY_POOL.index((c, g // G)) + 1)
                                last = project_pair(ps[:, 6 + k, D * m:D * m + D], c, b, g)
                        last.then_inc(projected, 1)

                def transpose_tokens(c):
                    e.wait_ge(f_z, c + 1)
                    if c:
                        e.wait_ge(h_full, DH * c)
                    for a in range(DH):
                        for n in range(CB):
                            last = t_.transpose(ps[:, a, P * n:P * n + P], Z[:, c % 2, n, P * a:P * a + P], ident[:, :])
                        last.then_inc(h_filled, 1)

                e.wait_ge(wvo_low, 1)
                project_first()
                project(1, [0])
                transpose_tokens(0)
                project(1, [1])
                for c in range(NC):
                    if c and c + 1 < NC:
                        project(c + 1)
                    if c == 0:
                        e.wait_ge(w_low, 2)
                    e.wait_ge(h_low, c + 1)
                    for hb in range(HB):
                        if HB * c + hb >= 2:
                            e.wait_ge(act_ready, HB * c + hb - 1)
                        for n in range(2):
                            k = 0
                            for w, h in ((WTH, hH), (WTL, hH), (WTH, hL)):
                                for a in range(DH):
                                    last = t_.matmul(ps[:, 2 + 2 * (hb % 2) + n, :], w[:, n, a, P * hb:P * hb + P], h[:, a, :],
                                                     start=(k == 0), stop=(k == 5))
                                    k += 1
                        last.then_inc(gu_ready, 1)
                    if c + 1 < NC:
                        transpose_tokens(c + 1)
                    for k in range(2):
                        if c + 1 < NC:
                            e.wait_ge(residual_added, 2 * (c + 1) + k + 1)
                        else:
                            e.wait_ge(out_ready, 2 * (c - 1) + k + 1)
                        for m in range(2):
                            b = 2 * k + m
                            for hb in range(HB):
                                if b == 0:
                                    e.wait_ge(act_low, HB * c + hb + 1)
                                cols = slice(P * b, P * b + P)
                                for n, (o, w) in enumerate(((AH, WDH), (AH, WDL), (AL, WDH))):
                                    last = t_.matmul(ps[:, 6 + k, D * m:D * m + D], o[:, hb, cols], w[:, hb, :],
                                                     start=(hb == 0 and n == 0), stop=(hb == HB - 1 and n == 2))
                        last.then_inc(down_ready, 1)


_INS = ["L0_attn_x", "L0_attn_wq_down", "L0_attn_q_norm_w", "L0_attn_wq_up", "L0_attn_wq_rope", "L0_attn_wkv_down",
        "L0_attn_kv_norm_w", "L0_attn_wkv_up", "L0_attn_wk_rope", "L0_attn_wo", "L0_ffn_wq_gate", "L0_ffn_s_gate",
        "L0_ffn_wq_up", "L0_ffn_s_up", "L0_ffn_wq_down", "L0_ffn_s_down", "L0_c", "L0_wmod"]


def shape_constants():
    inv = np.float32(1.0) / np.power(np.float32(10000.0), np.arange(0, ROPE, 2, dtype=np.float32) / np.float32(ROPE))
    angle = np.outer(np.arange(S, dtype=np.float32), inv.astype(np.float32)).astype(np.float32)
    cos, sin = np.cos(angle).astype(np.float32), np.sin(angle).astype(np.float32)
    row = np.arange(P)
    masks = np.stack([np.where(row[None, :] > row[:, None], NEG, 0.0), np.where(row[:, None] > row[None, :], NEG, 0.0)]).astype(np.float32)
    cosq = np.repeat(cos.T, 2, axis=0)
    sinq = np.repeat(sin.T, 2, axis=0) * np.tile([-1.0, 1.0], ROPE // 2)[:, None]
    rope_q = np.stack([np.concatenate([cosq, cosq]), np.concatenate([sinq, sinq])]).astype(np.float32)
    return {"ident": np.eye(P, dtype=np.float32), "masks": masks, "rope_nat": np.stack([cos, sin]), "rope_q": rope_q}


def kernel(**inputs):
    import concourse.bacc as _bacc
    from concourse import mybir as _mybir
    from concourse.bass_utils import run_bass_kernel_spmd as _run

    nc = _bacc.Bacc("TRN2", target_bir_lowering=False, num_devices=1)
    arrays, args = {}, []
    given = [(n, inputs[n]) for n in _INS] + list(shape_constants().items())
    for name, value in given:
        a = np.ascontiguousarray(value)
        arrays[f"in_{name}_dram"] = a
        args.append(nc.dram_tensor(f"in_{name}_dram", a.shape, _mybir.dt.from_np(a.dtype), kind="ExternalInput").ap())
    out = nc.dram_tensor("out_0_dram", (1, S, D), _mybir.dt.float32, kind="ExternalOutput").ap()
    build(nc, *args, out)
    r = _run(nc, [arrays], core_ids=[0])
    return r.results[0]["out_0_dram"]
```
